# Optimizing a Trainium2 kernel written in Bass

```python
import numpy as np
import jax
import jax.numpy as jnp

def _softmax(x, axis=-1):
    return jax.nn.softmax(x, axis=axis)

def _gelu(x):
    return jax.nn.gelu(x, approximate=True)

def _silu(x):
    return jax.nn.silu(x)

def _sigmoid(x):
    return jax.nn.sigmoid(x)

def _layernorm(x, axis=-1, eps=1e-05):
    m = jnp.mean(x, axis=axis, keepdims=True)
    v = jnp.var(x, axis=axis, keepdims=True)
    return (x - m) / jnp.sqrt(v + eps)

def _scatter_add(tgt, idx, src, axis=0):
    return tgt.at[idx].add(src)

def _segment_sum(src, seg, n):
    return jax.ops.segment_sum(src, seg, n)
kernel_name = 'mk_gnn_preln_d2_gnn_r8_868b84'

def setup_inputs(seed: int=0):
    np.random.seed(seed)
    _w = jnp.asarray

    def _rec_inputs():
        import jax
        import jax.numpy as jnp
        _gk = jax.random.key(seed)
        x = -8.776e-05 + 1 * jax.random.normal(jax.random.fold_in(_gk, 1), (10000, 64), jnp.float32)
        src = jax.random.randint(jax.random.fold_in(_gk, 2), (160000,), 0, 10000, jnp.int32)
        dst = jnp.minimum((10000 * jax.random.uniform(jax.random.fold_in(_gk, 3), (160000,)) ** 2.0).astype(jnp.int32), 79999)
        _o = jnp.argsort(dst, stable=True)
        src = src[_o]
        dst = dst[_o]
        edge_attr_64 = 2.93046e-05 + 1.00006 * jax.random.normal(jax.random.fold_in(_gk, 11), (160000, 64), jnp.float32)
        return (x, src, dst, edge_attr_64)
    x, src, dst, edge_attr_64 = _rec_inputs()

    def _L0_gnn_setup():
        import jax, jax.numpy as jnp
        import numpy as np
        N, E, D, L = (10000, 160000, 64, 4)
        EPS = 1e-07
        LN_EPS = 1e-05

        def _ln(h, g, b):
            mu = h.mean(-1, keepdims=True)
            var = ((h - mu) ** 2).mean(-1, keepdims=True)
            return (h - mu) / jnp.sqrt(var + LN_EPS) * g + b

        def _genconv(x, src, dst, ea, W1, b1, lg, lb, W2, b2, t):
            m = jax.nn.relu(x[src] + ea) + EPS
            logits = m * t
            mx = jax.ops.segment_max(logits, dst, num_segments=N)
            e = jnp.exp(logits - mx[dst])
            denom = jax.ops.segment_sum(e, dst, num_segments=N)
            alpha = e / denom[dst]
            agg = jax.ops.segment_sum(m * alpha, dst, num_segments=N)
            h = agg + x
            h = h @ W1 + b1
            h = jax.nn.relu(_ln(h, lg, lb))
            return h @ W2 + b2
        key = jax.random.key(seed)
        ks = jax.random.split(key, 10)
        g = lambda k, shape: jax.random.normal(k, shape, jnp.float32) * 0.05
        return {'x': jax.random.normal(ks[0], (N, D), jnp.float32), 'edge_index': jax.random.randint(ks[1], (2, E), 0, N), 'edge_attr': jax.random.normal(ks[2], (E, D), jnp.float32), 'encW': g(ks[3], (D, D)), 'encb': jnp.zeros((D,), jnp.float32), 'eencW': g(ks[4], (D, D)), 'eencb': jnp.zeros((D,), jnp.float32), 'convW1': g(ks[5], (L, D, 2 * D)), 'convb1': jnp.zeros((L, 2 * D), jnp.float32), 'convLnG': jnp.ones((L, 2 * D), jnp.float32), 'convLnB': jnp.zeros((L, 2 * D), jnp.float32), 'convW2': g(ks[6], (L, 2 * D, D)), 'convb2': jnp.zeros((L, D), jnp.float32), 't': jnp.ones((L,), jnp.float32), 'normG': jnp.ones((L, D), jnp.float32), 'normB': jnp.zeros((L, D), jnp.float32), 'linW': g(ks[7], (D, D)), 'linb': jnp.zeros((D,), jnp.float32)}
    _L0_gnn_all = _L0_gnn_setup()
    _L0_gnn_in = {k: v for k, v in _L0_gnn_all.items() if k in ('encW', 'encb', 'eencW', 'eencb', 'convW1', 'convb1', 'convLnG', 'convLnB', 'convW2', 'convb2', 't', 'normG', 'normB', 'linW', 'linb')}
    del _L0_gnn_all

    def _L1_gnn_setup():
        import jax, jax.numpy as jnp
        import numpy as np
        N = 12500
        NE = 200000
        IN_DIM = 64
        OUT_DIM = 64
        H = 8
        D = OUT_DIM // H
        key = jax.random.key(seed)
        ks = jax.random.split(key, 12)
        s = 1.0 / np.sqrt(IN_DIM)
        x = jax.random.normal(ks[0], (N, IN_DIM), jnp.float32)
        edge_attr = jax.random.normal(ks[1], (NE, IN_DIM), jnp.float32)
        edge_index = jax.random.randint(ks[2], (2, NE), 0, N, dtype=jnp.int32)
        WQ = jax.random.normal(ks[3], (IN_DIM, OUT_DIM), jnp.float32) * s
        WK = jax.random.normal(ks[4], (IN_DIM, OUT_DIM), jnp.float32) * s
        WE = jax.random.normal(ks[5], (IN_DIM, OUT_DIM), jnp.float32) * s
        WV = jax.random.normal(ks[6], (IN_DIM, OUT_DIM), jnp.float32) * s
        bQ = jax.random.normal(ks[7], (OUT_DIM,), jnp.float32) * 0.01
        bK = jax.random.normal(ks[8], (OUT_DIM,), jnp.float32) * 0.01
        bE = jax.random.normal(ks[9], (OUT_DIM,), jnp.float32) * 0.01
        bV = jax.random.normal(ks[10], (OUT_DIM,), jnp.float32) * 0.01
        return {'x': x, 'edge_attr': edge_attr, 'edge_index': edge_index, 'WQ': WQ, 'bQ': bQ, 'WK': WK, 'bK': bK, 'WE': WE, 'bE': bE, 'WV': WV, 'bV': bV}
    _L1_gnn_all = _L1_gnn_setup()
    _L1_gnn_in = {k: v for k, v in _L1_gnn_all.items() if k in ('WQ', 'bQ', 'WK', 'bK', 'WE', 'bE', 'WV', 'bV')}
    del _L1_gnn_all
    return {'x': x, 'src': src, 'dst': dst, 'edge_attr_64': edge_attr_64, 'L0_gnn_encW': _L0_gnn_in['encW'], 'L0_gnn_encb': _L0_gnn_in['encb'], 'L0_gnn_eencW': _L0_gnn_in['eencW'], 'L0_gnn_eencb': _L0_gnn_in['eencb'], 'L0_gnn_convW1': _L0_gnn_in['convW1'], 'L0_gnn_convb1': _L0_gnn_in['convb1'], 'L0_gnn_convLnG': _L0_gnn_in['convLnG'], 'L0_gnn_convLnB': _L0_gnn_in['convLnB'], 'L0_gnn_convW2': _L0_gnn_in['convW2'], 'L0_gnn_convb2': _L0_gnn_in['convb2'], 'L0_gnn_t': _L0_gnn_in['t'], 'L0_gnn_normG': _L0_gnn_in['normG'], 'L0_gnn_normB': _L0_gnn_in['normB'], 'L0_gnn_linW': _L0_gnn_in['linW'], 'L0_gnn_linb': _L0_gnn_in['linb'], 'L1_gnn_WQ': _L1_gnn_in['WQ'], 'L1_gnn_bQ': _L1_gnn_in['bQ'], 'L1_gnn_WK': _L1_gnn_in['WK'], 'L1_gnn_bK': _L1_gnn_in['bK'], 'L1_gnn_WE': _L1_gnn_in['WE'], 'L1_gnn_bE': _L1_gnn_in['bE'], 'L1_gnn_WV': _L1_gnn_in['WV'], 'L1_gnn_bV': _L1_gnn_in['bV']}

def reference(x, src, dst, edge_attr_64, L0_gnn_encW, L0_gnn_encb, L0_gnn_eencW, L0_gnn_eencb, L0_gnn_convW1, L0_gnn_convb1, L0_gnn_convLnG, L0_gnn_convLnB, L0_gnn_convW2, L0_gnn_convb2, L0_gnn_t, L0_gnn_normG, L0_gnn_normB, L0_gnn_linW, L0_gnn_linb, L1_gnn_WQ, L1_gnn_bQ, L1_gnn_WK, L1_gnn_bK, L1_gnn_WE, L1_gnn_bE, L1_gnn_WV, L1_gnn_bV):
    import jax
    import jax.numpy as jnp

    def _L0_gnn_ref(x, edge_index, edge_attr, encW, encb, eencW, eencb, convW1, convb1, convLnG, convLnB, convW2, convb2, t, normG, normB, linW, linb):
        import jax, jax.numpy as jnp
        import numpy as np
        N, E, D, L = (10000, 160000, 64, 4)
        EPS = 1e-07
        LN_EPS = 1e-05

        def _ln(h, g, b):
            mu = h.mean(-1, keepdims=True)
            var = ((h - mu) ** 2).mean(-1, keepdims=True)
            return (h - mu) / jnp.sqrt(var + LN_EPS) * g + b

        def _genconv(x, src, dst, ea, W1, b1, lg, lb, W2, b2, t):
            m = jax.nn.relu(x[src] + ea) + EPS
            logits = m * t
            mx = jax.ops.segment_max(logits, dst, num_segments=N)
            e = jnp.exp(logits - mx[dst])
            denom = jax.ops.segment_sum(e, dst, num_segments=N)
            alpha = e / denom[dst]
            agg = jax.ops.segment_sum(m * alpha, dst, num_segments=N)
            h = agg + x
            h = h @ W1 + b1
            h = jax.nn.relu(_ln(h, lg, lb))
            return h @ W2 + b2
        src, dst = (edge_index[0], edge_index[1])
        x = x @ encW + encb
        ea = edge_attr @ eencW + eencb
        x = _genconv(x, src, dst, ea, convW1[0], convb1[0], convLnG[0], convLnB[0], convW2[0], convb2[0], t[0])
        for i in range(1, L):
            h = jax.nn.relu(_ln(x, normG[i], normB[i]))
            h = _genconv(h, src, dst, ea, convW1[i], convb1[i], convLnG[i], convLnB[i], convW2[i], convb2[i], t[i])
            x = x + h
        x = jax.nn.relu(_ln(x, normG[0], normB[0]))
        return x @ linW + linb

    def _L1_gnn_ref(x, edge_attr, edge_index, WQ, bQ, WK, bK, WE, bE, WV, bV):
        import jax, jax.numpy as jnp
        import numpy as np
        N = 12500
        NE = 200000
        IN_DIM = 64
        OUT_DIM = 64
        H = 8
        D = OUT_DIM // H
        n = x.shape[0]
        Qh = (x @ WQ + bQ).reshape(n, H, D)
        Kh = (x @ WK + bK).reshape(n, H, D)
        Vh = (x @ WV + bV).reshape(n, H, D)
        Eh = (edge_attr @ WE + bE).reshape(-1, H, D)
        src = edge_index[0]
        dst = edge_index[1]
        inv_sqrt_d = jnp.float32(1.0 / np.sqrt(D))
        score = Kh[src] * Qh[dst] * inv_sqrt_d * Eh
        score = jnp.exp(jnp.clip(score.sum(-1, keepdims=True), -5.0, 5.0))
        msg = Vh[src] * score
        wV = jax.ops.segment_sum(msg, dst, num_segments=n)
        return wV.reshape(n, H * D)
    edge_index = jnp.stack([src, dst])
    h = jnp.maximum(_layernorm(x, axis=-1), 0.0)
    x = x + _L0_gnn_ref(h, edge_index, edge_attr_64, L0_gnn_encW, L0_gnn_encb, L0_gnn_eencW, L0_gnn_eencb, L0_gnn_convW1, L0_gnn_convb1, L0_gnn_convLnG, L0_gnn_convLnB, L0_gnn_convW2, L0_gnn_convb2, L0_gnn_t, L0_gnn_normG, L0_gnn_normB, L0_gnn_linW, L0_gnn_linb)
    h = jnp.maximum(_layernorm(x, axis=-1), 0.0)
    x = x + _L1_gnn_ref(h, edge_attr_64, edge_index, L1_gnn_WQ, L1_gnn_bQ, L1_gnn_WK, L1_gnn_bK, L1_gnn_WE, L1_gnn_bE, L1_gnn_WV, L1_gnn_bV)
    return x

_drawn_inputs = setup_inputs


def setup_inputs(seed=0):
    import zlib

    import numpy as np

    out = dict(_drawn_inputs(seed))
    spreads = {'L0_gnn_encb': (0.0, 0.549),
     'L0_gnn_eencb': (0.0, 0.518),
     'L0_gnn_convb1': (0.0, 0.1),
     'L0_gnn_convLnG': (1.0, 0.2),
     'L0_gnn_convLnB': (0.0, 0.324),
     'L0_gnn_convb2': (0.0, 0.1),
     'L0_gnn_t': (1.0, 0.6),
     'L0_gnn_normG': (1.0, 0.2),
     'L0_gnn_normB': (0.0, 0.321),
     'L0_gnn_linb': (0.0, 0.1)}
    factors = {'L0_gnn_eencW': 3.465,
     'L1_gnn_bQ': 8.0,
     'L1_gnn_bK': 8.0,
     'L1_gnn_bE': 8.0,
     'L0_gnn_encW': 3.045}
    for name, (base, spread) in spreads.items():
        noise = np.random.default_rng([zlib.crc32(name.encode()), seed]).standard_normal(out[name].shape)
        drawn = base * np.exp(spread * noise) if base else spread * noise
        out[name] = jnp.asarray(drawn.astype(out[name].dtype))
    for name, factor in factors.items():
        out[name] = (out[name] * factor).astype(out[name].dtype)
    return out
```

```python
from contextlib import ExitStack

import concourse.bass as bass
from concourse import mybir

N, E, D = 10000, 160000, 64
L, H = 4, 8
P = 128
EP = E // P
T = 25
NCH = EP // T
NPAIR = NCH // 2
NP = 125
NJ = N // NP
G = 8
NG = NJ // G
NGP = NG // 2
W = T + 1
WM = T + 2
HB = 128
HR = -(-N // HB)
BIG = 1.0e30
EPS, LN_EPS = 1e-7, 1e-5
C = 2
GATH = 16 * T
NGATH = 16 * G
INV_SQRT_HD = (D // H) ** -0.5

F32, I32, BF16 = mybir.dt.float32, mybir.dt.int32, mybir.dt.bfloat16
ALU, ACT, AX = mybir.AluOpType, mybir.ActivationFunctionType, mybir.AxisListType


def gnn_kernel(nc, a, out):
    ctx = ExitStack()
    with ctx:
        def sb(name, shape, dt=F32):
            return ctx.enter_context(nc.sbuf_tensor(name, shape, dt))

        def sem(name):
            return ctx.enter_context(nc.semaphore(name))

        def dram(name, shape, dt=F32):
            return nc.dram_tensor(name, shape, dt, kind="Internal").ap()

        def flat(t):
            return t[:, :, :].rearrange("p a b -> p (a b)")

        def groups(t, c):
            return t.rearrange("p (g c) -> p g c", c=c)

        xtab = dram("xtab", (N, D))
        kvtab = dram("kvtab", (N, 2 * D))
        qtab = dram("qtab", (N, D))
        qstart = dram("qstart", (E, D))
        ndrows = dram("ndrows", (E + 1, 2 * D))
        msrows = dram("msrows", (E + 1, D))
        endtab = dram("endtab", (NP, NJ), I32)
        starttab = dram("starttab", (NP, NJ), I32)
        cnttab = dram("cnttab", (HR, HB))

        ident = sb("ident", [P, P])
        tri = sb("tri", [P, P])
        start_f = sb("start_f", [P, EP + 1])
        headneg = sb("headneg", [P, EP])
        x_res = sb("x_res", [NP, NJ * D])
        eew = sb("eew", [D + 1, D])
        wew = sb("wew", [D + 1, D])
        encw = sb("encw", [D + 1, D])
        linw = sb("linw", [D + 1, D])
        kvqw = sb("kvqw", [D + 1, 3 * D])
        w1 = sb("w1", [D + 1, L * 2 * D])
        w1m = sb("w1m", [D + 1, L])
        w2 = sb("w2", [2 * D, L * D])
        b2 = sb("b2", [1, L * D])
        lng = sb("lng", [2 * D, L])
        lnb = sb("lnb", [2 * D, L])
        tcol = sb("tcol", [P, L])
        ng = sb("ng", [NP, L * D])
        nb = sb("nb", [NP, L * D])
        ones1 = sb("ones1", [1, P])
        epscol = sb("epscol", [P, 1])

        attr = [sb(f"attr{s}", [D + 1, T * P]) for s in range(2)]
        idx = [sb(f"idx{s}", [P, T], I32) for s in range(2)]
        kvg = [sb(f"kvg{s}", [P, T, 2 * D]) for s in range(2)]
        rows = [sb(f"rows{s}", [P, T, 2 * D]) for s in range(2)]
        zbuf = sb("zbuf", [P, D, T])
        mbuf = [sb(f"mbuf{s}", [P, D, T]) for s in range(2)]
        lbuf = sb("lbuf", [P, D, WM])
        flagx = sb("flagx", [P, D, WM])
        smax = sb("smax", [P, D, WM])
        wbuf = sb("wbuf", [P, D, T])
        ebuf = sb("ebuf", [P, D, W])
        fbuf = sb("fbuf", [P, D, W])
        mebuf = sb("mebuf", [P, D, W])
        dscan = sb("dscan", [P, D, W])
        nscan = sb("nscan", [P, D, W])
        headr = sb("headr", [P, D])
        headr2 = sb("headr2", [P, D])
        xg = [flat(k)[:, 0:T * D].rearrange("p (t c) -> p t c", c=D) for k in kvg]
        zt = flat(zbuf).rearrange("p (t c) -> p t c", c=D)
        keepx = flat(flagx)[:, 0:D * W].rearrange("p (c t) -> p c t", t=W)
        msout = [flat(r)[:, 0:T * D].rearrange("p (t c) -> p t c", c=D) for r in rows]
        qs = [flat(r)[:, T * D:2 * T * D].rearrange("p (t c) -> p t c", c=D) for r in rows]
        score = sb("score", [P, T, H])

        hidx = sb("hidx", [P, 1], I32)
        cont = sb("cont", [P, 1])
        contneg = sb("contneg", [P, 1])
        passneg = sb("passneg", [P, P])
        passkeep = sb("passkeep", [P, P])
        tailr = sb("tailr", [P, 2, D])
        rsc = sb("rsc", [P, P + 1])
        xsc = sb("xsc", [P, P + 1])
        g12 = sb("g12", [P, 2, P])
        headnd = sb("headnd", [P, 2 * D])
        rcar = sb("rcar", [P, D])
        ab = sb("ab", [P, 2, D])
        fixed = sb("fixed", [P, 2 * D])
        qhead = sb("qhead", [P, D])
        dsthead = sb("dsthead", [P, 1], I32)

        nidx = [sb(f"nidx{s}", [NP, G], I32) for s in range(2)]
        nd = [kvg[s][0:NP, 0:G, :] for s in range(2)]
        xold = [groups(flat(rows[s])[0:NP, 0:G * D], D) for s in range(2)]
        xnew = [groups(flat(rows[s])[0:NP, G * D:2 * G * D], D) for s in range(2)]
        kvq = [groups(flat(rows[s])[0:NP, 2 * G * D:5 * G * D], 3 * D) for s in range(2)]
        recd = groups(flat(zbuf)[0:NP, 0:G * D], D)
        h0 = groups(flat(zbuf)[0:NP, G * D:2 * G * D], D)
        h0T = sb("h0T", [D + 1, G * P])
        sqb = groups(flat(mbuf[0])[0:NP, 0:2 * G * D], 2 * D)
        hn = groups(flat(mbuf[1])[0:NP, 0:2 * G * D], 2 * D)
        hrT = flat(wbuf)[:, 0:G * P]
        lnx = groups(flat(dscan)[0:NP, 0:G * D], D)
        lnsq = groups(flat(dscan)[0:NP, G * D:2 * G * D], D)
        ss, std, rstd = (sb(n, [NP, G]) for n in ("ss", "std", "rstd"))
        mu, ss2, std2, rstd2 = (sb(n, [NP, G]) for n in ("mu", "ss2", "std2", "rstd2"))

        PS = ctx.enter_context(nc.psum_tensor("PS", [P, 4096], F32))
        ea = [PS[:, s * 2048:s * 2048 + T * D].rearrange("p (t c) -> p t c", c=D) for s in range(2)]
        psT = PS[0:D, 0:G * P].rearrange("p (g c) -> p g c", c=P)
        psH = PS[0:NP, 1024:2048].rearrange("p (g c) -> p g c", c=2 * D)
        psN = PS[:, 2048:3072].rearrange("p (g c) -> p g c", c=P)
        psX = PS[0:NP, 3072:3072 + G * D].rearrange("p (g c) -> p g c", c=D)
        psK = PS[0:NP, 1024:1024 + G * 256].rearrange("p (g c) -> p g c", c=256)
        psA, psB = PS[:, 3712:3840], PS[:, 3840:3968]
        psA2, psB2 = PS[:, 1664:1792], PS[:, 1792:1920]
        psHist = PS[0:HR, 3584:3584 + HB]
        psOff = PS[0:NP, 3712:3713]

        dst_i = flat(kvg[0])[:, 0:EP].bitcast(I32)
        dst_f = flat(kvg[0])[:, EP:2 * EP]
        ne_f = flat(kvg[1])[:, 0:EP]
        tmp_i = flat(kvg[1])[:, EP:2 * EP].bitcast(I32)
        hi_b = flat(rows[0])[:, 2560:2560 + EP // 2].bitcast(BF16)
        lo_b = flat(rows[1])[:, 2560:2560 + EP // 2].bitcast(BF16)
        iota_i = flat(smax)[:, 0:HB].bitcast(I32)
        iota_b = flat(smax)[:, HB:HB + HB // 2].bitcast(BF16)
        zero_b = flat(smax)[:, 2 * HB:2 * HB + HB // 2].bitcast(BF16)
        pcol_i = flat(smax)[:, 3 * HB:3 * HB + 1].bitcast(I32)
        col = [flat(smax)[:, 3 * HB + 1 + n:3 * HB + 2 + n] for n in range(8)]
        dprev = flat(smax)[:, 3 * HB + 16:3 * HB + 17].bitcast(I32)
        wbc = flat(smax)[:, 4 * HB:5 * HB]
        oh_lo = [flat(b)[:, 0:T * HB // 2].bitcast(BF16).rearrange("p (t c) -> p t c", c=HB) for b in (ebuf, fbuf)]
        oh_hi = [flat(b)[:, 0:T * HR // 2 + 1].bitcast(BF16)[:, 0:T * HR].rearrange("p (t c) -> p t c", c=HR)
                 for b in (nscan, lbuf)]
        cntbuf = flat(dscan)[0:HR, 0:HB]
        cnt = flat(smax)[0:NP, 5 * HB:5 * HB + NJ]
        cum = flat(smax)[0:NP, 6 * HB:6 * HB + NJ]
        has = flat(smax)[0:NP, 7 * HB:7 * HB + NJ]
        epos = flat(smax)[0:NP, 8 * HB:8 * HB + NJ]
        epos_i = flat(smax)[0:NP, 9 * HB:9 * HB + NJ].bitcast(I32)
        spos = flat(smax)[0:NP, 10 * HB:10 * HB + NJ]
        spos_i = flat(smax)[0:NP, 11 * HB:11 * HB + NJ].bitcast(I32)
        nrow = flat(smax)[0:1, 12 * HB:12 * HB + 2 * D]

        attrT = a["attrT"].rearrange("k (c m) -> k c m", c=NCH)
        src_v = a["src"].rearrange("(p e) -> p e", p=P)
        dst_v = a["dst"].rearrange("(p e) -> p e", p=P)
        x_v = a["x"].rearrange("(p j) c -> p j c", p=NP)
        out_v = out.rearrange("(p j) c -> p j c", p=NP)
        xtab_v = xtab.rearrange("(p j) c -> p j c", p=NP)
        kvtab_v = kvtab.rearrange("(p j) c -> p j c", p=NP)
        qtab_v = qtab.rearrange("(p j) c -> p j c", p=NP)
        nd_v = ndrows[0:E, :].rearrange("(p e) c -> p e c", p=P)
        ms_v = msrows[0:E, :].rearrange("(p e) c -> p e c", p=P)
        qst_v = qstart.rearrange("(p e) c -> p (e c)", p=P)
        qst_t = qstart.rearrange("(p e) c -> p e c", p=P)
        cnt_v = cnttab.rearrange("a b -> (a b)")[0:N].rearrange("(p j) -> p j", p=NP)
        x3 = x_res[:, :].rearrange("p (j c) -> p j c", c=D)

        w_in, x_in, dst_in = sem("w_in"), sem("x_in"), sem("dst_in")
        pool_pro, dve_pro, act_pro = sem("pool_pro"), sem("dve_pro"), sem("act_pro")
        qzero, const_out, cnt_out, cnt_in, tab_out = (sem(n) for n in "qzero const_out cnt_out cnt_in tab_out".split())
        dp_in, zero_done, onehots, hist, passT, offs = (sem(n) for n in "dp_in zero_done onehots hist passT offs".split())
        attr_in = [sem(f"attr_in{s}") for s in range(2)]
        idx_in = [sem(f"idx_in{s}") for s in range(2)]
        gathered = [sem(f"gathered{s}") for s in range(2)]
        stored = [sem(f"stored{s}") for s in range(2)]
        ea_done, z_done, m_done, l_done, flag_done = (sem(n) for n in "ea_done z_done m_done l_done flag_done".split())
        s_done, w_done, hadd_done, hred_done, hmax_done, cs_done = (
            sem(n) for n in "s_done w_done hadd_done hred_done hmax_done cs_done".split())
        er_done, fr_done, e_done, f_done = (sem(n) for n in "er_done fr_done e_done f_done".split())
        me_done, d_done, n_done, cd_done, cn_done, rows_done = (
            sem(n) for n in "me_done d_done n_done cd_done cn_done rows_done".split())
        reset_done = sem("reset_done")
        tail_done, br_pe, br_dve, br_act = (sem(n) for n in "tail_done br_pe br_dve br_act".split())
        head_in, head_out = sem("head_in"), sem("head_out")
        nidx_in = [sem(f"nidx_in{s}") for s in range(2)]
        nd_in = [sem(f"nd_in{s}") for s in range(2)]
        xold_in = [sem(f"xold_in{s}") for s in range(2)]
        xnew_out = [sem(f"xnew_out{s}") for s in range(2)]
        rec_done, agg_done, h0_done, h0T_done, h0c_done, hw1_done, sq_done, ss_done, std_done, rstd_done = (
            sem(n) for n in "rec_done agg_done h0_done h0T_done h0c_done hw1_done sq_done ss_done std_done rstd_done".split())
        hn_done, hnT_done, hr_done, hw2_done, xadd_done = (
            sem(n) for n in "hn_done hnT_done hr_done hw2_done xadd_done".split())
        ln_dve, ln_std, aff_done, xnew_done = (sem(n) for n in "ln_dve ln_std aff_done xnew_done".split())
        p_ln, p_std, p_h, p_hT, p_hc, p_x, p_new = (
            sem(n) for n in "p_ln p_std p_h p_hT p_hc p_x p_new".split())
        p_out = [sem(f"p_out{s}") for s in range(2)]
        q_in = [sem(f"q_in{s}") for s in range(2)]
        q_free = sem("q_free")
        q_out = [sem(f"q_out{s}") for s in range(2)]
        q_sc = [sem(f"q_sc{s}") for s in range(2)]
        q_hT, q_hc, q_lin, q_x1, q_ln, q_std, q_h, q_h2T, q_h2c, q_kvq, q_kc = (
            sem(n) for n in "q_hT q_hc q_lin q_x1 q_ln q_std q_h q_h2T q_h2c q_kvq q_kc".split())
        qs_in = [sem(f"qs_in{s}") for s in range(2)]
        ms_out = [sem(f"ms_out{s}") for s in range(2)]
        keep_done, qv_done, qsc_done, qc_done, kq_done, sr_done, c1_done, c2_done, ex_done, msg_done, ssc_done, sc_done, ro_done = (
            sem(n) for n in ("keep_done qv_done qsc_done qc_done kq_done sr_done c1_done c2_done ex_done msg_done "
                             "ssc_done sc_done ro_done").split())
        qhead_in, a_reset = sem("qhead_in"), sem("a_reset")
        b_pe, b_dve, mhead_in, mhead_out = (sem(n) for n in "b_pe b_dve mhead_in mhead_out".split())
        o_idx = [sem(f"o_idx{s}") for s in range(2)]
        o_in = [sem(f"o_in{s}") for s in range(2)]
        o_out = [sem(f"o_out{s}") for s in range(2)]
        o_done = sem("o_done")

        LNK = 7
        BRK = 13
        NW = 20
        block = ctx.enter_context(nc.Block())

        held = {e: sem(f"held_{e}") for e in ("sp", "pool", "act", "pe", "dve")}

        def hold(eng, name):
            eng.sem_inc(held[name], 1)

        @block.sync
        def _(sp):
            sp.dma_start(dst_i, dst_v).then_inc(dst_in, 16)
            sp.dma_start(x_res[:, :], x_v.rearrange("p j c -> p (j c)")).then_inc(x_in, 16)
            loads = [
                (eew[0:D, :], a["eencW"]), (eew[D:D + 1, :], a["eencb"].unsqueeze(0)),
                (wew[0:D, :], a["WE"]), (wew[D:D + 1, :], a["bE"].unsqueeze(0)),
                (encw[0:D, :], a["encW"]), (encw[D:D + 1, :], a["encb"].unsqueeze(0)),
                (linw[0:D, :], a["linW"]), (linw[D:D + 1, :], a["linb"].unsqueeze(0)),
                (kvqw[0:D, 0:D], a["WK"]), (kvqw[D:D + 1, 0:D], a["bK"].unsqueeze(0)),
                (kvqw[0:D, D:2 * D], a["WV"]), (kvqw[D:D + 1, D:2 * D], a["bV"].unsqueeze(0)),
                (kvqw[0:D, 2 * D:3 * D], a["WQ"]), (kvqw[D:D + 1, 2 * D:3 * D], a["bQ"].unsqueeze(0)),
                (w1[0:D, :].rearrange("k (l n) -> k l n", l=L), a["convW1"].rearrange("l k n -> k l n")),
                (w1[D:D + 1, :], a["convb1"].rearrange("l n -> (l n)").unsqueeze(0)),
                (w2[:, :].rearrange("k (l n) -> k l n", l=L), a["convW2"].rearrange("l k n -> k l n")),
                (b2[:, :], a["convb2"].rearrange("l n -> (l n)").unsqueeze(0)),
                (lng[:, :], a["convLnG_T"]), (lnb[:, :], a["convLnB_T"]),
            ]
            assert len(loads) == NW
            for dst, src in loads:
                sp.dma_start(dst, src).then_inc(w_in, 16)
            sp.dma_start(tcol[:, :], a["t"].partition_broadcast(P)).then_inc(w_in, 16)
            for dst, src in ((ng, a["normG"]), (nb, a["normB"])):
                sp.dma_start(dst[:, 0:(L - 1) * D], src[1:L, :].rearrange("l c -> (l c)").partition_broadcast(NP)).then_inc(w_in, 16)
                sp.dma_start(dst[:, (L - 1) * D:], src[0, :].partition_broadcast(NP)).then_inc(w_in, 16)
            sp.wait_ge(dve_pro, 1)
            sp.dma_start(dprev[1:P, :], dst_v[0:P - 1, EP - 1:EP], allow_slow_non_contiguous=True).then_inc(dp_in, 16)
            sp.wait_ge(dve_pro, 2)
            sp.dma_start(ndrows[E:E + 1, :], nrow).then_inc(const_out, 16)
            sp.dma_start(msrows[E:E + 1, :], nrow[:, 0:D]).then_inc(const_out, 16)
            sp.wait_ge(dve_pro, 3)
            with sp.Fori(0, NCH) as c:
                sp.dma_start(qst_v[:, bass.ds(c * T * D, T * D)], flat(mebuf)[:, 0:T * D]).then_inc(qzero, 16)
            with sp.Fori(0, NGP) as i:
                for s in range(2):
                    q = sp.snap(i * 2 + s)
                    sp.wait_ge(p_new, q + 1)
                    sp.dma_start(xtab_v[:, bass.ds(q * G, G), :], xnew[s]).then_inc(p_out[s], 16)
            sp.wait_ge(dve_pro, 5)
            sp.dma_start(cnttab, cntbuf).then_inc(cnt_out, 16)
            sp.wait_ge(cnt_out, 16)
            sp.dma_start(cnt, cnt_v).then_inc(cnt_in, 16)
            sp.wait_ge(dve_pro, 7)
            sp.dma_start(endtab, epos_i).then_inc(tab_out, 16)
            sp.dma_start(starttab, spos_i).then_inc(tab_out, 16)
            sp.wait_ge(tab_out, 32)

            def load_chunk(c, g, u, s):
                sp.wait_ge(ea_done, g + 1)
                sp.dma_start(attr[s][0:D, :], attrT[:, c, :]).then_inc(attr_in[s], 16)
                sp.wait_ge(z_done, g + 1)
                sp.dma_start(idx[s][:, :], src_v[:, bass.ds(c * T, T)]).then_inc(idx_in[s], 16)

            def load_group(layer, j, s):
                u = sp.snap(layer * NGP + j)
                sp.wait_ge(h0_done, u * 2 + s + 1)
                sp.dma_start(nidx[s][:, :], endtab[:, bass.ds((j * 2 + s) * G, G)]).then_inc(nidx_in[s], 16)
                sp.dma_start(xold[s], xtab_v[:, bass.ds((j * 2 + s) * G, G), :]).then_inc(xold_in[s], 16)

            def store_group(layer, j, s):
                sp.wait_ge(xnew_done, layer * NG + j * 2 + s + 1)
                sp.dma_start(xtab_v[:, bass.ds((j * 2 + s) * G, G), :], xnew[s]).then_inc(xnew_out[s], 16)

            with sp.Fori(0, L) as layer:
                with sp.Fori(0, NPAIR) as i:
                    for s in range(2):
                        c = sp.snap(i * 2 + s)
                        load_chunk(c, sp.snap(layer * NCH + c), sp.snap(layer * NPAIR + i), s)
                for s in range(2):
                    sp.wait_ge(stored[s], layer * (16 * NPAIR) + 16 * (NPAIR + 1))
                for s in range(2):
                    load_group(layer, 0, s)
                with sp.Fori(0, NGP - 1) as j:
                    for s in range(2):
                        store_group(layer, j, s)
                        load_group(layer, j + 1, s)
                for s in range(2):
                    store_group(layer, NGP - 1, s)

            with sp.Fori(0, NGP) as i:
                for s in range(2):
                    q = sp.snap(i * 2 + s)
                    sp.wait_ge(q_kc, q + 1)
                    for n in range(2):
                        sp.wait_ge(xnew_out[n], 16 * (L * NGP + 1))
                    sp.dma_start(xold[s], xtab_v[:, bass.ds(q * G, G), :]).then_inc(q_in[s], 16)
                    sp.dma_start(xnew[s], x_v[:, bass.ds(q * G, G), :]).then_inc(q_in[s], 16)
                    sp.wait_ge(q_free, q + 1)
                    hold(sp, "sp")
                    sp.dma_start(nidx[s][:, :], starttab[:, bass.ds(q * G, G)]).then_inc(q_in[s], 16)

            for s in range(2):
                sp.wait_ge(q_sc[s], NGP * NGATH)
                sp.wait_ge(q_out[s], NGP * 32 + 32)
            with sp.Fori(0, NPAIR) as i:
                for s in range(2):
                    c = sp.snap(i * 2 + s)
                    load_chunk(c, sp.snap(c + L * NCH), sp.snap(i + L * NPAIR), s)
                    sp.wait_ge(qv_done, c + 1)
                    sp.dma_start(qs[s], qst_t[:, bass.ds(c * T, T), :]).then_inc(qs_in[s], 16)

            for s in range(2):
                sp.wait_ge(ms_out[s], 16 * (NPAIR + 1))

            def load_out(j, s):
                sp.wait_ge(o_done, j * 2 + s + 1)
                sp.dma_start(nidx[s][:, :], endtab[:, bass.ds((j * 2 + s) * G, G)]).then_inc(o_idx[s], 16)

            def store_out(j, s):
                sp.wait_ge(o_done, j * 2 + s + 1 + C)
                sp.dma_start(out_v[:, bass.ds((j * 2 + s) * G, G), :], xnew[s]).then_inc(o_out[s], 16)

            for s in range(2):
                load_out(0, s)
            with sp.Fori(0, NGP - 1) as j:
                for s in range(2):
                    store_out(j, s)
                    load_out(j + 1, s)
            for s in range(2):
                store_out(NGP - 1, s)
            for s in range(2):
                sp.wait_ge(o_out[s], 16 * (NGP + 1))

        @block.gpsimd
        def _(pool):
            pool.sem_inc(q_free, C)
            pool.memset(ident[:, :], 0.0).then_inc(pool_pro, 1)
            pool.memset(tri[:, :], 1.0).then_inc(pool_pro, 1)
            pool.iota(iota_i, pattern=[[1, HB]], base=0, channel_multiplier=0).then_inc(pool_pro, 1)
            pool.iota(pcol_i, pattern=[[0, 1]], base=EP - 1, channel_multiplier=EP).then_inc(pool_pro, 1)
            pool.wait_ge(pool_pro, 4)
            pool.affine_select(out=ident[:, :], in_=ident[:, :], compare_op=ALU.not_equal, fill=1.0, base=0,
                               pattern=[[-1, P]], channel_multiplier=1).then_inc(pool_pro, 1)
            pool.affine_select(out=tri[:, :], in_=tri[:, :], compare_op=ALU.is_gt, fill=0.0, base=0,
                               pattern=[[1, P]], channel_multiplier=-1).then_inc(pool_pro, 1)

            for s in range(2):
                pool.wait_ge(p_out[s], 16 * (NGP + 1))
            with pool.Fori(0, L) as layer:
                with pool.Fori(0, NPAIR) as i:
                    for s in range(2):
                        g = pool.snap(layer * NCH + i * 2 + s)
                        u = pool.snap(layer * NPAIR + i)
                        pool.wait_ge(idx_in[s], (u + 1) * 16)
                        pool.wait_ge(z_done, g + 1)
                        hold(pool, "pool")
                        for k in range(T):
                            pool.indirect_dma_start(xg[s][:, k, :], None, xtab,
                                                    bass.IndirectOffsetOnAxis(ap=idx[s][:, k:k + 1], axis=0)).then_inc(gathered[s], 16)
                for s in range(2):
                    pool.wait_ge(stored[s], layer * (16 * NPAIR) + 16 * (NPAIR + 1))
                pool.wait_ge(const_out, 32)
                hold(pool, "pool")
                pool.indirect_dma_start(headnd[:, :], None, ndrows,
                                        bass.IndirectOffsetOnAxis(ap=hidx[:, :], axis=0)).then_inc(head_in, 16)
                pool.wait_ge(br_dve, layer * BRK + BRK)
                hold(pool, "pool")
                pool.indirect_dma_start(ndrows, bass.IndirectOffsetOnAxis(ap=hidx[:, :], axis=0),
                                        fixed[:, :], None).then_inc(head_out, 16)
                pool.wait_ge(head_out, layer * 16 + 16)
                hold(pool, "pool")
                with pool.Fori(0, NGP) as j:
                    for s in range(2):
                        u = pool.snap(layer * NGP + j)
                        pool.wait_ge(nidx_in[s], (u + 1) * 16)
                        pool.wait_ge(h0_done, u * 2 + s + 1)
                        hold(pool, "pool")
                        for k in range(G):
                            pool.indirect_dma_start(nd[s][:, k, :], None, ndrows,
                                                    bass.IndirectOffsetOnAxis(ap=nidx[s][:, k:k + 1], axis=0)).then_inc(nd_in[s], 16)
                for s in range(2):
                    pool.wait_ge(xnew_out[s], layer * (16 * NGP) + 16 * (NGP + 1))

            pool.wait_ge(qzero, 16 * NCH)
            with pool.Fori(0, NGP) as i:
                for s in range(2):
                    pool.wait_ge(q_in[s], i * 48 + 48)
                    pool.wait_ge(q_kc, i * 2 + s + 1 + C)
                    hold(pool, "pool")
                    for k in range(G):
                        pool.indirect_dma_start(qstart, bass.IndirectOffsetOnAxis(ap=nidx[s][:, k:k + 1], axis=0),
                                                kvq[s][:, k, 2 * D:3 * D], None,
                                                bounds_check=E - 1, oob_is_err=False).then_inc(q_sc[s], 16)
                    pool.wait_ge(q_sc[s], i * NGATH + NGATH)
                    pool.sem_inc(q_free, 1)
            for s in range(2):
                pool.wait_ge(q_out[s], NGP * 32 + 32)
            pool.indirect_dma_start(qhead[:, :], None, qtab,
                                    bass.IndirectOffsetOnAxis(ap=dsthead[:, :], axis=0)).then_inc(qhead_in, 16)
            with pool.Fori(0, NPAIR) as i:
                for s in range(2):
                    pool.wait_ge(idx_in[s], i * 16 + (16 + 16 * L * NPAIR))
                    pool.wait_ge(msg_done, i * 2 + s + 1)
                    hold(pool, "pool")
                    for k in range(T):
                        pool.indirect_dma_start(kvg[s][:, k, :], None, kvtab,
                                                bass.IndirectOffsetOnAxis(ap=idx[s][:, k:k + 1], axis=0)).then_inc(gathered[s], 16)
            for s in range(2):
                pool.wait_ge(ms_out[s], 16 * (NPAIR + 1))
            pool.indirect_dma_start(headnd[:, 0:D], None, msrows,
                                    bass.IndirectOffsetOnAxis(ap=hidx[:, :], axis=0)).then_inc(mhead_in, 16)
            pool.wait_ge(b_dve, 3)
            pool.indirect_dma_start(msrows, bass.IndirectOffsetOnAxis(ap=hidx[:, :], axis=0),
                                    fixed[:, 0:D], None).then_inc(mhead_out, 16)
            pool.wait_ge(mhead_out, 16)
            with pool.Fori(0, NGP) as j:
                for s in range(2):
                    pool.wait_ge(o_idx[s], j * 16 + 16)
                    pool.wait_ge(o_done, j * 2 + s + 1)
                    hold(pool, "pool")
                    for k in range(G):
                        pool.indirect_dma_start(nd[s][:, k, 0:D], None, msrows,
                                                bass.IndirectOffsetOnAxis(ap=nidx[s][:, k:k + 1], axis=0)).then_inc(o_in[s], 16)

        @block.scalar
        def _(act):
            for x in (l_done, flag_done, er_done, fr_done, e_done, f_done, rows_done, qv_done, q_kc, ro_done):
                act.sem_inc(x, C)
            for s in range(2):
                act.sem_inc(stored[s], 16)
                act.sem_inc(ms_out[s], 16)

            with act.Fori(0, NG) as q:
                act.wait_ge(p_ln, q * LNK + 5)
                act.activation(std2[:, :], ss2[:, :], ACT.Sqrt, bias=epscol[0:NP, :], scale=1.0 / D).then_inc(p_std, 1)
                act.wait_ge(p_hT, q + 1)
                act.activation(h0T[0:D, :].rearrange("p (g c) -> p g c", c=P)[:, :, 0:NP], psT[:, :, 0:NP], ACT.Copy).then_inc(p_hc, 1)

            def flags_and_logits(c, g, s, layer):
                act.wait_ge(s_done, g + C)
                act.activation(flagx[:, :, 1:T + 1],
                               start_f[:, bass.ds(c * T + 1, T)].unsqueeze(1).to_broadcast([P, D, T]),
                               ACT.Copy, scale=-BIG).then_inc(flag_done, 1)
                act.wait_ge(m_done, g + 1 + C)
                act.wait_ge(cs_done, g + C)
                hold(act, "act")
                act.activation(lbuf[:, :, 1:T + 1], mbuf[s][:, :, :], ACT.Copy, scale=tcol[:, bass.ds(layer, 1)]).then_inc(l_done, 1)

            def exponentials(g):
                act.wait_ge(w_done, g + 1 + C)
                act.wait_ge(cn_done, g + C)
                act.activation(ebuf[:, :, 1:W], wbuf[:, :, :], ACT.Relu, scale=-1.0).then_inc(er_done, 1)
                act.activation(fbuf[:, :, 1:W], wbuf[:, :, :], ACT.Relu).then_inc(fr_done, 1)
                act.wait_ge(er_done, g + 1 + C)
                act.activation(ebuf[:, :, 1:W], ebuf[:, :, 1:W], ACT.Exp, scale=-1.0).then_inc(e_done, 1)
                act.wait_ge(fr_done, g + 1 + C)
                act.activation(fbuf[:, :, 1:W], fbuf[:, :, 1:W], ACT.Exp, scale=-1.0).then_inc(f_done, 1)

            def store_rows(c, g, u, s):
                act.wait_ge(n_done, g + 1 + C)
                act.wait_ge(stored[s], u * 16 + 16)
                act.activation(rows[s][:, :, 0:D].rearrange("p t c -> p c t"), nscan[:, :, 1:W], ACT.Copy)
                act.activation(rows[s][:, :, D:2 * D].rearrange("p t c -> p c t"), dscan[:, :, 1:W], ACT.Copy).then_inc(rows_done, 1)
                act.wait_ge(rows_done, g + 1 + C)
                act.dma_start(nd_v[:, bass.ds(c * T, T), :], rows[s][:, :, :]).then_inc(stored[s], 16)

            with act.Fori(0, L) as layer:
                g0 = act.snap(layer * NCH)
                u0 = act.snap(layer * NPAIR)
                act.wait_ge(reset_done, layer + 1)
                flags_and_logits(0, g0, 0, layer)
                exponentials(g0)
                with act.Fori(0, NPAIR - 1) as i:
                    for s in range(2):
                        c = act.snap(i * 2 + s)
                        g = act.snap(g0 + c)
                        flags_and_logits(c + 1, g + 1, 1 - s, layer)
                        store_rows(c, g, u0 + i, s)
                        exponentials(g + 1)
                flags_and_logits(NCH - 1, g0 + (NCH - 1), 1, layer)
                store_rows(NCH - 2, g0 + (NCH - 2), u0 + (NPAIR - 1), 0)
                exponentials(g0 + (NCH - 1))
                store_rows(NCH - 1, g0 + (NCH - 1), u0 + (NPAIR - 1), 1)
                act.activation(tailr[:, :, :], smax[:, :, T].unsqueeze(1).to_broadcast([P, 2, D]), ACT.Copy).then_inc(tail_done, 1)
                act.wait_ge(br_dve, layer * BRK + 4)
                act.activation(g12[:, :, :], g12[:, :, :], ACT.Exp).then_inc(br_act, 1)
                act.wait_ge(br_dve, layer * BRK + 10)
                act.activation(ab[:, :, :], ab[:, :, :], ACT.Exp).then_inc(br_act, 1)
                with act.Fori(0, NG) as j:
                    q = act.snap(layer * NG + j)
                    act.wait_ge(h0T_done, q + 1)
                    act.activation(h0T[0:D, :].rearrange("p (g c) -> p g c", c=P)[:, :, 0:NP], psT[:, :, 0:NP], ACT.Copy).then_inc(h0c_done, 1)
                    act.wait_ge(hw1_done, q + 1)
                    act.activation(sqb, psH, ACT.Square).then_inc(sq_done, 1)
                    act.wait_ge(ss_done, q + 1)
                    act.activation(std[:, :], ss[:, :], ACT.Sqrt, bias=epscol[0:NP, :], scale=1.0 / (2 * D)).then_inc(std_done, 1)
                    act.wait_ge(hnT_done, q + 1)
                    act.activation(hrT.rearrange("p (g c) -> p g c", c=P)[:, :, 0:NP], psN[:, :, 0:NP], ACT.Relu,
                                   bias=lnb[:, bass.ds(layer, 1)], scale=lng[:, bass.ds(layer, 1)]).then_inc(hr_done, 1)
                    act.wait_ge(ln_dve, q * LNK + 5)
                    act.activation(std2[:, :], ss2[:, :], ACT.Sqrt, bias=epscol[0:NP, :], scale=1.0 / D).then_inc(ln_std, 1)

            for s in range(2):
                act.sem_inc(q_out[s], 32)
            with act.Fori(0, NGP) as i:
                for s in range(2):
                    q = act.snap(i * 2 + s)
                    act.wait_ge(q_hT, q + 1)
                    act.activation(h0T[0:D, :].rearrange("p (g c) -> p g c", c=P)[:, :, 0:NP], psT[:, :, 0:NP], ACT.Copy).then_inc(q_hc, 1)
                    act.wait_ge(q_ln, q * LNK + 5)
                    act.activation(std2[:, :], ss2[:, :], ACT.Sqrt, bias=epscol[0:NP, :], scale=1.0 / D).then_inc(q_std, 1)
                    act.wait_ge(q_h2T, q + 1)
                    act.activation(h0T[0:D, :].rearrange("p (g c) -> p g c", c=P)[:, :, 0:NP], psT[:, :, 0:NP], ACT.Copy).then_inc(q_h2c, 1)
                    act.wait_ge(q_kvq, q + 1)
                    act.wait_ge(q_out[s], i * 32 + 32)
                    act.wait_ge(q_free, q + 1)
                    act.activation(kvq[s], psK[:, :, 0:3 * D], ACT.Copy).then_inc(q_kc, 1)
                    act.wait_ge(q_kc, q + 1 + C)
                    act.dma_start(kvtab_v[:, bass.ds(q * G, G), :], kvq[s][:, :, 0:2 * D]).then_inc(q_out[s], 16)
                    act.dma_start(qtab_v[:, bass.ds(q * G, G), :], kvq[s][:, :, 2 * D:3 * D]).then_inc(q_out[s], 16)

            act.wait_ge(a_reset, 1)
            with act.Fori(0, NPAIR) as i:
                for s in range(2):
                    c = act.snap(i * 2 + s)
                    act.wait_ge(ssc_done, c + C)
                    act.activation(keepx[:, :, 1:W], start_f[:, bass.ds(c * T, T)].unsqueeze(1).to_broadcast([P, D, T]),
                                   ACT.Copy, bias=1.0, scale=-1.0).then_inc(keep_done, 1)
                    act.wait_ge(qs_in[s], i * 16 + 16)
                    act.wait_ge(qsc_done, c + C)
                    act.activation(ebuf[:, :, 1:W], qs[s].rearrange("p t c -> p c t"), ACT.Copy).then_inc(qv_done, 1)
                    act.wait_ge(c2_done, c + 1)
                    act.activation(score[:, :, :], score[:, :, :], ACT.Exp).then_inc(ex_done, 1)
                    act.wait_ge(ssc_done, c + 1 + C)
                    act.wait_ge(ms_out[s], i * 16 + 16)
                    act.activation(msout[s].rearrange("p t c -> p c t"), nscan[:, :, 1:W], ACT.Copy).then_inc(ro_done, 1)
                    act.wait_ge(ro_done, c + 1 + C)
                    act.dma_start(ms_v[:, bass.ds(c * T, T), :], msout[s]).then_inc(ms_out[s], 16)

        @block.tensor
        def _(pe):
            pe.sem_inc(ea_done, C)
            pe.sem_inc(hist, C)

            def transposes(out, rows_, last):
                hold(pe, "pe")
                for k in range(G):
                    ins = pe.transpose(out[:, k, 0:NP], rows_[:, k, :], ident[0:NP, 0:NP])
                ins.then_inc(last, 1)

            pe.wait_ge(pool_pro, 6)
            pe.wait_ge(w_in, 16 * (NW + 5))
            with pe.Fori(0, NG) as q:
                pe.wait_ge(p_h, q + 1)
                transposes(psT, h0, p_hT)
                pe.wait_ge(p_hc, q + 1)
                for k in range(G):
                    ins = pe.matmul(psX[:, k, :], h0T[:, k * P:k * P + NP], encw[:, :], start=True, stop=True)
                ins.then_inc(p_x, 1)
            pe.wait_ge(dve_pro, 4)
            pe.matmul(psA, wbc, ident[:, :], start=True, stop=True).then_inc(passT, 1)
            pe.wait_ge(zero_done, 1)
            pe.matmul(psHist, zero_b[:, 0:HR], zero_b, start=True, stop=False)
            with pe.Fori(0, NPAIR) as i:
                for s in range(2):
                    pe.wait_ge(onehots, i * 2 + s + 1 + C)
                    for k in range(T):
                        ins = pe.matmul(psHist, oh_hi[s][:, k, :], oh_lo[s][:, k, :], start=False, stop=False)
                    ins.then_inc(hist, 1)
            pe.matmul(psHist, zero_b[:, 0:HR], zero_b, start=False, stop=True).then_inc(hist, 1)
            pe.wait_ge(dve_pro, 6)
            pe.matmul(psOff, tri[0:NP, 0:NP], cum[:, NJ - 1:NJ], start=True, stop=True).then_inc(offs, 1)

            def edge_terms(g, u, s, weight):
                pe.wait_ge(attr_in[s], u * 16 + 16)
                pe.wait_ge(z_done, g + 1)
                for k in range(T):
                    ins = pe.matmul(ea[s][:, k, :], attr[s][:, k * P:(k + 1) * P], weight[:, :], start=True, stop=True)
                ins.then_inc(ea_done, 1)

            pe.wait_ge(dve_pro, 8)
            with pe.Fori(0, L) as layer:
                with pe.Fori(0, NPAIR) as i:
                    for s in range(2):
                        edge_terms(pe.snap(layer * NCH + i * 2 + s), pe.snap(layer * NPAIR + i), s, eew)
                pe.wait_ge(tail_done, layer + 1)
                pe.wait_ge(cn_done, layer * NCH + NCH + C)
                pe.transpose(psA, tailr[:, :, :].rearrange("p a c -> p (a c)"), ident[:, :])
                pe.transpose(psB, rows[1][:, T - 1, :], ident[:, :]).then_inc(br_pe, 1)
                pe.wait_ge(br_dve, layer * BRK + 6)
                pe.transpose(psA2, rsc[:, 0:P], ident[:, :])
                pe.transpose(psB2, xsc[:, 0:P], ident[:, :]).then_inc(br_pe, 1)
                with pe.Fori(0, NG) as j:
                    q = pe.snap(layer * NG + j)
                    pe.wait_ge(h0_done, q + 1 + C)
                    transposes(psT, h0, h0T_done)
                    pe.wait_ge(h0c_done, q + 1)
                    for k in range(G):
                        ins = pe.matmul(psH[:, k, :], h0T[:, k * P:k * P + NP], w1[:, bass.ds(layer * (2 * D), 2 * D)], start=True, stop=True)
                    ins.then_inc(hw1_done, 1)
                    pe.wait_ge(hn_done, q + 1)
                    transposes(psN, hn, hnT_done)
                    pe.wait_ge(hr_done, q + 1)
                    for k in range(G):
                        pe.matmul(psX[:, k, :], hrT[:, k * P:k * P + NP], w2[:, bass.ds(layer * D, D)], start=True, stop=False)
                        ins = pe.matmul(psX[:, k, :], ones1[:, 0:NP], b2[:, bass.ds(layer * D, D)], start=False, stop=True)
                    ins.then_inc(hw2_done, 1)
                pe.wait_ge(xadd_done, layer * NG + NG)

            with pe.Fori(0, NGP) as i:
                for s in range(2):
                    q = pe.snap(i * 2 + s)
                    pe.wait_ge(q_in[s], i * 48 + 48)
                    transposes(psT, xold[s], q_hT)
                    pe.wait_ge(q_hc, q + 1)
                    for k in range(G):
                        ins = pe.matmul(psX[:, k, :], h0T[:, k * P:k * P + NP], linw[:, :], start=True, stop=True)
                    ins.then_inc(q_lin, 1)
                    pe.wait_ge(q_h, q + 1)
                    transposes(psT, h0, q_h2T)
                    pe.wait_ge(q_h2c, q + 1)
                    pe.wait_ge(q_kc, q + C)
                    for k in range(G):
                        ins = pe.matmul(psK[:, k, 0:3 * D], h0T[:, k * P:k * P + NP], kvqw[:, :], start=True, stop=True)
                    ins.then_inc(q_kvq, 1)
            pe.wait_ge(q_kc, NG + C)
            with pe.Fori(0, NPAIR) as i:
                for s in range(2):
                    edge_terms(pe.snap(i * 2 + (s + L * NCH)), pe.snap(i + L * NPAIR), s, wew)
            pe.wait_ge(ro_done, NCH + C)
            pe.transpose(psA[0:D, :], msout[1][:, T - 1, :], ident[:, :]).then_inc(b_pe, 1)
            pe.wait_ge(b_dve, 1)
            pe.transpose(psB2[:, 0:D], xsc[0:D, 0:P], ident[0:D, 0:D]).then_inc(b_pe, 1)

        @block.vector
        def _(v):
            for x in (z_done, m_done, s_done, w_done, cs_done, me_done, d_done, n_done, cd_done, cn_done,
                      h0_done, onehots, msg_done, qsc_done, ssc_done, o_done):
                v.sem_inc(x, C)
            for s in range(2):
                v.sem_inc(xnew_out[s], 16)
                v.sem_inc(o_out[s], 16)
                v.sem_inc(p_out[s], 16)
            chain = sem("dve_chain")
            count = [0, 0]

            def link(ins):
                count[0] += 1
                ins.then_inc(chain, 1)
                v.wait_ge(chain, count[0])

            def signal(ins):
                count[1] += 1
                ins.then_inc(dve_pro, 1)
                v.wait_ge(dve_pro, count[1])


            signal(v.memset(dprev, -1))
            v.memset(nrow[:, 0:D], 0.0)
            signal(v.memset(nrow[:, D:2 * D], 1.0))
            signal(v.memset(mebuf[:, :, :], 0.0))
            for s in range(2):
                v.memset(attr[s][D:D + 1, :], 1.0)
            v.memset(h0T[:, :], 1.0)
            v.memset(ones1[:, :], 1.0)
            v.memset(rsc[:, 0:1], -BIG)
            v.memset(xsc[:, 0:1], 0.0)
            link(v.memset(epscol[:, :], LN_EPS))
            v.wait_ge(w_in, 16 * (NW + 5))
            w1v = w1[:, :].rearrange("k (l n) -> k l n", l=L)
            link(v.tensor_reduce(w1m[:, :], w1v, AX.X, ALU.add))
            link(v.tensor_scalar(w1m[:, :], w1m[:, :], 1.0 / (2 * D), None, ALU.mult))
            link(v.tensor_tensor(w1v, w1v, w1m[:, :].unsqueeze(2).to_broadcast([D + 1, L, 2 * D]), ALU.subtract))

            def layer_norm(x, q, steps, std_sem):
                hold(v, "dve")
                v.tensor_reduce(mu[:, :], x, AX.X, ALU.add).then_inc(steps, 1)
                v.wait_ge(steps, q * LNK + 1)
                v.tensor_scalar(mu[:, :], mu[:, :], 1.0 / D, None, ALU.mult).then_inc(steps, 1)
                v.wait_ge(steps, q * LNK + 2)
                v.tensor_tensor(lnx, x, mu[:, :].unsqueeze(2).to_broadcast([NP, G, D]), ALU.subtract).then_inc(steps, 1)
                v.wait_ge(steps, q * LNK + 3)
                v.tensor_tensor(lnsq, lnx, lnx, ALU.mult).then_inc(steps, 1)
                v.wait_ge(steps, q * LNK + 4)
                v.tensor_reduce(ss2[:, :], lnsq, AX.X, ALU.add).then_inc(steps, 1)
                v.wait_ge(std_sem, q + 1)
                v.reciprocal(rstd2[:, :], std2[:, :]).then_inc(steps, 1)
                v.wait_ge(steps, q * LNK + 6)
                v.tensor_tensor(lnx, lnx, rstd2[:, :].unsqueeze(2).to_broadcast([NP, G, D]), ALU.mult).then_inc(steps, 1)
                v.wait_ge(steps, q * LNK + 7)

            v.wait_ge(x_in, 16)
            with v.Fori(0, NGP) as i:
                for s in range(2):
                    q = v.snap(i * 2 + s)
                    layer_norm(x3[:, bass.ds(q * G, G), :], q, p_ln, p_std)
                    v.tensor_scalar(h0, lnx, 0.0, None, ALU.max).then_inc(p_h, 1)
                    v.wait_ge(p_x, q + 1)
                    v.wait_ge(p_out[s], i * 16 + 16)
                    v.tensor_copy(xnew[s], psX).then_inc(p_new, 1)
                    v.wait_ge(p_new, q + 1)
            link(v.memset(x_res[:, :], 0.0))

            v.wait_ge(dst_in, 16)
            v.wait_ge(dp_in, 16)
            v.wait_ge(pool_pro, 6)
            link(v.tensor_copy(dst_f, dst_i))
            v.tensor_copy(dsthead[:, :], dst_i[:, 0:1])
            link(v.tensor_copy(col[0], dprev))
            v.tensor_tensor(start_f[:, 1:EP], dst_f[:, 1:EP], dst_f[:, 0:EP - 1], ALU.not_equal)
            v.memset(start_f[:, EP:EP + 1], 0.0)
            v.tensor_tensor(start_f[:, 0:1], dst_f[:, 0:1], col[0], ALU.not_equal)
            v.tensor_tensor(cont[:, :], dst_f[:, 0:1], col[0], ALU.is_equal)
            link(v.tensor_scalar(ne_f, dst_f, dst_f[:, 0:1], None, ALU.not_equal))
            v.tensor_scalar(headneg[:, :], ne_f, -BIG, None, ALU.mult)
            v.tensor_scalar(contneg[:, :], cont[:, :], -1.0, BIG, ALU.add, ALU.mult)
            v.tensor_copy(col[1], pcol_i)
            link(v.tensor_reduce(col[2], ne_f, AX.X, ALU.add))
            link(v.tensor_tensor(col[3], col[1], col[2], ALU.subtract))
            v.tensor_copy(hidx[:, :], col[3])
            link(v.tensor_scalar(col[4], col[2], 0.0, None, ALU.is_equal))
            link(v.tensor_tensor(col[5], col[4], cont[:, :], ALU.mult))
            signal(v.tensor_copy(wbc, col[5].to_broadcast([P, P])))
            v.wait_ge(passT, 1)
            link(v.tensor_copy(passkeep[:, :], psA))
            link(v.tensor_scalar(passneg[:, :], passkeep[:, :], -1.0, BIG, ALU.add, ALU.mult))

            v.memset(zero_b, 0.0).then_inc(zero_done, 1)
            v.tensor_copy(iota_b, iota_i)
            link(v.tensor_scalar(tmp_i, dst_i, 7, None, ALU.logical_shift_right))
            link(v.tensor_copy(hi_b, tmp_i))
            link(v.tensor_scalar(tmp_i, dst_i, HB - 1, None, ALU.bitwise_and))
            link(v.tensor_copy(lo_b, tmp_i))
            with v.Fori(0, NPAIR) as i:
                for s in range(2):
                    c = v.snap(i * 2 + s)
                    v.wait_ge(hist, c + 1)
                    v.tensor_tensor(oh_hi[s], hi_b[:, bass.ds(c * T, T)].unsqueeze(2).to_broadcast([P, T, HR]),
                                    iota_b[:, 0:HR].unsqueeze(1).to_broadcast([P, T, HR]), ALU.is_equal)
                    v.tensor_tensor(oh_lo[s], lo_b[:, bass.ds(c * T, T)].unsqueeze(2).to_broadcast([P, T, HB]),
                                    iota_b.unsqueeze(1).to_broadcast([P, T, HB]), ALU.is_equal).then_inc(onehots, 1)
            v.wait_ge(hist, NCH + 1 + C)
            signal(v.tensor_copy(cntbuf, psHist))
            v.wait_ge(cnt_in, 16)
            link(v.tensor_tensor_scan(cum, cnt, cnt, 0.0, ALU.add, ALU.max))
            signal(v.tensor_scalar(has, cnt, 0.0, None, ALU.is_gt))
            v.wait_ge(offs, 1)
            link(v.tensor_copy(col[6][0:NP, :], psOff))
            link(v.tensor_scalar(cum, cum, col[6][0:NP, :], None, ALU.add))
            link(v.tensor_tensor(spos, cum, cnt, ALU.subtract))
            for pos, before in ((epos, 1.0), (spos, 0.0)):
                link(v.tensor_scalar(pos, cum if before else spos, -before - E, None, ALU.add))
                link(v.tensor_tensor(pos, pos, has, ALU.mult))
                link(v.tensor_scalar(pos, pos, float(E), None, ALU.add))
            link(v.tensor_copy(epos_i, epos))
            signal(v.tensor_copy(spos_i, spos))
            v.wait_ge(const_out, 32)
            v.wait_ge(tab_out, 32)
            v.wait_ge(qzero, 16 * NCH)
            for s in range(2):
                v.wait_ge(p_out[s], 16 * (NGP + 1))
            v.memset(lbuf[:, :, T + 1:WM], -BIG)
            v.memset(flagx[:, :, 0:1], 0.0)
            v.memset(flagx[:, :, T + 1:WM], -BIG)
            signal(v.memset(fbuf[:, :, 0:1], 0.0))

            def message(c, g, u, s):
                v.wait_ge(gathered[s], u * GATH + GATH)
                v.wait_ge(ea_done, g + 1 + C)
                v.wait_ge(cs_done, g + C)
                v.tensor_tensor(zbuf[:, :, :], ea[s].rearrange("p t c -> p c t"), xg[s].rearrange("p t c -> p c t"),
                                ALU.add).then_inc(z_done, 1)
                v.wait_ge(z_done, g + 1 + C)
                v.tensor_scalar(mbuf[s][:, :, :], zbuf[:, :, :], 0.0, EPS, ALU.max, ALU.add).then_inc(m_done, 1)

            def maximum(c, g, s):
                v.wait_ge(l_done, g + 1 + C)
                v.wait_ge(cs_done, g + C)
                v.tensor_tensor_scan(flat(smax), flat(lbuf), flat(flagx), -BIG, ALU.max, ALU.add).then_inc(s_done, 1)
                v.wait_ge(s_done, g + 1 + C)
                v.wait_ge(f_done, g + C)
                v.tensor_tensor(wbuf[:, :, :], lbuf[:, :, 1:T + 1], smax[:, :, 0:T], ALU.subtract).then_inc(w_done, 1)
                v.tensor_tensor(zbuf[:, :, :], lbuf[:, :, 1:T + 1],
                                headneg[:, bass.ds(c * T, T)].unsqueeze(1).to_broadcast([P, D, T]), ALU.add).then_inc(hadd_done, 1)
                v.wait_ge(hadd_done, g + 1)
                v.tensor_reduce(headr2[:, :], zbuf[:, :, :], AX.X, ALU.max).then_inc(hred_done, 1)
                v.wait_ge(hred_done, g + 1)
                v.tensor_tensor(headr[:, :], headr[:, :], headr2[:, :], ALU.max).then_inc(hmax_done, 1)
                v.wait_ge(hmax_done, g + 1)
                v.tensor_copy(lbuf[:, :, 0], smax[:, :, T]).then_inc(cs_done, 1)

            def sums(g, s):
                v.wait_ge(f_done, g + 1 + C)
                v.wait_ge(cn_done, g + C)
                v.tensor_tensor(mebuf[:, :, 1:W], mbuf[s][:, :, :], ebuf[:, :, 1:W], ALU.mult).then_inc(me_done, 1)
                v.wait_ge(rows_done, g + C)
                v.tensor_tensor_scan(flat(dscan), flat(fbuf), flat(ebuf), 0.0, ALU.mult, ALU.add).then_inc(d_done, 1)
                v.wait_ge(me_done, g + 1 + C)
                v.tensor_tensor_scan(flat(nscan), flat(fbuf), flat(mebuf), 0.0, ALU.mult, ALU.add).then_inc(n_done, 1)
                v.wait_ge(d_done, g + 1 + C)
                v.tensor_copy(ebuf[:, :, 0], dscan[:, :, T]).then_inc(cd_done, 1)
                v.wait_ge(n_done, g + 1 + C)
                v.tensor_copy(mebuf[:, :, 0], nscan[:, :, T]).then_inc(cn_done, 1)

            with v.Fori(0, L) as layer:
                g0 = v.snap(layer * NCH)
                u0 = v.snap(layer * NPAIR)
                v.memset(lbuf[:, :, 0:1], -BIG)
                v.memset(ebuf[:, :, 0:1], 0.0)
                v.memset(mebuf[:, :, 0:1], 0.0)
                v.memset(headr[:, :], -BIG).then_inc(reset_done, 1)
                v.wait_ge(reset_done, layer + 1)
                message(0, g0, u0, 0)
                maximum(0, g0, 0)
                with v.Fori(0, NPAIR - 1) as i:
                    for s in range(2):
                        c = v.snap(i * 2 + s)
                        g = v.snap(g0 + c)
                        message(c + 1, g + 1, u0 + i + s, 1 - s)
                        sums(g, s)
                        maximum(c + 1, g + 1, 1 - s)
                message(NCH - 1, g0 + (NCH - 1), u0 + (NPAIR - 1), 1)
                sums(g0 + (NCH - 2), 0)
                maximum(NCH - 1, g0 + (NCH - 1), 1)
                sums(g0 + (NCH - 1), 1)

                step = [0]

                def bridge(ins):
                    step[0] += 1
                    ins.then_inc(br_dve, 1)
                    v.wait_ge(br_dve, layer * BRK + step[0])

                v.wait_ge(br_pe, layer * 2 + 1)
                bridge(v.tensor_tensor_scan(rsc[:, 1:P + 1], passneg[:, :], psA, -BIG, ALU.add, ALU.max))
                bridge(v.tensor_tensor(g12[:, 0, :], rsc[:, 0:P], passneg[:, :], ALU.add))
                bridge(v.tensor_tensor(g12[:, 0, :], g12[:, 0, :], rsc[:, 1:P + 1], ALU.subtract))
                bridge(v.tensor_tensor(g12[:, 1, :], psA, rsc[:, 1:P + 1], ALU.subtract))
                v.wait_ge(br_act, layer * 2 + 1)
                bridge(v.tensor_tensor(g12[:, 1, :], g12[:, 1, :], psB, ALU.mult))
                bridge(v.tensor_tensor_scan(xsc[:, 1:P + 1], g12[:, 0, :], g12[:, 1, :], 0.0, ALU.mult, ALU.add))
                v.wait_ge(br_pe, layer * 2 + 2)
                bridge(v.tensor_scalar(rcar[:, :], psA2[:, 0:D], contneg[:, :], None, ALU.add))
                bridge(v.tensor_tensor(headr2[:, :], rcar[:, :], headr[:, :], ALU.max))
                bridge(v.tensor_tensor(ab[:, 0, :], rcar[:, :], headr2[:, :], ALU.subtract))
                bridge(v.tensor_tensor(ab[:, 1, :], headr[:, :], headr2[:, :], ALU.subtract))
                v.wait_ge(br_act, layer * 2 + 2)
                nd2 = [t.rearrange("p (a c) -> p a c", a=2) for t in (fixed[:, :], psB2, headnd[:, :])]
                bridge(v.tensor_tensor(nd2[0], nd2[1], ab[:, 0, :].unsqueeze(1).to_broadcast([P, 2, D]), ALU.mult))
                v.wait_ge(head_in, layer * 16 + 16)
                bridge(v.tensor_tensor(nd2[2], nd2[2], ab[:, 1, :].unsqueeze(1).to_broadcast([P, 2, D]), ALU.mult))
                bridge(v.tensor_tensor(fixed[:, :], fixed[:, :], headnd[:, :], ALU.add))
                assert step[0] == BRK

                hold(v, "dve")
                with v.Fori(0, NGP) as j:
                    for s in range(2):
                        q = v.snap(layer * NG + j * 2 + s)
                        u = v.snap(layer * NGP + j)
                        grp = bass.ds((j * 2 + s) * G, G)
                        v.wait_ge(nd_in[s], u * NGATH + NGATH)
                        v.reciprocal(recd, nd[s][:, :, D:2 * D]).then_inc(rec_done, 1)
                        v.wait_ge(rec_done, q + 1)
                        v.tensor_tensor(recd, recd, nd[s][:, :, 0:D], ALU.mult).then_inc(agg_done, 1)
                        v.wait_ge(agg_done, q + 1)
                        v.wait_ge(xold_in[s], u * 16 + 16)
                        v.tensor_tensor(h0, recd, xold[s], ALU.add).then_inc(h0_done, 1)
                        v.wait_ge(sq_done, q + 1)
                        v.tensor_reduce(ss[:, :], sqb, AX.X, ALU.add).then_inc(ss_done, 1)
                        v.wait_ge(std_done, q + 1)
                        v.reciprocal(rstd[:, :], std[:, :]).then_inc(rstd_done, 1)
                        v.wait_ge(rstd_done, q + 1)
                        v.tensor_tensor(hn, psH, rstd[:, :].unsqueeze(2).to_broadcast([NP, G, 2 * D]), ALU.mult).then_inc(hn_done, 1)
                        v.wait_ge(hw2_done, q + 1)
                        v.tensor_tensor(x3[:, grp, :], x3[:, grp, :], psX, ALU.add).then_inc(xadd_done, 1)
                        v.wait_ge(xadd_done, q + 1)
                        layer_norm(x3[:, grp, :], q, ln_dve, ln_std)
                        v.tensor_tensor(lnx, lnx, ng[:, bass.ds(layer * D, D)].unsqueeze(1).to_broadcast([NP, G, D]), ALU.mult).then_inc(aff_done, 1)
                        v.wait_ge(aff_done, q * 2 + 1)
                        v.tensor_tensor(lnx, lnx, nb[:, bass.ds(layer * D, D)].unsqueeze(1).to_broadcast([NP, G, D]), ALU.add).then_inc(aff_done, 1)
                        v.wait_ge(aff_done, q * 2 + 2)
                        v.wait_ge(xnew_out[s], u * 16 + 16)
                        v.tensor_scalar(xnew[s], lnx, 0.0, None, ALU.max).then_inc(xnew_done, 1)
                        v.wait_ge(xnew_done, q + 1)

            with v.Fori(0, NGP) as i:
                for s in range(2):
                    q = v.snap(i * 2 + s)
                    grp = bass.ds(q * G, G)
                    v.wait_ge(q_lin, q + 1)
                    v.wait_ge(q_in[s], i * 48 + 48)
                    v.tensor_tensor(x3[:, grp, :], psX, xnew[s], ALU.add).then_inc(q_x1, 1)
                    v.wait_ge(q_x1, q + 1)
                    layer_norm(x3[:, grp, :], q, q_ln, q_std)
                    v.tensor_scalar(h0, lnx, 0.0, None, ALU.max).then_inc(q_h, 1)
                    v.wait_ge(q_h, q + 1)

            v.wait_ge(qhead_in, 16)
            v.wait_ge(q_kc, NG + C)
            v.memset(keepx[:, :, 0:1], 0.0)
            v.tensor_copy(ebuf[:, :, 0], qhead[:, :])
            v.memset(mebuf[:, :, 0:1], 0.0).then_inc(a_reset, 1)
            v.wait_ge(a_reset, 1)
            with v.Fori(0, NPAIR) as i:
                for s in range(2):
                    c = v.snap(i * 2 + s)
                    g = v.snap(c + L * NCH)
                    kg, vg = kvg[s][:, :, 0:D], kvg[s][:, :, D:2 * D]
                    v.wait_ge(gathered[s], i * GATH + (L * NPAIR + 1) * GATH)
                    v.wait_ge(ea_done, g + 1 + C)
                    v.tensor_tensor(zt, ea[s], kg, ALU.mult).then_inc(z_done, 1)
                    v.wait_ge(keep_done, c + 1)
                    v.wait_ge(qv_done, c + 1 + C)
                    v.tensor_tensor_scan(flat(dscan), flat(flagx)[:, 0:D * W], flat(ebuf), 0.0, ALU.mult, ALU.add).then_inc(qsc_done, 1)
                    v.wait_ge(qsc_done, c + 1 + C)
                    v.tensor_copy(ebuf[:, :, 0], dscan[:, :, T]).then_inc(qc_done, 1)
                    v.tensor_tensor(zt, zt, dscan[:, :, 1:W].rearrange("p c t -> p t c"), ALU.mult).then_inc(kq_done, 1)
                    v.wait_ge(kq_done, c + 1)
                    v.tensor_reduce(score[:, :, :], zt.rearrange("p t (h d) -> p t h d", h=H), AX.X, ALU.add).then_inc(sr_done, 1)
                    v.wait_ge(sr_done, c + 1)
                    v.tensor_scalar(score[:, :, :], score[:, :, :], INV_SQRT_HD, 5.0, ALU.mult, ALU.min).then_inc(c1_done, 1)
                    v.wait_ge(c1_done, c + 1)
                    v.tensor_scalar(score[:, :, :], score[:, :, :], -5.0, None, ALU.max).then_inc(c2_done, 1)
                    v.wait_ge(ex_done, c + 1)
                    v.tensor_tensor(mebuf[:, :, 1:W].rearrange("p (h d) t -> p t h d", h=H),
                                    vg.rearrange("p t (h d) -> p t h d", h=H),
                                    score[:, :, :].unsqueeze(3).to_broadcast([P, T, H, D // H]), ALU.mult).then_inc(msg_done, 1)
                    v.wait_ge(msg_done, c + 1 + C)
                    v.wait_ge(ro_done, c + C)
                    v.tensor_tensor_scan(flat(nscan), flat(flagx)[:, 0:D * W], flat(mebuf), 0.0, ALU.mult, ALU.add).then_inc(ssc_done, 1)
                    v.wait_ge(ssc_done, c + 1 + C)
                    v.tensor_copy(mebuf[:, :, 0], nscan[:, :, T]).then_inc(sc_done, 1)
                    v.wait_ge(sc_done, c + 1)

            v.wait_ge(b_pe, 1)
            v.tensor_tensor_scan(xsc[0:D, 1:P + 1], passkeep[0:D, :], psA[0:D, :], 0.0, ALU.mult, ALU.add).then_inc(b_dve, 1)
            v.wait_ge(b_pe, 2)
            v.tensor_scalar(fixed[:, 0:D], psB2[:, 0:D], cont[:, :], None, ALU.mult).then_inc(b_dve, 1)
            v.wait_ge(b_dve, 2)
            v.wait_ge(mhead_in, 16)
            v.tensor_tensor(fixed[:, 0:D], fixed[:, 0:D], headnd[:, 0:D], ALU.add).then_inc(b_dve, 1)

            with v.Fori(0, NGP) as j:
                for s in range(2):
                    v.wait_ge(o_in[s], j * NGATH + NGATH)
                    v.wait_ge(o_out[s], j * 16 + 16)
                    v.tensor_tensor(xnew[s], x3[:, bass.ds((j * 2 + s) * G, G), :], nd[s][:, :, 0:D], ALU.add).then_inc(o_done, 1)


def kernel(x, src, dst, edge_attr_64, **w):
    import numpy as np
    import concourse.bacc as bacc
    from concourse.bass_utils import run_bass_kernel_spmd

    w = {k: np.asarray(v) for k, v in w.items()}
    ins = {"x": x, "src": src, "dst": dst,
           "attrT": np.asarray(edge_attr_64).reshape(P, EP, D).transpose(2, 1, 0).reshape(D, E),
           "convLnG_T": w["L0_gnn_convLnG"].T, "convLnB_T": w["L0_gnn_convLnB"].T}
    for n in ("encW", "encb", "eencW", "eencb", "convW1", "convb1", "convW2", "convb2", "t", "normG", "normB", "linW", "linb"):
        ins[n] = w["L0_gnn_" + n]
    for n in ("WQ", "bQ", "WK", "bK", "WE", "bE", "WV", "bV"):
        ins[n] = w["L1_gnn_" + n]
    nc = bacc.Bacc("TRN2", target_bir_lowering=False, num_devices=1)
    arrays, aps = {}, {}
    for n, v in ins.items():
        v = np.ascontiguousarray(v)
        arrays["in_" + n] = v
        aps[n] = nc.dram_tensor("in_" + n, v.shape, mybir.dt.from_np(v.dtype), kind="ExternalInput").ap()
    out = nc.dram_tensor("out", (N, D), F32, kind="ExternalOutput").ap()
    gnn_kernel(nc, aps, out)
    r = run_bass_kernel_spmd(nc, [arrays], core_ids=[0])
    return r.results[0]["out"]
```

```python
from contextlib import ExitStack

import concourse.bass as bass
from concourse import mybir

N, E, D = 10000, 160000, 64
L, H = 4, 8
P = 128
EP = E // P
T = 25
NCH = EP // T
NPAIR = NCH // 2
NP = 125
NJ = N // NP
G = 8
NG = NJ // G
NGP = NG // 2
W = T + 1
WM = T + 2
HB = 128
HR = -(-N // HB)
BIG = 1.0e30
EPS, LN_EPS = 1e-7, 1e-5
C = 2
GATH = 16 * T
NGATH = 16 * G
INV_SQRT_HD = (D // H) ** -0.5

F32, I32, BF16 = mybir.dt.float32, mybir.dt.int32, mybir.dt.bfloat16
ALU, ACT, AX = mybir.AluOpType, mybir.ActivationFunctionType, mybir.AxisListType


def gnn_kernel(nc, a, out):
    ctx = ExitStack()
    with ctx:
        def sb(name, shape, dt=F32):
            return ctx.enter_context(nc.sbuf_tensor(name, shape, dt))

        def sem(name):
            return ctx.enter_context(nc.semaphore(name))

        def dram(name, shape, dt=F32):
            return nc.dram_tensor(name, shape, dt, kind="Internal").ap()

        def flat(t):
            return t[:, :, :].rearrange("p a b -> p (a b)")

        def groups(t, c):
            return t.rearrange("p (g c) -> p g c", c=c)

        xtab = dram("xtab", (N, D))
        kvtab = dram("kvtab", (N, 2 * D))
        qtab = dram("qtab", (N, D))
        qstart = dram("qstart", (E, D))
        ndrows = dram("ndrows", (E + 1, 2 * D))
        msrows = dram("msrows", (E + 1, D))
        cnttab = dram("cnttab", (HR, HB))

        ident = sb("ident", [P, P])
        tri = sb("tri", [P, P])
        start_f = sb("start_f", [P, EP + 1])
        headneg = sb("headneg", [P, EP])
        x_all = sb("x_all", [P, NJ * D])
        x_res = x_all[0:NP, :]
        endix = sb("endix", [NP, NJ], I32)
        startix = sb("startix", [NP, NJ], I32)
        counts = sb("counts", [HR, HB])
        zeros = sb("zeros", [P, T * D // 4])
        eew = sb("eew", [D + 1, D])
        wew = sb("wew", [D + 1, D])
        encw = sb("encw", [D + 1, D])
        linw = sb("linw", [D + 1, D])
        kvqw = sb("kvqw", [D + 1, 3 * D])
        w1 = sb("w1", [D + 1, L * 2 * D])
        w1m = sb("w1m", [D + 1, L])
        w2 = sb("w2", [2 * D, L * D])
        b2 = sb("b2", [NP, L * D])
        w2m = sb("w2m", [2 * D, L])
        b2m = sb("b2m", [NP, L])
        lng = sb("lng", [2 * D, L])
        lnb = sb("lnb", [2 * D, L])
        tcol = sb("tcol", [P, L])
        ng = sb("ng", [NP, L * D])
        nb = sb("nb", [NP, L * D])
        epscol = sb("epscol", [P, 1])

        attr = [sb(f"attr{s}", [D + 1, T * P]) for s in range(2)]
        idx = [sb(f"idx{s}", [P, T], I32) for s in range(2)]
        kvg = [sb(f"kvg{s}", [P, T, 2 * D]) for s in range(2)]
        rows = [sb(f"rows{s}", [P, T, 2 * D]) for s in range(2)]
        zbuf = sb("zbuf", [P, D, T])
        mbuf = [sb(f"mbuf{s}", [P, D, T]) for s in range(2)]
        lbuf = sb("lbuf", [P, D, WM])
        flagx = sb("flagx", [P, D, WM])
        smax = sb("smax", [P, D, WM])
        wbuf = sb("wbuf", [P, D, T])
        ebuf = sb("ebuf", [P, D, W])
        fbuf = sb("fbuf", [P, D, W])
        mebuf = sb("mebuf", [P, D, W])
        dscan = sb("dscan", [P, D, W])
        nscan = sb("nscan", [P, D, W])
        headr = sb("headr", [P, D])
        headr2 = sb("headr2", [P, D])
        xg = [flat(k)[:, 0:T * D].rearrange("p (t c) -> p t c", c=D) for k in kvg]
        zt = flat(zbuf).rearrange("p (t c) -> p t c", c=D)
        keepx = flat(flagx)[:, 0:D * W].rearrange("p (c t) -> p c t", t=W)
        msout = [flat(r)[:, 0:T * D].rearrange("p (t c) -> p t c", c=D) for r in rows]
        qs = [flat(r)[:, T * D:2 * T * D].rearrange("p (t c) -> p t c", c=D) for r in rows]
        score = sb("score", [P, T, H])

        hidx = sb("hidx", [P, 1], I32)
        cont = sb("cont", [P, 1])
        contneg = sb("contneg", [P, 1])
        passneg = sb("passneg", [P, P])
        passkeep = sb("passkeep", [P, P])
        tailr = sb("tailr", [P, 2, D])
        rsc = sb("rsc", [P, P + 1])
        xsc = sb("xsc", [P, P + 1])
        g12 = sb("g12", [P, 2, P])
        headnd = sb("headnd", [P, 2 * D])
        rcar = sb("rcar", [P, D])
        ab = sb("ab", [P, 2, D])
        fixed = sb("fixed", [P, 2 * D])
        qhead = sb("qhead", [P, D])
        dsthead = sb("dsthead", [P, 1], I32)

        nd = [kvg[s][0:NP, 0:G, :] for s in range(2)]
        xold = [groups(flat(rows[s])[0:NP, 0:G * D], D) for s in range(2)]
        xnew = [groups(flat(rows[s])[0:NP, G * D:2 * G * D], D) for s in range(2)]
        kvq = [groups(flat(rows[s])[0:NP, 2 * G * D:5 * G * D], 3 * D) for s in range(2)]
        recd = groups(flat(zbuf)[0:NP, 0:G * D], D)
        h0 = groups(flat(zbuf)[0:NP, G * D:2 * G * D], D)
        h0T = sb("h0T", [D + 1, G * P])
        sqb = groups(flat(mbuf[0])[0:NP, 0:2 * G * D], 2 * D)
        hn = groups(flat(mbuf[1])[0:NP, 0:2 * G * D], 2 * D)
        hrT = flat(wbuf)[:, 0:G * P]
        lnx = groups(flat(dscan)[0:NP, 0:G * D], D)
        lnsq = groups(flat(dscan)[0:NP, G * D:2 * G * D], D)
        ss, std, rstd = (sb(n, [NP, G]) for n in ("ss", "std", "rstd"))
        mu, ss2, std2, rstd2 = (sb(n, [NP, G]) for n in ("mu", "ss2", "std2", "rstd2"))

        PS = ctx.enter_context(nc.psum_tensor("PS", [P, 4096], F32))
        ea = [PS[:, s * 2048:s * 2048 + T * D].rearrange("p (t c) -> p t c", c=D) for s in range(2)]
        psT = PS[0:D, 0:G * P].rearrange("p (g c) -> p g c", c=P)
        psH = PS[0:NP, 1024:2048].rearrange("p (g c) -> p g c", c=2 * D)
        psN = PS[:, 2048:3072].rearrange("p (g c) -> p g c", c=P)
        psX = PS[0:NP, 3072:3072 + G * D].rearrange("p (g c) -> p g c", c=D)
        psK = PS[0:NP, 1024:1024 + G * 256].rearrange("p (g c) -> p g c", c=256)
        psA, psB = PS[:, 3712:3840], PS[:, 3840:3968]
        psA2, psB2 = PS[:, 1664:1792], PS[:, 1792:1920]
        psHist, psOff = PS[0:HR, 1664:1792], PS[0:NP, 1792:1793]

        dst_i = flat(wbuf)[:, 0:EP].bitcast(I32)
        dst_f = flat(mbuf[0])[:, 0:EP]
        ne_f = flat(mbuf[1])[:, 0:EP]
        tmp_i = flat(nscan)[:, 0:EP].bitcast(I32)
        iota_i = flat(smax)[:, 0:HB].bitcast(I32)
        pcol_i = flat(smax)[:, HB:HB + 1].bitcast(I32)
        dprev = flat(smax)[:, HB + 1:HB + 2].bitcast(I32)
        col = [flat(smax)[:, HB + 2 + n:HB + 3 + n] for n in range(6)]
        wbc = flat(smax)[:, 2 * HB:3 * HB]
        nrow = flat(smax)[0:1, 3 * HB:3 * HB + 2 * D]
        used = [0]

        def part(floats):
            used[0] += floats
            return x_all[:, used[0] - floats:used[0]]

        oh_lo = part(T * HB // 2).bitcast(BF16).rearrange("p (t c) -> p t c", c=HB)
        oh_hi = part(-(-T * HR // 2)).bitcast(BF16)[:, 0:T * HR].rearrange("p (t c) -> p t c", c=HR)
        hi_b, lo_b = part(EP // 2).bitcast(BF16), part(EP // 2).bitcast(BF16)
        iota_b = part(HB // 2).bitcast(BF16)
        cnt, cum, has, epos, spos = (part(NJ)[0:NP, :] for n in range(5))
        off = part(1)[0:NP, :]

        attrT = a["attrT"].rearrange("k (c m) -> k c m", c=NCH)
        src_v = a["src"].rearrange("(p e) -> p e", p=P)
        dst_v = a["dst"].rearrange("(p e) -> p e", p=P)
        x_v = a["x"].rearrange("(p j) c -> p j c", p=NP)
        out_v = out.rearrange("(p j) c -> p j c", p=NP)
        xtab_v = xtab.rearrange("(p j) c -> p j c", p=NP)
        kvtab_v = kvtab.rearrange("(p j) c -> p j c", p=NP)
        qtab_v = qtab.rearrange("(p j) c -> p j c", p=NP)
        nd_v = ndrows[0:E, :].rearrange("(p e) c -> p e c", p=P)
        ms_v = msrows[0:E, :].rearrange("(p e) c -> p e c", p=P)
        qst_v = qstart.rearrange("(p e) c -> p (e c)", p=P)
        qst_t = qstart.rearrange("(p e) c -> p e c", p=P)
        cnt_v = cnttab.rearrange("a b -> (a b)")[0:N].rearrange("(p j) -> p j", p=NP)
        x3 = x_res.rearrange("p (j c) -> p j c", c=D)

        w_in, x_in, dst_in = sem("w_in"), sem("x_in"), sem("dst_in")
        pool_pro, dve_pro = sem("pool_pro"), sem("dve_pro")
        qzero, const_out, cnt_out, cnt_in = (sem(n) for n in "qzero const_out cnt_out cnt_in".split())
        dp_in, onehots, hist, counted, tables, passT, offs = (
            sem(n) for n in "dp_in onehots hist counted tables passT offs".split())
        attr_in = [sem(f"attr_in{s}") for s in range(2)]
        idx_in = [sem(f"idx_in{s}") for s in range(2)]
        gathered = [sem(f"gathered{s}") for s in range(2)]
        stored = [sem(f"stored{s}") for s in range(2)]
        ea_done, z_done, m_done, l_done, flag_done = (sem(n) for n in "ea_done z_done m_done l_done flag_done".split())
        s_done, w_done, hadd_done, hred_done, hmax_done, cs_done = (
            sem(n) for n in "s_done w_done hadd_done hred_done hmax_done cs_done".split())
        er_done, fr_done, e_done, f_done = (sem(n) for n in "er_done fr_done e_done f_done".split())
        me_done, d_done, n_done, cd_done, cn_done, rows_done = (
            sem(n) for n in "me_done d_done n_done cd_done cn_done rows_done".split())
        reset_done, bias_done = sem("reset_done"), sem("bias_done")
        tail_done, br_pe, br_dve, br_act = (sem(n) for n in "tail_done br_pe br_dve br_act".split())
        head_in, head_out = sem("head_in"), sem("head_out")
        nd_in = [sem(f"nd_in{s}") for s in range(2)]
        xold_in = [sem(f"xold_in{s}") for s in range(2)]
        xnew_out = [sem(f"xnew_out{s}") for s in range(2)]
        rec_done, agg_done, h0_done, h0T_done, h0c_done, hw1_done, sq_done, ss_done, std_done, rstd_done = (
            sem(n) for n in "rec_done agg_done h0_done h0T_done h0c_done hw1_done sq_done ss_done std_done rstd_done".split())
        hn_done, hnT_done, hr_done, hw2_done, xadd_done = (
            sem(n) for n in "hn_done hnT_done hr_done hw2_done xadd_done".split())
        sq2_done, ss2_done, std2_done, rstd2_done, aff_done, xnew_done = (
            sem(n) for n in "sq2_done ss2_done std2_done rstd2_done aff_done xnew_done".split())
        p_ln, p_std, p_h, p_hT, p_hc, p_x, p_new = (
            sem(n) for n in "p_ln p_std p_h p_hT p_hc p_x p_new".split())
        p_out = [sem(f"p_out{s}") for s in range(2)]
        q_in = [sem(f"q_in{s}") for s in range(2)]
        q_free = sem("q_free")
        q_out = [sem(f"q_out{s}") for s in range(2)]
        q_sc = [sem(f"q_sc{s}") for s in range(2)]
        q_hT, q_hc, q_lin, q_x1, q_ln, q_std, q_h, q_h2T, q_h2c, q_kvq, q_kc = (
            sem(n) for n in "q_hT q_hc q_lin q_x1 q_ln q_std q_h q_h2T q_h2c q_kvq q_kc".split())
        qs_in = [sem(f"qs_in{s}") for s in range(2)]
        ms_out = [sem(f"ms_out{s}") for s in range(2)]
        keep_done, qv_done, qsc_done, qc_done, kq_done, sr_done, c1_done, c2_done, ex_done, msg_done, ssc_done, sc_done, ro_done = (
            sem(n) for n in ("keep_done qv_done qsc_done qc_done kq_done sr_done c1_done c2_done ex_done msg_done "
                             "ssc_done sc_done ro_done").split())
        qhead_in, a_reset = sem("qhead_in"), sem("a_reset")
        b_pe, b_dve, mhead_in, mhead_out = (sem(n) for n in "b_pe b_dve mhead_in mhead_out".split())
        o_in = [sem(f"o_in{s}") for s in range(2)]
        o_out = [sem(f"o_out{s}") for s in range(2)]
        o_done = sem("o_done")

        LNK = 7
        BRK = 13
        NW = 20
        block = ctx.enter_context(nc.Block())

        held = {e: sem(f"held_{e}") for e in ("sp", "pool", "act", "pe", "dve")}

        def hold(eng, name):
            eng.sem_inc(held[name], 1)

        @block.sync
        def _(sp):
            sp.dma_start(x_res, x_v.rearrange("p j c -> p (j c)")).then_inc(x_in, 16)
            loads = [
                (eew[0:D, :], a["eencW"]), (eew[D:D + 1, :], a["eencb"].unsqueeze(0)),
                (wew[0:D, :], a["WE"]), (wew[D:D + 1, :], a["bE"].unsqueeze(0)),
                (encw[0:D, :], a["encW"]), (encw[D:D + 1, :], a["encb"].unsqueeze(0)),
                (linw[0:D, :], a["linW"]), (linw[D:D + 1, :], a["linb"].unsqueeze(0)),
                (kvqw[0:D, 0:D], a["WK"]), (kvqw[D:D + 1, 0:D], a["bK"].unsqueeze(0)),
                (kvqw[0:D, D:2 * D], a["WV"]), (kvqw[D:D + 1, D:2 * D], a["bV"].unsqueeze(0)),
                (kvqw[0:D, 2 * D:3 * D], a["WQ"]), (kvqw[D:D + 1, 2 * D:3 * D], a["bQ"].unsqueeze(0)),
                (w1[0:D, :].rearrange("k (l n) -> k l n", l=L), a["convW1"].rearrange("l k n -> k l n")),
                (w1[D:D + 1, :], a["convb1"].rearrange("l n -> (l n)").unsqueeze(0)),
                (w2[:, :].rearrange("k (l n) -> k l n", l=L), a["convW2"].rearrange("l k n -> k l n")),
                (b2[:, :], a["convb2"].rearrange("l n -> (l n)").partition_broadcast(NP)),
                (lng[:, :], a["convLnG_T"]), (lnb[:, :], a["convLnB_T"]),
            ]
            assert len(loads) == NW
            for dst, src in loads:
                sp.dma_start(dst, src).then_inc(w_in, 16)
            sp.dma_start(tcol[:, :], a["t"].partition_broadcast(P)).then_inc(w_in, 16)
            for dst, src in ((ng, a["normG"]), (nb, a["normB"])):
                sp.dma_start(dst[:, 0:(L - 1) * D], src[1:L, :].rearrange("l c -> (l c)").partition_broadcast(NP)).then_inc(w_in, 16)
                sp.dma_start(dst[:, (L - 1) * D:], src[0, :].partition_broadcast(NP)).then_inc(w_in, 16)
            sp.dma_start(dst_i, dst_v).then_inc(dst_in, 16)
            sp.wait_ge(dve_pro, 1)
            sp.dma_start(dprev[1:P, :], dst_v[0:P - 1, EP - 1:EP], allow_slow_non_contiguous=True).then_inc(dp_in, 16)
            sp.wait_ge(dve_pro, 2)
            sp.dma_start(ndrows[E:E + 1, :], nrow).then_inc(const_out, 16)
            sp.dma_start(msrows[E:E + 1, :], nrow[:, 0:D]).then_inc(const_out, 16)
            with sp.Fori(0, NGP) as i:
                for s in range(2):
                    q = sp.snap(i * 2 + s)
                    sp.wait_ge(p_new, q + 1 + C)
                    sp.dma_start(xtab_v[:, bass.ds(q * G, G), :], xnew[s]).then_inc(p_out[s], 16)
            sp.wait_ge(dve_pro, 3)

            def load_chunk(c, g, u, s):
                sp.wait_ge(ea_done, g + 1)
                sp.dma_start(attr[s][0:D, :], attrT[:, c, :]).then_inc(attr_in[s], 16)
                sp.wait_ge(z_done, g + 1)
                sp.dma_start(idx[s][:, :], src_v[:, bass.ds(c * T, T)]).then_inc(idx_in[s], 16)

            def load_group(layer, j, s):
                sp.wait_ge(h0_done, layer * NG + (j * 2 + s + 1))
                sp.dma_start(xold[s], xtab_v[:, bass.ds((j * 2 + s) * G, G), :]).then_inc(xold_in[s], 16)

            def store_group(layer, j, s):
                sp.wait_ge(xnew_done, layer * NG + j * 2 + s + 1)
                sp.dma_start(xtab_v[:, bass.ds((j * 2 + s) * G, G), :], xnew[s]).then_inc(xnew_out[s], 16)

            with sp.Fori(0, L) as layer:
                with sp.Fori(0, NPAIR) as i:
                    for s in range(2):
                        c = sp.snap(i * 2 + s)
                        load_chunk(c, sp.snap(layer * NCH + c), sp.snap(layer * NPAIR + i), s)
                        with sp.If(layer < 1):
                            sp.dma_start(qst_v[:, bass.ds(c * (T * D), T * D)].rearrange("p (n f) -> p n f", n=4),
                                         zeros[:, :].unsqueeze(1).to_broadcast([P, 4, T * D // 4])).then_inc(qzero, 16)
                with sp.If(layer < 1):
                    sp.wait_ge(counted, NCH + C)
                    sp.dma_start(cnttab, counts[:, :]).then_inc(cnt_out, 16)
                    sp.wait_ge(cnt_out, 16)
                    sp.dma_start(cnt, cnt_v).then_inc(cnt_in, 16)
                for s in range(2):
                    sp.wait_ge(stored[s], layer * (16 * NPAIR) + 16 * (NPAIR + 1))
                for j in range(4):
                    load_group(layer, j // 2, j % 2)
                with sp.Fori(2, NGP) as j:
                    for s in range(2):
                        load_group(layer, j, s)
                        store_group(layer, j - 2, s)
                for j in range(NG - 4, NG):
                    store_group(layer, j // 2, j % 2)

            def load_x(q, s):
                sp.wait_ge(q_x1, q + 1)
                hold(sp, "sp")
                sp.dma_start(xold[s], xtab_v[:, bass.ds(q * G, G), :]).then_inc(q_in[s], 16)
                sp.dma_start(xnew[s], x_v[:, bass.ds(q * G, G), :]).then_inc(q_in[s], 16)

            for s in range(2):
                sp.wait_ge(xnew_out[s], 16 * (L * NGP + 1))
            for q in range(2):
                load_x(q, q)
            with sp.Fori(0, NGP - 1) as i:
                for s in range(2):
                    q = sp.snap(i * 2 + s)
                    load_x(q + 2, s)

            for s in range(2):
                sp.wait_ge(q_sc[s], NGP * NGATH)
                sp.wait_ge(q_out[s], NGP * 32 + 32)
            with sp.Fori(0, NPAIR) as i:
                for s in range(2):
                    c = sp.snap(i * 2 + s)
                    load_chunk(c, sp.snap(c + L * NCH), sp.snap(i + L * NPAIR), s)
                    sp.wait_ge(qv_done, c + 1)
                    sp.dma_start(qs[s], qst_t[:, bass.ds(c * T, T), :]).then_inc(qs_in[s], 16)

            for s in range(2):
                sp.wait_ge(ms_out[s], 16 * (NPAIR + 1))

            with sp.Fori(0, NGP) as j:
                for s in range(2):
                    sp.wait_ge(o_done, j * 2 + s + 1 + C)
                    sp.dma_start(out_v[:, bass.ds((j * 2 + s) * G, G), :], xnew[s]).then_inc(o_out[s], 16)
            for s in range(2):
                sp.wait_ge(o_out[s], 16 * (NGP + 1))

        @block.gpsimd
        def _(pool):
            pool.sem_inc(q_free, C)
            pool.memset(ident[:, :], 0.0).then_inc(pool_pro, 1)
            pool.memset(tri[:, :], 1.0).then_inc(pool_pro, 1)
            pool.iota(iota_i, pattern=[[1, HB]], base=0, channel_multiplier=0).then_inc(pool_pro, 1)
            pool.iota(pcol_i, pattern=[[0, 1]], base=EP - 1, channel_multiplier=EP).then_inc(pool_pro, 1)
            pool.wait_ge(pool_pro, 4)
            pool.affine_select(out=ident[:, :], in_=ident[:, :], compare_op=ALU.not_equal, fill=1.0, base=0,
                               pattern=[[-1, P]], channel_multiplier=1).then_inc(pool_pro, 1)
            pool.affine_select(out=tri[:, :], in_=tri[:, :], compare_op=ALU.is_gt, fill=0.0, base=0,
                               pattern=[[1, P]], channel_multiplier=-1).then_inc(pool_pro, 1)

            for s in range(2):
                pool.wait_ge(p_out[s], 16 * (NGP + 1))
            with pool.Fori(0, L) as layer:
                with pool.Fori(0, NPAIR) as i:
                    for s in range(2):
                        g = pool.snap(layer * NCH + i * 2 + s)
                        u = pool.snap(layer * NPAIR + i)
                        pool.wait_ge(idx_in[s], (u + 1) * 16)
                        pool.wait_ge(z_done, g + 1)
                        hold(pool, "pool")
                        for k in range(T):
                            pool.indirect_dma_start(xg[s][:, k, :], None, xtab,
                                                    bass.IndirectOffsetOnAxis(ap=idx[s][:, k:k + 1], axis=0)).then_inc(gathered[s], 16)
                for s in range(2):
                    pool.wait_ge(stored[s], layer * (16 * NPAIR) + 16 * (NPAIR + 1))
                pool.wait_ge(const_out, 32)
                hold(pool, "pool")
                pool.indirect_dma_start(headnd[:, :], None, ndrows,
                                        bass.IndirectOffsetOnAxis(ap=hidx[:, :], axis=0)).then_inc(head_in, 16)
                pool.wait_ge(br_dve, layer * BRK + BRK)
                hold(pool, "pool")
                pool.indirect_dma_start(ndrows, bass.IndirectOffsetOnAxis(ap=hidx[:, :], axis=0),
                                        fixed[:, :], None).then_inc(head_out, 16)
                pool.wait_ge(head_out, layer * 16 + 16)
                hold(pool, "pool")
                for j in range(NG):
                    pool.wait_ge(h0_done, layer * NG + (j + 1))
                    hold(pool, "pool")
                    for k in range(G):
                        pool.indirect_dma_start(nd[j % 2][:, k, :], None, ndrows,
                                                bass.IndirectOffsetOnAxis(ap=endix[:, j * G + k:j * G + k + 1], axis=0)).then_inc(nd_in[j % 2], 16)
                for s in range(2):
                    pool.wait_ge(xnew_out[s], layer * (16 * NGP) + 16 * (NGP + 1))

            pool.wait_ge(qzero, 16 * NCH)
            for j in range(NG):
                pool.wait_ge(q_kc, j + 1 + C)
                for k in range(G):
                    pool.indirect_dma_start(qstart, bass.IndirectOffsetOnAxis(ap=startix[:, j * G + k:j * G + k + 1], axis=0),
                                            kvq[j % 2][:, k, 2 * D:3 * D], None,
                                            bounds_check=E - 1, oob_is_err=False).then_inc(q_sc[j % 2], 16)
                if j:
                    pool.wait_ge(q_sc[(j - 1) % 2], ((j - 1) // 2 + 1) * NGATH)
                    pool.sem_inc(q_free, 1)
            for s in range(2):
                pool.wait_ge(q_out[s], NGP * 32 + 32)
            pool.indirect_dma_start(qhead[:, :], None, qtab,
                                    bass.IndirectOffsetOnAxis(ap=dsthead[:, :], axis=0)).then_inc(qhead_in, 16)
            with pool.Fori(0, NPAIR) as i:
                for s in range(2):
                    pool.wait_ge(idx_in[s], i * 16 + (16 + 16 * L * NPAIR))
                    pool.wait_ge(msg_done, i * 2 + s + 1)
                    hold(pool, "pool")
                    for k in range(T):
                        pool.indirect_dma_start(kvg[s][:, k, :], None, kvtab,
                                                bass.IndirectOffsetOnAxis(ap=idx[s][:, k:k + 1], axis=0)).then_inc(gathered[s], 16)
            for s in range(2):
                pool.wait_ge(ms_out[s], 16 * (NPAIR + 1))
            pool.indirect_dma_start(headnd[:, 0:D], None, msrows,
                                    bass.IndirectOffsetOnAxis(ap=hidx[:, :], axis=0)).then_inc(mhead_in, 16)
            pool.wait_ge(b_dve, 3)
            pool.indirect_dma_start(msrows, bass.IndirectOffsetOnAxis(ap=hidx[:, :], axis=0),
                                    fixed[:, 0:D], None).then_inc(mhead_out, 16)
            pool.wait_ge(mhead_out, 16)
            for j in range(NG):
                pool.wait_ge(o_done, j + 1)
                for k in range(G):
                    pool.indirect_dma_start(nd[j % 2][:, k, 0:D], None, msrows,
                                            bass.IndirectOffsetOnAxis(ap=endix[:, j * G + k:j * G + k + 1], axis=0)).then_inc(o_in[j % 2], 16)

        @block.scalar
        def _(act):
            for x in (l_done, flag_done, er_done, fr_done, e_done, f_done, rows_done, qv_done, q_kc, ro_done):
                act.sem_inc(x, C)
            for s in range(2):
                act.sem_inc(stored[s], 16)
                act.sem_inc(ms_out[s], 16)

            act.sem_inc(p_new, C)

            def root(q):
                act.wait_ge(p_ln, q * LNK + 5)
                act.activation(std2[:, :], ss2[:, :], ACT.Sqrt, bias=epscol[0:NP, :], scale=1.0 / D).then_inc(p_std, 1)

            def encoded(q, u, s, following):
                act.wait_ge(p_hT, q + 1 + C)
                act.activation(h0T[0:D, :].rearrange("p (g c) -> p g c", c=P)[:, :, 0:NP], psT[:, :, 0:NP], ACT.Copy).then_inc(p_hc, 1)
                if following:
                    root(q + 1)
                act.wait_ge(p_x, q + 1)
                act.wait_ge(p_out[s], u * 16 + 16)
                hold(act, "act")
                act.activation(xnew[s], psX, ACT.Copy).then_inc(p_new, 1)

            root(0)
            with act.Fori(0, NGP - 1) as i:
                for s in range(2):
                    encoded(act.snap(i * 2 + s), i, s, True)
            for s in range(2):
                encoded(NG - 2 + s, NGP - 1, s, s == 0)

            def flags_and_logits(c, g, s, layer):
                act.wait_ge(s_done, g + C)
                act.activation(flagx[:, :, 1:T + 1],
                               start_f[:, bass.ds(c * T + 1, T)].unsqueeze(1).to_broadcast([P, D, T]),
                               ACT.Copy, scale=-BIG).then_inc(flag_done, 1)
                act.wait_ge(m_done, g + 1 + C)
                act.wait_ge(cs_done, g + C)
                hold(act, "act")
                act.activation(lbuf[:, :, 1:T + 1], mbuf[s][:, :, :], ACT.Copy, scale=tcol[:, bass.ds(layer, 1)]).then_inc(l_done, 1)

            def exponentials(g):
                act.wait_ge(w_done, g + 1 + C)
                act.wait_ge(cn_done, g + C)
                act.activation(ebuf[:, :, 1:W], wbuf[:, :, :], ACT.Relu, scale=-1.0).then_inc(er_done, 1)
                act.activation(fbuf[:, :, 1:W], wbuf[:, :, :], ACT.Relu).then_inc(fr_done, 1)
                act.wait_ge(er_done, g + 1 + C)
                act.activation(ebuf[:, :, 1:W], ebuf[:, :, 1:W], ACT.Exp, scale=-1.0).then_inc(e_done, 1)
                act.wait_ge(fr_done, g + 1 + C)
                act.activation(fbuf[:, :, 1:W], fbuf[:, :, 1:W], ACT.Exp, scale=-1.0).then_inc(f_done, 1)

            def store_rows(c, g, u, s):
                act.wait_ge(n_done, g + 1 + C)
                act.wait_ge(stored[s], u * 16 + 16)
                act.activation(rows[s][:, :, 0:D].rearrange("p t c -> p c t"), nscan[:, :, 1:W], ACT.Copy)
                act.activation(rows[s][:, :, D:2 * D].rearrange("p t c -> p c t"), dscan[:, :, 1:W], ACT.Copy).then_inc(rows_done, 1)
                act.wait_ge(rows_done, g + 1 + C)
                act.dma_start(nd_v[:, bass.ds(c * T, T), :], rows[s][:, :, :]).then_inc(stored[s], 16)

            with act.Fori(0, L) as layer:
                g0 = act.snap(layer * NCH)
                u0 = act.snap(layer * NPAIR)
                act.wait_ge(reset_done, layer + 1)
                flags_and_logits(0, g0, 0, layer)
                exponentials(g0)
                with act.Fori(0, NPAIR - 1) as i:
                    for s in range(2):
                        c = act.snap(i * 2 + s)
                        g = act.snap(g0 + c)
                        flags_and_logits(c + 1, g + 1, 1 - s, layer)
                        store_rows(c, g, u0 + i, s)
                        exponentials(g + 1)
                store_rows(NCH - 2, g0 + (NCH - 2), u0 + (NPAIR - 1), 0)
                flags_and_logits(NCH - 1, g0 + (NCH - 1), 1, layer)
                exponentials(g0 + (NCH - 1))
                store_rows(NCH - 1, g0 + (NCH - 1), u0 + (NPAIR - 1), 1)
                act.activation(tailr[:, :, :], smax[:, :, T].unsqueeze(1).to_broadcast([P, 2, D]), ACT.Copy).then_inc(tail_done, 1)
                act.wait_ge(br_dve, layer * BRK + 4)
                act.activation(g12[:, :, :], g12[:, :, :], ACT.Exp).then_inc(br_act, 1)
                act.wait_ge(br_dve, layer * BRK + 10)
                act.activation(ab[:, :, :], ab[:, :, :], ACT.Exp).then_inc(br_act, 1)
                def transposed(q):
                    act.wait_ge(h0T_done, q + 1)
                    act.activation(h0T[0:D, :].rearrange("p (g c) -> p g c", c=P)[:, :, 0:NP], psT[:, :, 0:NP], ACT.Copy).then_inc(h0c_done, 1)

                def squares(q):
                    act.wait_ge(hw1_done, q + 1)
                    act.activation(sqb, psH, ACT.Square).then_inc(sq_done, 1)
                    act.wait_ge(ss_done, q + 1)
                    act.activation(std[:, :], ss[:, :], ACT.Sqrt, bias=epscol[0:NP, :], scale=1.0 / (2 * D)).then_inc(std_done, 1)

                def normed():
                    for k in range(G):
                        ins = act.activation(hn[:, k, :], psH[:, k, :], ACT.Copy, scale=rstd[:, k:k + 1])
                    ins.then_inc(hn_done, 1)

                def hidden(q):
                    act.wait_ge(hnT_done, q + 1)
                    hold(act, "act")
                    act.activation(hrT.rearrange("p (g c) -> p g c", c=P)[:, :, 0:NP], psN[:, :, 0:NP], ACT.Relu,
                                   bias=lnb[:, bass.ds(layer, 1)], scale=lng[:, bass.ds(layer, 1)]).then_inc(hr_done, 1)

                def residual_squares(j, q):
                    act.wait_ge(xadd_done, q + 1 + C)
                    hold(act, "act")
                    act.activation(lnsq, x3[:, bass.ds(j * G, G), :], ACT.Square).then_inc(sq2_done, 1)

                def residual_std(q):
                    act.wait_ge(ss2_done, q + 1)
                    act.activation(std2[:, :], ss2[:, :], ACT.Sqrt, bias=epscol[0:NP, :], scale=1.0 / D).then_inc(std2_done, 1)

                q0 = act.snap(layer * NG)
                transposed(q0)
                squares(q0)
                transposed(q0 + 1)
                act.wait_ge(rstd_done, q0 + 1)
                normed()
                hidden(q0)
                with act.Fori(1, NG - 1) as j:
                    q = act.snap(q0 + j)
                    squares(q)
                    transposed(q + 1)
                    act.wait_ge(rstd_done, q + 1)
                    normed()
                    residual_squares(j - 1, q - 1)
                    hidden(q)
                    residual_std(q - 1)
                squares(q0 + (NG - 1))
                act.wait_ge(rstd_done, q0 + NG)
                normed()
                residual_squares(NG - 2, q0 + (NG - 2))
                hidden(q0 + (NG - 1))
                residual_std(q0 + (NG - 2))
                residual_squares(NG - 1, q0 + (NG - 1))
                residual_std(q0 + (NG - 1))

            for s in range(2):
                act.sem_inc(q_out[s], 32)

            def x_T(q):
                act.wait_ge(q_hT, q + 1)
                act.activation(h0T[0:D, :].rearrange("p (g c) -> p g c", c=P)[:, :, 0:NP], psT[:, :, 0:NP], ACT.Copy).then_inc(q_hc, 1)

            def x1_std(q):
                act.wait_ge(q_ln, q * LNK + 5)
                act.activation(std2[:, :], ss2[:, :], ACT.Sqrt, bias=epscol[0:NP, :], scale=1.0 / D).then_inc(q_std, 1)

            def h_T(q):
                act.wait_ge(q_h2T, q + 1 + C)
                act.activation(hrT[0:D, :].rearrange("p (g c) -> p g c", c=P)[:, :, 0:NP], psT[:, :, 0:NP], ACT.Copy).then_inc(q_h2c, 1)

            def store_kvq(q, u, s):
                act.wait_ge(q_kvq, q + 1)
                act.wait_ge(q_out[s], u * 32 + 32)
                act.wait_ge(q_free, q + 1)
                hold(act, "act")
                act.activation(kvq[s], psK[:, :, 0:3 * D], ACT.Copy).then_inc(q_kc, 1)
                act.wait_ge(q_kc, q + 1 + C)
                act.dma_start(kvtab_v[:, bass.ds(q * G, G), :], kvq[s][:, :, 0:2 * D]).then_inc(q_out[s], 16)
                act.dma_start(qtab_v[:, bass.ds(q * G, G), :], kvq[s][:, :, 2 * D:3 * D]).then_inc(q_out[s], 16)

            x_T(0)
            x_T(1)
            x1_std(0)
            h_T(0)
            x1_std(1)
            with act.Fori(0, NGP - 1) as i:
                for s in range(2):
                    q = act.snap(i * 2 + s)
                    x_T(q + 2)
                    store_kvq(q, i, s)
                    h_T(q + 1)
                    x1_std(q + 2)
            store_kvq(NG - 2, NGP - 1, 0)
            h_T(NG - 1)
            store_kvq(NG - 1, NGP - 1, 1)

            act.wait_ge(a_reset, 1)
            with act.Fori(0, NPAIR) as i:
                for s in range(2):
                    c = act.snap(i * 2 + s)
                    act.wait_ge(ssc_done, c + C)
                    act.activation(keepx[:, :, 1:W], start_f[:, bass.ds(c * T, T)].unsqueeze(1).to_broadcast([P, D, T]),
                                   ACT.Copy, bias=1.0, scale=-1.0).then_inc(keep_done, 1)
                    act.wait_ge(qs_in[s], i * 16 + 16)
                    act.wait_ge(qsc_done, c + C)
                    act.activation(ebuf[:, :, 1:W], qs[s].rearrange("p t c -> p c t"), ACT.Copy).then_inc(qv_done, 1)
                    act.wait_ge(c2_done, c + 1)
                    act.activation(score[:, :, :], score[:, :, :], ACT.Exp).then_inc(ex_done, 1)
                    act.wait_ge(ssc_done, c + 1 + C)
                    act.wait_ge(ms_out[s], i * 16 + 16)
                    act.activation(msout[s].rearrange("p t c -> p c t"), nscan[:, :, 1:W], ACT.Copy).then_inc(ro_done, 1)
                    act.wait_ge(ro_done, c + 1 + C)
                    act.dma_start(ms_v[:, bass.ds(c * T, T), :], msout[s]).then_inc(ms_out[s], 16)

        @block.tensor
        def _(pe):
            pe.sem_inc(ea_done, C)
            pe.sem_inc(p_hT, C)

            def transposes(out, rows_, last):
                hold(pe, "pe")
                for k in range(G):
                    ins = pe.transpose(out[:, k, 0:NP], rows_[:, k, :], ident[0:NP, 0:NP])
                ins.then_inc(last, 1)

            pe.wait_ge(pool_pro, 6)
            pe.wait_ge(w_in, 16 * (NW + 5))
            with pe.Fori(0, NG) as q:
                pe.wait_ge(p_h, q + 1)
                transposes(psT, h0, p_hT)
                pe.wait_ge(p_hc, q + 1)
                pe.wait_ge(p_new, q + C)
                hold(pe, "pe")
                for k in range(G):
                    ins = pe.matmul(psX[:, k, :], h0T[:, k * P:k * P + NP], encw[:, :], start=True, stop=True)
                ins.then_inc(p_x, 1)
            pe.wait_ge(dve_pro, 4)
            pe.matmul(psA, wbc, ident[:, :], start=True, stop=True).then_inc(passT, 1)
            def edge_terms(g, u, s, weight):
                pe.wait_ge(attr_in[s], u * 16 + 16)
                pe.wait_ge(z_done, g + 1)
                for k in range(T):
                    ins = pe.matmul(ea[s][:, k, :], attr[s][:, k * P:(k + 1) * P], weight[:, :], start=True, stop=True)
                ins.then_inc(ea_done, 1)

            with pe.Fori(0, L) as layer:
                with pe.Fori(0, NPAIR) as i:
                    for s in range(2):
                        c = pe.snap(i * 2 + s)
                        with pe.If(layer < 1):
                            pe.wait_ge(counted, c + C)
                            hold(pe, "pe")
                        edge_terms(pe.snap(layer * NCH + c), pe.snap(layer * NPAIR + i), s, eew)
                        with pe.If(layer < 1):
                            pe.wait_ge(onehots, c + 1)
                            hold(pe, "pe")
                            for k in range(T):
                                ins = pe.matmul(psHist, oh_hi[:, k, :], oh_lo[:, k, :], start=k == 0, stop=k == T - 1)
                            ins.then_inc(hist, 1)
                with pe.If(layer < 1):
                    pe.wait_ge(tables, 1)
                    pe.matmul(psOff, tri[0:NP, 0:NP], cum[:, NJ - 1:NJ], start=True, stop=True).then_inc(offs, 1)
                pe.wait_ge(tail_done, layer + 1)
                pe.wait_ge(cn_done, layer * NCH + NCH + C)
                pe.transpose(psA, tailr[:, :, :].rearrange("p a c -> p (a c)"), ident[:, :])
                pe.transpose(psB, rows[1][:, T - 1, :], ident[:, :]).then_inc(br_pe, 1)
                pe.wait_ge(br_dve, layer * BRK + 6)
                pe.transpose(psA2, rsc[:, 0:P], ident[:, :])
                pe.transpose(psB2, xsc[:, 0:P], ident[:, :]).then_inc(br_pe, 1)
                def sums_T(q):
                    pe.wait_ge(h0_done, q + 1 + C)
                    transposes(psT, h0, h0T_done)

                def times_w1(q):
                    pe.wait_ge(h0c_done, q + 1)
                    for k in range(G):
                        ins = pe.matmul(psH[:, k, :], h0T[:, k * P:k * P + NP], w1[:, bass.ds(layer * (2 * D), 2 * D)], start=True, stop=True)
                    ins.then_inc(hw1_done, 1)

                def hidden_T(q):
                    pe.wait_ge(hn_done, q + 1)
                    transposes(psN, hn, hnT_done)

                def times_w2(q):
                    pe.wait_ge(hr_done, q + 1)
                    pe.wait_ge(xadd_done, q + C)
                    hold(pe, "pe")
                    for k in range(G):
                        ins = pe.matmul(psX[:, k, :], hrT[:, k * P:k * P + NP], w2[:, bass.ds(layer * D, D)], start=True, stop=True)
                    ins.then_inc(hw2_done, 1)

                q0 = pe.snap(layer * NG)
                sums_T(q0)
                times_w1(q0)
                sums_T(q0 + 1)
                hidden_T(q0)
                with pe.Fori(1, NG - 1) as j:
                    q = pe.snap(q0 + j)
                    times_w1(q)
                    sums_T(q + 1)
                    times_w2(q - 1)
                    hidden_T(q)
                times_w1(q0 + (NG - 1))
                times_w2(q0 + (NG - 2))
                hidden_T(q0 + (NG - 1))
                times_w2(q0 + (NG - 1))
                pe.wait_ge(xadd_done, layer * NG + NG + C)

            pe.sem_inc(q_h2T, C)

            def x_T(u, s):
                pe.wait_ge(q_in[s], u * 32 + 32)
                transposes(psT, xold[s], q_hT)

            def times_lin(q):
                pe.wait_ge(q_hc, q + 1)
                pe.wait_ge(q_x1, q + C)
                hold(pe, "pe")
                for k in range(G):
                    ins = pe.matmul(psX[:, k, :], h0T[:, k * P:k * P + NP], linw[:, :], start=True, stop=True)
                ins.then_inc(q_lin, 1)

            def h_T(q):
                pe.wait_ge(q_h, q + 1)
                transposes(psT, h0, q_h2T)

            def times_kvq(q):
                pe.wait_ge(q_h2c, q + 1)
                pe.wait_ge(q_kc, q + C)
                hold(pe, "pe")
                for k in range(G):
                    ins = pe.matmul(psK[:, k, 0:3 * D], hrT[0:D + 1, k * P:k * P + NP], kvqw[:, :], start=True, stop=True)
                ins.then_inc(q_kvq, 1)

            x_T(0, 0)
            times_lin(0)
            x_T(0, 1)
            times_lin(1)
            h_T(0)
            with pe.Fori(0, NGP - 1) as i:
                for s in range(2):
                    q = pe.snap(i * 2 + s)
                    pe.wait_ge(q_h2c, q + 1)
                    hold(pe, "pe")
                    x_T(i + 1, s)
                    times_kvq(q)
                    times_lin(q + 2)
                    h_T(q + 1)
            times_kvq(NG - 2)
            h_T(NG - 1)
            times_kvq(NG - 1)
            pe.wait_ge(q_kc, NG + C)
            with pe.Fori(0, NPAIR) as i:
                for s in range(2):
                    edge_terms(pe.snap(i * 2 + (s + L * NCH)), pe.snap(i + L * NPAIR), s, wew)
            pe.wait_ge(ro_done, NCH + C)
            pe.transpose(psA[0:D, :], msout[1][:, T - 1, :], ident[:, :]).then_inc(b_pe, 1)
            pe.wait_ge(b_dve, 1)
            pe.transpose(psB2[:, 0:D], xsc[0:D, 0:P], ident[0:D, 0:D]).then_inc(b_pe, 1)

        @block.vector
        def _(v):
            for x in (z_done, m_done, s_done, w_done, cs_done, me_done, d_done, n_done, cd_done, cn_done,
                      h0_done, xadd_done, q_x1, counted, msg_done, qsc_done, ssc_done, o_done):
                v.sem_inc(x, C)
            for s in range(2):
                v.sem_inc(xnew_out[s], 16)
                v.sem_inc(o_out[s], 16)
                v.sem_inc(p_out[s], 16)
            chain = sem("dve_chain")
            count = [0, 0]

            def link(ins):
                count[0] += 1
                ins.then_inc(chain, 1)
                v.wait_ge(chain, count[0])

            def signal(ins):
                count[1] += 1
                ins.then_inc(dve_pro, 1)
                v.wait_ge(dve_pro, count[1])


            signal(v.memset(dprev, -1))
            v.memset(nrow[:, 0:D], 0.0)
            signal(v.memset(nrow[:, D:2 * D], 1.0))
            v.memset(h0T[D:D + 1, :], 1.0)
            v.memset(rsc[:, 0:1], -BIG)
            v.memset(xsc[:, 0:1], 0.0)
            link(v.memset(epscol[:, :], LN_EPS))
            def layer_norm(x, q, steps, std_sem):
                hold(v, "dve")
                v.tensor_reduce(mu[:, :], x, AX.X, ALU.add).then_inc(steps, 1)
                v.wait_ge(steps, q * LNK + 1)
                v.tensor_scalar(mu[:, :], mu[:, :], 1.0 / D, None, ALU.mult).then_inc(steps, 1)
                v.wait_ge(steps, q * LNK + 2)
                v.tensor_tensor(lnx, x, mu[:, :].unsqueeze(2).to_broadcast([NP, G, D]), ALU.subtract).then_inc(steps, 1)
                v.wait_ge(steps, q * LNK + 3)
                v.tensor_tensor(lnsq, lnx, lnx, ALU.mult).then_inc(steps, 1)
                v.wait_ge(steps, q * LNK + 4)
                v.tensor_reduce(ss2[:, :], lnsq, AX.X, ALU.add).then_inc(steps, 1)
                v.wait_ge(std_sem, q + 1)
                v.reciprocal(rstd2[:, :], std2[:, :]).then_inc(steps, 1)
                v.wait_ge(steps, q * LNK + 6)
                v.tensor_tensor(lnx, lnx, rstd2[:, :].unsqueeze(2).to_broadcast([NP, G, D]), ALU.mult).then_inc(steps, 1)
                v.wait_ge(steps, q * LNK + 7)

            v.wait_ge(x_in, 16)
            with v.Fori(0, NG) as q:
                layer_norm(x3[:, bass.ds(q * G, G), :], q, p_ln, p_std)
                v.wait_ge(p_hT, q + C)
                v.tensor_scalar(h0, lnx, 0.0, None, ALU.max).then_inc(p_h, 1)
                v.wait_ge(p_h, q + 1)
            for s in range(2):
                v.memset(attr[s][D:D + 1, :], 1.0)
            v.memset(counts[:, :], 0.0)
            signal(v.memset(zeros[:, :], 0.0))

            v.wait_ge(dst_in, 16)
            v.wait_ge(dp_in, 16)
            v.wait_ge(pool_pro, 6)
            link(v.tensor_copy(dst_f, dst_i))
            v.tensor_copy(dsthead[:, :], dst_i[:, 0:1])
            link(v.tensor_copy(col[0], dprev))
            v.tensor_tensor(start_f[:, 1:EP], dst_f[:, 1:EP], dst_f[:, 0:EP - 1], ALU.not_equal)
            v.memset(start_f[:, EP:EP + 1], 0.0)
            v.tensor_tensor(start_f[:, 0:1], dst_f[:, 0:1], col[0], ALU.not_equal)
            v.tensor_tensor(cont[:, :], dst_f[:, 0:1], col[0], ALU.is_equal)
            link(v.tensor_scalar(ne_f, dst_f, dst_f[:, 0:1], None, ALU.not_equal))
            v.tensor_scalar(headneg[:, :], ne_f, -BIG, None, ALU.mult)
            v.tensor_scalar(contneg[:, :], cont[:, :], -1.0, BIG, ALU.add, ALU.mult)
            v.tensor_copy(col[1], pcol_i)
            link(v.tensor_reduce(col[2], ne_f, AX.X, ALU.add))
            link(v.tensor_tensor(col[3], col[1], col[2], ALU.subtract))
            v.tensor_copy(hidx[:, :], col[3])
            link(v.tensor_scalar(col[4], col[2], 0.0, None, ALU.is_equal))
            link(v.tensor_tensor(col[5], col[4], cont[:, :], ALU.mult))
            signal(v.tensor_copy(wbc, col[5].to_broadcast([P, P])))
            v.wait_ge(passT, 1)
            link(v.tensor_copy(passkeep[:, :], psA))
            link(v.tensor_scalar(passneg[:, :], passkeep[:, :], -1.0, BIG, ALU.add, ALU.mult))

            v.tensor_copy(iota_b, iota_i)
            link(v.tensor_scalar(tmp_i, dst_i, 7, None, ALU.logical_shift_right))
            link(v.tensor_copy(hi_b, tmp_i))
            link(v.tensor_scalar(tmp_i, dst_i, HB - 1, None, ALU.bitwise_and))
            link(v.tensor_copy(lo_b, tmp_i))

            def one_hots(c):
                v.tensor_tensor(oh_hi, hi_b[:, bass.ds(c * T, T)].unsqueeze(2).to_broadcast([P, T, HR]),
                                iota_b[:, 0:HR].unsqueeze(1).to_broadcast([P, T, HR]), ALU.is_equal)
                v.tensor_tensor(oh_lo, lo_b[:, bass.ds(c * T, T)].unsqueeze(2).to_broadcast([P, T, HB]),
                                iota_b.unsqueeze(1).to_broadcast([P, T, HB]), ALU.is_equal).then_inc(onehots, 1)

            def add_counts(c):
                v.wait_ge(counted, c + C)
                v.wait_ge(hist, c + 1)
                v.tensor_tensor(counts[:, :], counts[:, :], psHist, ALU.add).then_inc(counted, 1)

            for c in range(2):
                one_hots(c)
                add_counts(c)

            v.wait_ge(w_in, 16 * (NW + 5))
            for weight, mean, k, n in ((w1, w1m, D + 1, 2 * D), (w2, w2m, 2 * D, D), (b2, b2m, NP, D)):
                wv = weight[:, :].rearrange("k (l n) -> k l n", l=L)
                link(v.tensor_reduce(mean[:, :], wv, AX.X, ALU.add))
                link(v.tensor_scalar(mean[:, :], mean[:, :], 1.0 / n, None, ALU.mult))
                link(v.tensor_tensor(wv, wv, mean[:, :].unsqueeze(2).to_broadcast([k, L, n]), ALU.subtract))
            v.wait_ge(const_out, 32)
            for s in range(2):
                v.wait_ge(p_out[s], 16 * (NGP + 1))
            v.memset(lbuf[:, :, T + 1:WM], -BIG)
            v.memset(flagx[:, :, 0:1], 0.0)
            v.memset(flagx[:, :, T + 1:WM], -BIG)
            link(v.memset(fbuf[:, :, 0:1], 0.0))

            def node_tables():
                steps = [0]

                def table(ins):
                    steps[0] += 1
                    ins.then_inc(tables, 1)
                    v.wait_ge(tables, steps[0])

                v.wait_ge(cnt_in, 16)
                table(v.tensor_tensor_scan(cum, cnt, cnt, 0.0, ALU.add, ALU.max))
                v.tensor_scalar(has, cnt, 0.0, None, ALU.is_gt)
                v.wait_ge(offs, 1)
                table(v.tensor_copy(off, psOff))
                table(v.tensor_scalar(cum, cum, off, None, ALU.add))
                table(v.tensor_tensor(spos, cum, cnt, ALU.subtract))
                for pos, before in ((epos, 1.0), (spos, 0.0)):
                    table(v.tensor_scalar(pos, cum if before else spos, -before - E, None, ALU.add))
                    table(v.tensor_tensor(pos, pos, has, ALU.mult))
                    table(v.tensor_scalar(pos, pos, float(E), None, ALU.add))
                v.tensor_copy(endix[:, :], epos)
                table(v.tensor_copy(startix[:, :], spos))
                table(v.memset(x_res, 0.0))

            def message(c, g, u, s):
                v.wait_ge(gathered[s], u * GATH + GATH)
                v.wait_ge(ea_done, g + 1 + C)
                v.wait_ge(cs_done, g + C)
                v.tensor_tensor(zbuf[:, :, :], ea[s].rearrange("p t c -> p c t"), xg[s].rearrange("p t c -> p c t"),
                                ALU.add).then_inc(z_done, 1)
                v.wait_ge(z_done, g + 1 + C)
                v.tensor_scalar(mbuf[s][:, :, :], zbuf[:, :, :], 0.0, EPS, ALU.max, ALU.add).then_inc(m_done, 1)

            def maximum(c, g, s):
                v.wait_ge(l_done, g + 1 + C)
                v.wait_ge(cs_done, g + C)
                v.tensor_tensor_scan(flat(smax), flat(lbuf), flat(flagx), -BIG, ALU.max, ALU.add).then_inc(s_done, 1)
                v.wait_ge(s_done, g + 1 + C)
                v.wait_ge(f_done, g + C)
                v.tensor_tensor(wbuf[:, :, :], lbuf[:, :, 1:T + 1], smax[:, :, 0:T], ALU.subtract).then_inc(w_done, 1)
                v.tensor_tensor(zbuf[:, :, :], lbuf[:, :, 1:T + 1],
                                headneg[:, bass.ds(c * T, T)].unsqueeze(1).to_broadcast([P, D, T]), ALU.add).then_inc(hadd_done, 1)
                v.wait_ge(hadd_done, g + 1)
                v.tensor_reduce(headr2[:, :], zbuf[:, :, :], AX.X, ALU.max).then_inc(hred_done, 1)
                v.wait_ge(hred_done, g + 1)
                v.tensor_tensor(headr[:, :], headr[:, :], headr2[:, :], ALU.max).then_inc(hmax_done, 1)
                v.wait_ge(hmax_done, g + 1)
                v.tensor_copy(lbuf[:, :, 0], smax[:, :, T]).then_inc(cs_done, 1)

            def sums(g, s):
                v.wait_ge(f_done, g + 1 + C)
                v.wait_ge(cn_done, g + C)
                v.tensor_tensor(mebuf[:, :, 1:W], mbuf[s][:, :, :], ebuf[:, :, 1:W], ALU.mult).then_inc(me_done, 1)
                v.wait_ge(rows_done, g + C)
                v.tensor_tensor_scan(flat(dscan), flat(fbuf), flat(ebuf), 0.0, ALU.mult, ALU.add).then_inc(d_done, 1)
                v.wait_ge(me_done, g + 1 + C)
                v.tensor_tensor_scan(flat(nscan), flat(fbuf), flat(mebuf), 0.0, ALU.mult, ALU.add).then_inc(n_done, 1)
                v.wait_ge(d_done, g + 1 + C)
                v.tensor_copy(ebuf[:, :, 0], dscan[:, :, T]).then_inc(cd_done, 1)
                v.wait_ge(n_done, g + 1 + C)
                v.tensor_copy(mebuf[:, :, 0], nscan[:, :, T]).then_inc(cn_done, 1)

            with v.Fori(0, L) as layer:
                g0 = v.snap(layer * NCH)
                u0 = v.snap(layer * NPAIR)
                v.memset(lbuf[:, :, 0:1], -BIG)
                v.memset(ebuf[:, :, 0:1], 0.0)
                v.memset(mebuf[:, :, 0:1], 0.0)
                v.memset(headr[:, :], -BIG).then_inc(reset_done, 1)
                v.wait_ge(reset_done, layer + 1)
                message(0, g0, u0, 0)
                maximum(0, g0, 0)
                with v.Fori(0, NPAIR - 1) as i:
                    for s in range(2):
                        c = v.snap(i * 2 + s)
                        g = v.snap(g0 + c)
                        message(c + 1, g + 1, u0 + i + s, 1 - s)
                        with v.If(layer < 1):
                            one_hots(c + 2)
                        sums(g, s)
                        maximum(c + 1, g + 1, 1 - s)
                        with v.If(layer < 1):
                            add_counts(c + 2)
                with v.If(layer < 1):
                    node_tables()
                v.tensor_tensor(x3, x3, b2[:, bass.ds(layer * D, D)].unsqueeze(1).to_broadcast([NP, NJ, D]), ALU.add).then_inc(bias_done, 1)
                sums(g0 + (NCH - 2), 0)
                message(NCH - 1, g0 + (NCH - 1), u0 + (NPAIR - 1), 1)
                maximum(NCH - 1, g0 + (NCH - 1), 1)
                sums(g0 + (NCH - 1), 1)

                step = [0]

                def bridge(ins):
                    step[0] += 1
                    ins.then_inc(br_dve, 1)
                    v.wait_ge(br_dve, layer * BRK + step[0])

                v.wait_ge(br_pe, layer * 2 + 1)
                bridge(v.tensor_tensor_scan(rsc[:, 1:P + 1], passneg[:, :], psA, -BIG, ALU.add, ALU.max))
                bridge(v.tensor_tensor(g12[:, 0, :], rsc[:, 0:P], passneg[:, :], ALU.add))
                bridge(v.tensor_tensor(g12[:, 0, :], g12[:, 0, :], rsc[:, 1:P + 1], ALU.subtract))
                bridge(v.tensor_tensor(g12[:, 1, :], psA, rsc[:, 1:P + 1], ALU.subtract))
                v.wait_ge(br_act, layer * 2 + 1)
                bridge(v.tensor_tensor(g12[:, 1, :], g12[:, 1, :], psB, ALU.mult))
                bridge(v.tensor_tensor_scan(xsc[:, 1:P + 1], g12[:, 0, :], g12[:, 1, :], 0.0, ALU.mult, ALU.add))
                v.wait_ge(br_pe, layer * 2 + 2)
                bridge(v.tensor_scalar(rcar[:, :], psA2[:, 0:D], contneg[:, :], None, ALU.add))
                bridge(v.tensor_tensor(headr2[:, :], rcar[:, :], headr[:, :], ALU.max))
                bridge(v.tensor_tensor(ab[:, 0, :], rcar[:, :], headr2[:, :], ALU.subtract))
                bridge(v.tensor_tensor(ab[:, 1, :], headr[:, :], headr2[:, :], ALU.subtract))
                v.wait_ge(br_act, layer * 2 + 2)
                nd2 = [t.rearrange("p (a c) -> p a c", a=2) for t in (fixed[:, :], psB2, headnd[:, :])]
                bridge(v.tensor_tensor(nd2[0], nd2[1], ab[:, 0, :].unsqueeze(1).to_broadcast([P, 2, D]), ALU.mult))
                v.wait_ge(head_in, layer * 16 + 16)
                bridge(v.tensor_tensor(nd2[2], nd2[2], ab[:, 1, :].unsqueeze(1).to_broadcast([P, 2, D]), ALU.mult))
                bridge(v.tensor_tensor(fixed[:, :], fixed[:, :], headnd[:, :], ALU.add))
                assert step[0] == BRK

                hold(v, "dve")
                q0 = v.snap(layer * NG)
                n0 = v.snap(layer * NGP)

                def reciprocals(u, s):
                    v.wait_ge(nd_in[s], u * NGATH + NGATH)
                    v.reciprocal(recd, nd[s][:, :, D:2 * D]).then_inc(rec_done, 1)

                def aggregates(q, u, s):
                    v.wait_ge(rec_done, q + 1)
                    v.tensor_tensor(recd, recd, nd[s][:, :, 0:D], ALU.mult).then_inc(agg_done, 1)
                    v.wait_ge(agg_done, q + 1)
                    v.wait_ge(xold_in[s], u * 16 + 16)
                    v.tensor_tensor(h0, recd, xold[s], ALU.add).then_inc(h0_done, 1)

                def deviation(q):
                    v.wait_ge(sq_done, q + 1)
                    v.tensor_reduce(ss[:, :], sqb, AX.X, ALU.add).then_inc(ss_done, 1)
                    v.wait_ge(std_done, q + 1)
                    v.reciprocal(rstd[:, :], std[:, :]).then_inc(rstd_done, 1)

                def residual(j, q):
                    grp = bass.ds(j * G, G)
                    v.wait_ge(hw2_done, q + 1)
                    hold(v, "dve")
                    v.tensor_tensor(x3[:, grp, :], x3[:, grp, :], psX, ALU.add).then_inc(xadd_done, 1)

                def norm(j, q, u, s):
                    v.wait_ge(sq2_done, q + 1)
                    v.tensor_reduce(ss2[:, :], lnsq, AX.X, ALU.add).then_inc(ss2_done, 1)
                    v.wait_ge(std2_done, q + 1)
                    v.reciprocal(rstd2[:, :], std2[:, :]).then_inc(rstd2_done, 1)
                    v.wait_ge(rstd2_done, q + 1)
                    hold(v, "dve")
                    v.tensor_tensor(lnx, x3[:, bass.ds(j * G, G), :], rstd2[:, :].unsqueeze(2).to_broadcast([NP, G, D]), ALU.mult).then_inc(aff_done, 1)
                    v.wait_ge(aff_done, q * 3 + 1)
                    v.tensor_tensor(lnx, lnx, ng[:, bass.ds(layer * D, D)].unsqueeze(1).to_broadcast([NP, G, D]), ALU.mult).then_inc(aff_done, 1)
                    v.wait_ge(aff_done, q * 3 + 2)
                    v.tensor_tensor(lnx, lnx, nb[:, bass.ds(layer * D, D)].unsqueeze(1).to_broadcast([NP, G, D]), ALU.add).then_inc(aff_done, 1)
                    v.wait_ge(aff_done, q * 3 + 3)
                    v.wait_ge(xnew_out[s], u * 16 + 16)
                    v.tensor_scalar(xnew[s], lnx, 0.0, None, ALU.max).then_inc(xnew_done, 1)

                reciprocals(n0, 0)
                aggregates(q0, n0, 0)
                v.wait_ge(h0T_done, q0 + 1)
                reciprocals(n0, 1)
                aggregates(q0 + 1, n0, 1)
                deviation(q0)
                v.wait_ge(h0T_done, q0 + 2)
                reciprocals(n0 + 1, 0)
                aggregates(q0 + 2, n0 + 1, 0)
                with v.Fori(0, NGP - 2) as i:
                    for n in range(2):
                        j = v.snap(i * 2 + (n + 1))
                        q = v.snap(q0 + j)
                        u = v.snap(n0 + i)
                        deviation(q)
                        v.wait_ge(h0T_done, q + 2)
                        reciprocals(u + 1 + n, 1 - n)
                        residual(j - 1, q - 1)
                        aggregates(q + 2, u + 1 + n, 1 - n)
                        norm(j - 1, q - 1, u, n)
                j = NG - 3
                deviation(q0 + j)
                v.wait_ge(h0T_done, q0 + (j + 2))
                reciprocals(n0 + (NGP - 1), 1)
                residual(j - 1, q0 + (j - 1))
                aggregates(q0 + (j + 2), n0 + (NGP - 1), 1)
                norm(j - 1, q0 + (j - 1), n0 + (NGP - 2), 0)
                for j in (NG - 2, NG - 1):
                    deviation(q0 + j)
                    residual(j - 1, q0 + (j - 1))
                    norm(j - 1, q0 + (j - 1), n0 + (j - 1) // 2, (j - 1) % 2)
                residual(NG - 1, q0 + (NG - 1))
                norm(NG - 1, q0 + (NG - 1), n0 + (NGP - 1), 1)
                v.wait_ge(xnew_done, q0 + NG)

            v.memset(hrT[D:D + 1, :], 1.0)
            with v.Fori(0, NGP) as i:
                for s in range(2):
                    q = v.snap(i * 2 + s)
                    grp = bass.ds(q * G, G)
                    v.wait_ge(q_lin, q + 1)
                    v.wait_ge(q_in[s], i * 32 + 32)
                    hold(v, "dve")
                    v.tensor_tensor(x3[:, grp, :], psX, xnew[s], ALU.add).then_inc(q_x1, 1)
                    v.wait_ge(q_x1, q + 1 + C)
                    layer_norm(x3[:, grp, :], q, q_ln, q_std)
                    v.wait_ge(q_h2T, q + C)
                    v.tensor_scalar(h0, lnx, 0.0, None, ALU.max).then_inc(q_h, 1)
                    v.wait_ge(q_h, q + 1)

            v.wait_ge(qhead_in, 16)
            v.wait_ge(q_kc, NG + C)
            v.memset(keepx[:, :, 0:1], 0.0)
            v.tensor_copy(ebuf[:, :, 0], qhead[:, :])
            v.memset(mebuf[:, :, 0:1], 0.0).then_inc(a_reset, 1)
            v.wait_ge(a_reset, 1)
            with v.Fori(0, NPAIR) as i:
                for s in range(2):
                    c = v.snap(i * 2 + s)
                    g = v.snap(c + L * NCH)
                    kg, vg = kvg[s][:, :, 0:D], kvg[s][:, :, D:2 * D]
                    v.wait_ge(gathered[s], i * GATH + (L * NPAIR + 1) * GATH)
                    v.wait_ge(ea_done, g + 1 + C)
                    v.tensor_tensor(zt, ea[s], kg, ALU.mult).then_inc(z_done, 1)
                    v.wait_ge(keep_done, c + 1)
                    v.wait_ge(qv_done, c + 1 + C)
                    v.tensor_tensor_scan(flat(dscan), flat(flagx)[:, 0:D * W], flat(ebuf), 0.0, ALU.mult, ALU.add).then_inc(qsc_done, 1)
                    v.wait_ge(qsc_done, c + 1 + C)
                    v.tensor_copy(ebuf[:, :, 0], dscan[:, :, T]).then_inc(qc_done, 1)
                    v.tensor_tensor(zt, zt, dscan[:, :, 1:W].rearrange("p c t -> p t c"), ALU.mult).then_inc(kq_done, 1)
                    v.wait_ge(kq_done, c + 1)
                    v.tensor_reduce(score[:, :, :], zt.rearrange("p t (h d) -> p t h d", h=H), AX.X, ALU.add).then_inc(sr_done, 1)
                    v.wait_ge(sr_done, c + 1)
                    v.tensor_scalar(score[:, :, :], score[:, :, :], INV_SQRT_HD, 5.0, ALU.mult, ALU.min).then_inc(c1_done, 1)
                    v.wait_ge(c1_done, c + 1)
                    v.tensor_scalar(score[:, :, :], score[:, :, :], -5.0, None, ALU.max).then_inc(c2_done, 1)
                    v.wait_ge(ex_done, c + 1)
                    v.tensor_tensor(mebuf[:, :, 1:W].rearrange("p (h d) t -> p t h d", h=H),
                                    vg.rearrange("p t (h d) -> p t h d", h=H),
                                    score[:, :, :].unsqueeze(3).to_broadcast([P, T, H, D // H]), ALU.mult).then_inc(msg_done, 1)
                    v.wait_ge(msg_done, c + 1 + C)
                    v.wait_ge(ro_done, c + C)
                    v.tensor_tensor_scan(flat(nscan), flat(flagx)[:, 0:D * W], flat(mebuf), 0.0, ALU.mult, ALU.add).then_inc(ssc_done, 1)
                    v.wait_ge(ssc_done, c + 1 + C)
                    v.tensor_copy(mebuf[:, :, 0], nscan[:, :, T]).then_inc(sc_done, 1)
                    v.wait_ge(sc_done, c + 1)

            v.wait_ge(b_pe, 1)
            v.tensor_tensor_scan(xsc[0:D, 1:P + 1], passkeep[0:D, :], psA[0:D, :], 0.0, ALU.mult, ALU.add).then_inc(b_dve, 1)
            v.wait_ge(b_pe, 2)
            v.tensor_scalar(fixed[:, 0:D], psB2[:, 0:D], cont[:, :], None, ALU.mult).then_inc(b_dve, 1)
            v.wait_ge(b_dve, 2)
            v.wait_ge(mhead_in, 16)
            v.tensor_tensor(fixed[:, 0:D], fixed[:, 0:D], headnd[:, 0:D], ALU.add).then_inc(b_dve, 1)

            with v.Fori(0, NGP) as j:
                for s in range(2):
                    v.wait_ge(o_in[s], j * NGATH + NGATH)
                    v.wait_ge(o_out[s], j * 16 + 16)
                    v.tensor_tensor(xnew[s], x3[:, bass.ds((j * 2 + s) * G, G), :], nd[s][:, :, 0:D], ALU.add).then_inc(o_done, 1)


def kernel(x, src, dst, edge_attr_64, **w):
    import numpy as np
    import concourse.bacc as bacc
    from concourse.bass_utils import run_bass_kernel_spmd

    w = {k: np.asarray(v) for k, v in w.items()}
    ins = {"x": x, "src": src, "dst": dst,
           "attrT": np.asarray(edge_attr_64).reshape(P, EP, D).transpose(2, 1, 0).reshape(D, E),
           "convLnG_T": w["L0_gnn_convLnG"].T, "convLnB_T": w["L0_gnn_convLnB"].T}
    for n in ("encW", "encb", "eencW", "eencb", "convW1", "convb1", "convW2", "convb2", "t", "normG", "normB", "linW", "linb"):
        ins[n] = w["L0_gnn_" + n]
    for n in ("WQ", "bQ", "WK", "bK", "WE", "bE", "WV", "bV"):
        ins[n] = w["L1_gnn_" + n]
    nc = bacc.Bacc("TRN2", target_bir_lowering=False, num_devices=1)
    arrays, aps = {}, {}
    for n, v in ins.items():
        v = np.ascontiguousarray(v)
        arrays["in_" + n] = v
        aps[n] = nc.dram_tensor("in_" + n, v.shape, mybir.dt.from_np(v.dtype), kind="ExternalInput").ap()
    out = nc.dram_tensor("out", (N, D), F32, kind="ExternalOutput").ap()
    gnn_kernel(nc, aps, out)
    r = run_bass_kernel_spmd(nc, [arrays], core_ids=[0])
    return r.results[0]["out"]
```

```python
from contextlib import ExitStack

import concourse.bass as bass
from concourse import mybir

N, E, D = 10000, 160000, 64
L, H = 4, 8
P = 128
EP = E // P
T = 25
NCH = EP // T
NPAIR = NCH // 2
NP = 125
NJ = N // NP
G = 8
NG = NJ // G
NGP = NG // 2
W = T + 1
WM = T + 2
HB = 128
HR = -(-N // HB)
BIG = 1.0e30
EPS, LN_EPS = 1e-7, 1e-5
C = 2
GATH = 16 * T
NGATH = 16 * G
INV_SQRT_HD = (D // H) ** -0.5

F32, I32, BF16 = mybir.dt.float32, mybir.dt.int32, mybir.dt.bfloat16
ALU, ACT, AX = mybir.AluOpType, mybir.ActivationFunctionType, mybir.AxisListType


def gnn_kernel(nc, a, out):
    ctx = ExitStack()
    with ctx:
        def sb(name, shape, dt=F32):
            return ctx.enter_context(nc.sbuf_tensor(name, shape, dt))

        def sem(name):
            return ctx.enter_context(nc.semaphore(name))

        def dram(name, shape, dt=F32):
            return nc.dram_tensor(name, shape, dt, kind="Internal").ap()

        def flat(t):
            return t[:, :, :].rearrange("p a b -> p (a b)")

        def groups(t, c):
            return t.rearrange("p (g c) -> p g c", c=c)

        xtab = dram("xtab", (N, D))
        kvtab = dram("kvtab", (N, 2 * D))
        qtab = dram("qtab", (N, D))
        qstart = dram("qstart", (E, D))
        ndrows = dram("ndrows", (E + 1, 2 * D))
        msrows = dram("msrows", (E + 1, D))
        cnttab = dram("cnttab", (HR, HB))
        place = dram("place", (N, 1), I32)
        edges_s = dram("edges_s", (E, D + 2))
        src_s, dst_s = dram("src_s", (P, EP), I32), dram("dst_s", (P, EP), I32)
        attrT_s = dram("attrT_s", (D, NCH, T * P))

        ident = sb("ident", [P, P])
        tri = sb("tri", [P, P])
        start_f = sb("start_f", [P, EP + 1])
        headneg = sb("headneg", [P, EP])
        x_all = sb("x_all", [P, NJ * D])
        x_res = x_all[0:NP, :]
        endix = sb("endix", [NP, NJ], I32)
        startix = sb("startix", [NP, NJ], I32)
        counts = sb("counts", [HR, HB])
        zeros = sb("zeros", [P, T * D // 4])
        eew = sb("eew", [D + 1, D])
        wew = sb("wew", [D + 1, D])
        encw = sb("encw", [D + 1, D])
        linw = sb("linw", [D + 1, D])
        kvqw = sb("kvqw", [D + 1, 3 * D])
        w1 = sb("w1", [D + 1, L * 2 * D])
        w1m = sb("w1m", [D + 1, L])
        w2 = sb("w2", [2 * D, L * D])
        b2 = sb("b2", [NP, L * D])
        w2m = sb("w2m", [2 * D, L])
        b2m = sb("b2m", [NP, L])
        lng = sb("lng", [2 * D, L])
        lnb = sb("lnb", [2 * D, L])
        tcol = sb("tcol", [P, L])
        ng = sb("ng", [NP, L * D])
        nb = sb("nb", [NP, L * D])
        epscol = sb("epscol", [P, 1])

        attr = [sb(f"attr{s}", [D + 1, T * P]) for s in range(2)]
        idx = [sb(f"idx{s}", [P, T], I32) for s in range(2)]
        kvg = [sb(f"kvg{s}", [P, T, 2 * D]) for s in range(2)]
        rows = [sb(f"rows{s}", [P, T, 2 * D]) for s in range(2)]
        zbuf = sb("zbuf", [P, D, T])
        mbuf = [sb(f"mbuf{s}", [P, D, T]) for s in range(2)]
        lbuf = sb("lbuf", [P, D, WM])
        flagx = sb("flagx", [P, D, WM])
        smax = sb("smax", [P, D, WM])
        wbuf = sb("wbuf", [P, D, T])
        ebuf = sb("ebuf", [P, D, W])
        fbuf = sb("fbuf", [P, D, W])
        mebuf = sb("mebuf", [P, D, W])
        dscan = sb("dscan", [P, D, W])
        nscan = sb("nscan", [P, D, W])
        headr = sb("headr", [P, D])
        headr2 = sb("headr2", [P, D])
        xg = [flat(k)[:, 0:T * D].rearrange("p (t c) -> p t c", c=D) for k in kvg]
        zt = flat(zbuf).rearrange("p (t c) -> p t c", c=D)
        keepx = flat(flagx)[:, 0:D * W].rearrange("p (c t) -> p c t", t=W)
        msout = [flat(r)[:, 0:T * D].rearrange("p (t c) -> p t c", c=D) for r in rows]
        qs = [flat(r)[:, T * D:2 * T * D].rearrange("p (t c) -> p t c", c=D) for r in rows]
        score = sb("score", [P, T, H])

        hidx = sb("hidx", [P, 1], I32)
        cont = sb("cont", [P, 1])
        contneg = sb("contneg", [P, 1])
        passneg = sb("passneg", [P, P])
        passkeep = sb("passkeep", [P, P])
        tailr = sb("tailr", [P, 2, D])
        rsc = sb("rsc", [P, P + 1])
        xsc = sb("xsc", [P, P + 1])
        g12 = sb("g12", [P, 2, P])
        headnd = sb("headnd", [P, 2 * D])
        rcar = sb("rcar", [P, D])
        ab = sb("ab", [P, 2, D])
        fixed = sb("fixed", [P, 2 * D])
        qhead = sb("qhead", [P, D])
        dsthead = sb("dsthead", [P, 1], I32)

        nd = [kvg[s][0:NP, 0:G, :] for s in range(2)]
        xold = [groups(flat(rows[s])[0:NP, 0:G * D], D) for s in range(2)]
        xnew = [groups(flat(rows[s])[0:NP, G * D:2 * G * D], D) for s in range(2)]
        kvq = [groups(flat(rows[s])[0:NP, 2 * G * D:5 * G * D], 3 * D) for s in range(2)]
        recd = groups(flat(zbuf)[0:NP, 0:G * D], D)
        h0 = groups(flat(zbuf)[0:NP, G * D:2 * G * D], D)
        h0T = sb("h0T", [D + 1, G * P])
        sqb = groups(flat(mbuf[0])[0:NP, 0:2 * G * D], 2 * D)
        hn = groups(flat(mbuf[1])[0:NP, 0:2 * G * D], 2 * D)
        hrT = flat(wbuf)[:, 0:G * P]
        hT = [h0T[:, :], hrT[0:D + 1, :]]
        lnx = groups(flat(dscan)[0:NP, 0:G * D], D)
        lnsq = groups(flat(dscan)[0:NP, G * D:2 * G * D], D)
        ss, std, rstd = (sb(n, [NP, G]) for n in ("ss", "std", "rstd"))
        mu, ss2, std2, rstd2 = (sb(n, [NP, G]) for n in ("mu", "ss2", "std2", "rstd2"))

        PS = ctx.enter_context(nc.psum_tensor("PS", [P, 4096], F32))
        ea = [PS[:, s * 2048:s * 2048 + T * D].rearrange("p (t c) -> p t c", c=D) for s in range(2)]
        psT = PS[0:D, 0:G * P].rearrange("p (g c) -> p g c", c=P)
        psH = PS[0:NP, 1024:1024 + G * 2 * D].rearrange("p (g c) -> p g c", c=2 * D)
        psN = PS[:, 2048:2048 + G * P].rearrange("p (g c) -> p g c", c=P)
        psX = PS[0:NP, 3072:3072 + G * D].rearrange("p (g c) -> p g c", c=D)
        psK = PS[0:NP, 1024:1024 + G * 256].rearrange("p (g c) -> p g c", c=256)
        psA, psB = PS[:, 3712:3840], PS[:, 3840:3968]
        psA2, psB2 = PS[:, 1664:1792], PS[:, 1792:1920]
        psHist, psOff, psOrd = PS[0:HR, 1664:1792], PS[0:NP, 1792:1793], PS[0:1, 1793:1794]

        dst_i = flat(nscan)[:, 0:EP].bitcast(I32)
        dst_f = flat(mbuf[0])[:, 0:EP]
        ne_f = flat(mbuf[1])[:, 0:EP]
        tmp_i = flat(ebuf)[:, 0:EP].bitcast(I32)
        iota_i = flat(smax)[:, 0:HB].bitcast(I32)
        pcol_i = flat(smax)[:, HB:HB + 1].bitcast(I32)
        dprev = flat(smax)[:, HB + 1:HB + 2].bitcast(I32)
        col = [flat(smax)[:, HB + 2 + n:HB + 3 + n] for n in range(6)]
        wbc = flat(smax)[:, 2 * HB:3 * HB]
        nrow = flat(smax)[0:1, 3 * HB:3 * HB + 2 * D]
        used = [0]

        def part(floats):
            used[0] += floats
            return x_all[:, used[0] - floats:used[0]]

        oh_lo = part(T * HB // 2).bitcast(BF16).rearrange("p (t c) -> p t c", c=HB)
        oh_hi = part(-(-T * HR // 2)).bitcast(BF16)[:, 0:T * HR].rearrange("p (t c) -> p t c", c=HR)
        hi_b, lo_b = part(EP // 2).bitcast(BF16), part(EP // 2).bitcast(BF16)
        iota_b = part(HB // 2).bitcast(BF16)
        cnt, cum, has, epos, spos = (part(NJ)[0:NP, :] for n in range(5))
        off = part(1)[0:NP, :]

        unsorted = sb("unsorted", [1, 1], I32)
        row_i = flat(lbuf)[:, 0:2 * P].bitcast(I32).rearrange("p (k n) -> p k n", k=2)
        row_f, same, after = (flat(lbuf)[:, n * P:(n + 1) * P] for n in (2, 3, 4))
        edge = flat(lbuf)[:, 5 * P:5 * P + 2 * (D + 2)].rearrange("p (k c) -> p k c", k=2)
        src_i, node_i = ([edge[:, k, D + n:D + n + 1].bitcast(I32) for k in range(2)] for n in range(2))
        scol = [flat(lbuf)[:, 8 * P + n:8 * P + n + 1] for n in range(12)]
        (base_i, next_i, pos_i, last_i) = (x.bitcast(I32) for x in scol[0:4])
        (node_f, total, later, base_f, next_f, pos_f, last_f, skip_f) = scol[4:12]
        place_i = flat(flagx)[0:NP, 0:NJ].bitcast(I32)
        place_c, place_f, place_o = (flat(flagx)[0:NP, n * NJ:(n + 1) * NJ] for n in (1, 2, 3))
        sorted_rows = flat(rows[0])[:, 0:T * (D + 2)].rearrange("p (t c) -> p t c", c=D + 2)
        psS = PS[0:D, 0:T * P]

        attrT = a["attrT"].rearrange("k (c m) -> k c m", c=NCH)
        src_v = a["src"].rearrange("(p e) -> p e", p=P)
        dst_v = a["dst"].rearrange("(p e) -> p e", p=P)
        node_t, src_t = a["dst"].rearrange("(i p) -> p i", p=P), a["src"].rearrange("(i p) -> p i", p=P)
        attr_t = a["attr"].rearrange("(i p) c -> p i c", p=P)
        edges_v = edges_s.rearrange("(p e) c -> p e c", p=P)
        place_v = place.rearrange("(p j) o -> p (j o)", p=NP)
        x_v = a["x"].rearrange("(p j) c -> p j c", p=NP)
        out_v = out.rearrange("(p j) c -> p j c", p=NP)
        xtab_v = xtab.rearrange("(p j) c -> p j c", p=NP)
        kvtab_v = kvtab.rearrange("(p j) c -> p j c", p=NP)
        qtab_v = qtab.rearrange("(p j) c -> p j c", p=NP)
        nd_v = ndrows[0:E, :].rearrange("(p e) c -> p e c", p=P)
        ms_v = msrows[0:E, :].rearrange("(p e) c -> p e c", p=P)
        qst_v = qstart.rearrange("(p e) c -> p (e c)", p=P)
        qst_t = qstart.rearrange("(p e) c -> p e c", p=P)
        cnt_v = cnttab.rearrange("a b -> (a b)")[0:N].rearrange("(p j) -> p j", p=NP)
        x3 = x_res.rearrange("p (j c) -> p j c", c=D)

        w_in, x_in, dst_in = sem("w_in"), sem("x_in"), sem("dst_in")
        pool_pro, dve_pro = sem("pool_pro"), sem("dve_pro")
        qzero, const_out, cnt_out, cnt_in = (sem(n) for n in "qzero const_out cnt_out cnt_in".split())
        onehots, hist, counted, tables, passT, offs = (
            sem(n) for n in "onehots hist counted tables passT offs".split())
        ordered = sem("ordered")
        so_in, so_place, so_steps, so_ready, so_sc, so_free = (
            sem(n) for n in "so_in so_place so_steps so_ready so_sc so_free".split())
        so_tab, so_back, so_scan, so_off, so_new = (sem(n) for n in "so_tab so_back so_scan so_off so_new".split())
        so_rows, so_T, so_copied, so_out = (sem(n) for n in "so_rows so_T so_copied so_out".split())
        attr_in = [sem(f"attr_in{s}") for s in range(2)]
        idx_in = [sem(f"idx_in{s}") for s in range(2)]
        gathered = [sem(f"gathered{s}") for s in range(2)]
        stored = [sem(f"stored{s}") for s in range(2)]
        ea_done, z_done, m_done, l_done, flag_done = (sem(n) for n in "ea_done z_done m_done l_done flag_done".split())
        s_done, w_done, hadd_done, hred_done, hmax_done, cs_done = (
            sem(n) for n in "s_done w_done hadd_done hred_done hmax_done cs_done".split())
        er_done, fr_done, e_done, f_done = (sem(n) for n in "er_done fr_done e_done f_done".split())
        me_done, d_done, n_done, cd_done, cn_done, rows_done = (
            sem(n) for n in "me_done d_done n_done cd_done cn_done rows_done".split())
        reset_done = sem("reset_done")
        tail_done, br_pe, br_dve, br_act = (sem(n) for n in "tail_done br_pe br_dve br_act".split())
        head_in, head_out = sem("head_in"), sem("head_out")
        nd_in = [sem(f"nd_in{s}") for s in range(2)]
        xold_in = [sem(f"xold_in{s}") for s in range(2)]
        xnew_out = [sem(f"xnew_out{s}") for s in range(2)]
        rec_done, agg_done, h0_done, h0T_done, h0c_done, hw1_done, sq_done, ss_done, std_done, rstd_done = (
            sem(n) for n in "rec_done agg_done h0_done h0T_done h0c_done hw1_done sq_done ss_done std_done rstd_done".split())
        hn_done, hnT_done, hr_done, hw2_done, xadd_done = (
            sem(n) for n in "hn_done hnT_done hr_done hw2_done xadd_done".split())
        sq2_done, ss2_done, std2_done, rstd2_done, aff_done, xnew_done = (
            sem(n) for n in "sq2_done ss2_done std2_done rstd2_done aff_done xnew_done".split())
        p_ln, p_std, p_h, p_hT, p_hc, p_x, p_new = (
            sem(n) for n in "p_ln p_std p_h p_hT p_hc p_x p_new".split())
        p_out = [sem(f"p_out{s}") for s in range(2)]
        q_in = [sem(f"q_in{s}") for s in range(2)]
        q_free = sem("q_free")
        q_out = [sem(f"q_out{s}") for s in range(2)]
        q_sc = [sem(f"q_sc{s}") for s in range(2)]
        q_hT, q_hc, q_lin, q_x1, q_ln, q_std, q_h, q_h2T, q_h2c, q_kvq, q_kc = (
            sem(n) for n in "q_hT q_hc q_lin q_x1 q_ln q_std q_h q_h2T q_h2c q_kvq q_kc".split())
        qs_in = [sem(f"qs_in{s}") for s in range(2)]
        ms_out = [sem(f"ms_out{s}") for s in range(2)]
        keep_done, qv_done, qsc_done, qc_done, kq_done, sr_done, c1_done, c2_done, ex_done, msg_done, ssc_done, sc_done, ro_done = (
            sem(n) for n in ("keep_done qv_done qsc_done qc_done kq_done sr_done c1_done c2_done ex_done msg_done "
                             "ssc_done sc_done ro_done").split())
        qhead_in, a_reset = sem("qhead_in"), sem("a_reset")
        b_pe, b_dve, mhead_in, mhead_out = (sem(n) for n in "b_pe b_dve mhead_in mhead_out".split())
        o_in = [sem(f"o_in{s}") for s in range(2)]
        o_out = [sem(f"o_out{s}") for s in range(2)]
        o_done = sem("o_done")

        LNK = 7
        TILES = E // P
        SOK = 9
        BRK = 13
        NW = 20
        block = ctx.enter_context(nc.Block())

        held = {e: sem(f"held_{e}") for e in ("sp", "pool", "act", "pe", "dve")}

        def hold(eng, name):
            eng.sem_inc(held[name], 1)

        @block.sync
        def _(sp):
            sp.dma_start(dst_i, dst_v).then_inc(dst_in, 16)
            sp.wait_ge(dve_pro, 1)
            sp.dma_start(dprev[1:P, :], dst_v[0:P - 1, EP - 1:EP], allow_slow_non_contiguous=True).then_inc(dst_in, 16)
            sp.dma_start(x_res, x_v.rearrange("p j c -> p (j c)")).then_inc(x_in, 16)
            loads = [
                (eew[0:D, :], a["eencW"]), (eew[D:D + 1, :], a["eencb"].unsqueeze(0)),
                (wew[0:D, :], a["WE"]), (wew[D:D + 1, :], a["bE"].unsqueeze(0)),
                (encw[0:D, :], a["encW"]), (encw[D:D + 1, :], a["encb"].unsqueeze(0)),
                (linw[0:D, :], a["linW"]), (linw[D:D + 1, :], a["linb"].unsqueeze(0)),
                (kvqw[0:D, 0:D], a["WK"]), (kvqw[D:D + 1, 0:D], a["bK"].unsqueeze(0)),
                (kvqw[0:D, D:2 * D], a["WV"]), (kvqw[D:D + 1, D:2 * D], a["bV"].unsqueeze(0)),
                (kvqw[0:D, 2 * D:3 * D], a["WQ"]), (kvqw[D:D + 1, 2 * D:3 * D], a["bQ"].unsqueeze(0)),
                (w1[0:D, :].rearrange("k (l n) -> k l n", l=L), a["convW1"].rearrange("l k n -> k l n")),
                (w1[D:D + 1, :], a["convb1"].rearrange("l n -> (l n)").unsqueeze(0)),
                (w2[:, :].rearrange("k (l n) -> k l n", l=L), a["convW2"].rearrange("l k n -> k l n")),
                (b2[:, :], a["convb2"].rearrange("l n -> (l n)").partition_broadcast(NP)),
                (lng[:, :], a["convLnG_T"]), (lnb[:, :], a["convLnB_T"]),
            ]
            assert len(loads) == NW
            for dst, src in loads:
                sp.dma_start(dst, src).then_inc(w_in, 16)
            sp.dma_start(tcol[:, :], a["t"].partition_broadcast(P)).then_inc(w_in, 16)
            for dst, src in ((ng, a["normG"]), (nb, a["normB"])):
                sp.dma_start(dst[:, 0:(L - 1) * D], src[1:L, :].rearrange("l c -> (l c)").partition_broadcast(NP)).then_inc(w_in, 16)
                sp.dma_start(dst[:, (L - 1) * D:], src[0, :].partition_broadcast(NP)).then_inc(w_in, 16)
            sp.wait_ge(dve_pro, 2)
            sp.dma_start(ndrows[E:E + 1, :], nrow).then_inc(const_out, 16)
            sp.dma_start(msrows[E:E + 1, :], nrow[:, 0:D]).then_inc(const_out, 16)
            sp.wait_ge(dve_pro, 4)
            flag = sp.value_load(unsorted[0:1, 0:1], min_val=0, max_val=P)
            with sp.If(flag > 0):
                sp.dma_start(place_v, zeros[0:NP, 0:NJ].bitcast(I32)).then_inc(so_tab, 16)
                sp.wait_ge(so_tab, 16)
                for moves in (False, True):
                    with sp.Fori(0, TILES // 2) as i:
                        sp.wait_ge(so_free, i * 2 + (TILES + 1 if moves else 1))
                        hold(sp, "sp")
                        two = bass.ds(i * 2, 2)
                        sp.dma_start(edge[:, :, D + 1].bitcast(I32), node_t[:, two], allow_slow_non_contiguous=True).then_inc(so_in, 16)
                        sp.dma_start(row_i.rearrange("p k n -> p (k n)"), a["dst"][bass.ds(i * (2 * P), 2 * P)].partition_broadcast(P)).then_inc(so_in, 16)
                        if moves:
                            sp.dma_start(edge[:, :, D].bitcast(I32), src_t[:, two], allow_slow_non_contiguous=True).then_inc(so_in, 16)
                            sp.dma_start(edge[:, :, 0:D], attr_t[:, two, :]).then_inc(so_in, 16)
                    if not moves:
                        sp.wait_ge(so_free, TILES + 1)
                        sp.dma_start(place_i, place_v).then_inc(so_back, 16)
                        sp.wait_ge(so_new, 3)
                        sp.dma_start(place_v, place_i).then_inc(so_tab, 16)
                        sp.wait_ge(so_tab, 32)
                sp.wait_ge(so_free, 2 * TILES + 1)
                with sp.Fori(0, NCH) as c:
                    sp.dma_start(sorted_rows, edges_v[:, bass.ds(c * T, T), :]).then_inc(so_rows, 16)
                    sp.wait_ge(so_copied, c + 1)
                    sp.dma_start(attrT_s[:, c, :], attr[0][0:D, :]).then_inc(so_out, 16)
                    sp.dma_start(src_s[:, bass.ds(c * T, T)], idx[0][:, :]).then_inc(so_out, 16)
                    sp.dma_start(dst_s[:, bass.ds(c * T, T)], idx[1][:, :]).then_inc(so_out, 16)
                    sp.wait_ge(so_out, c * 48 + 48)
                    hold(sp, "sp")
                sp.dma_start(dst_i, dst_s).then_inc(so_back, 16)
                sp.dma_start(dprev[1:P, :], dst_s[0:P - 1, EP - 1:EP], allow_slow_non_contiguous=True).then_inc(so_back, 16)

            def load_chunk(c, g, s):
                for came, attrs, srcs in ((flag < 1, attrT, src_v), (flag > 0, attrT_s, src_s)):
                    with sp.If(came):
                        sp.wait_ge(z_done, g + 1)
                        sp.dma_start(idx[s][:, :], srcs[:, bass.ds(c * T, T)]).then_inc(idx_in[s], 16)
                        sp.wait_ge(ea_done, g + 1)
                        sp.dma_start(attr[s][0:D, :], attrs[:, c, :]).then_inc(attr_in[s], 16)

            def zero_rows(c):
                sp.dma_start(qst_v[:, bass.ds(c * (T * D), T * D)].rearrange("p (n f) -> p n f", n=4),
                             zeros[:, :].unsqueeze(1).to_broadcast([P, 4, T * D // 4])).then_inc(qzero, 16)

            def load_group(layer, j, s):
                sp.wait_ge(h0_done, layer * NG + (j * 2 + s + 1))
                sp.dma_start(xold[s], xtab_v[:, bass.ds((j * 2 + s) * G, G), :]).then_inc(xold_in[s], 16)

            def store_group(layer, j, s):
                sp.wait_ge(xnew_done, layer * NG + j * 2 + s + 1)
                sp.dma_start(xtab_v[:, bass.ds((j * 2 + s) * G, G), :], xnew[s]).then_inc(xnew_out[s], 16)

            for s in range(2):
                load_chunk(s, s, s)
            with sp.Fori(0, NGP) as i:
                for s in range(2):
                    q = sp.snap(i * 2 + s)
                    sp.wait_ge(p_new, q + 1 + C)
                    sp.dma_start(xtab_v[:, bass.ds(q * G, G), :], xnew[s]).then_inc(p_out[s], 16)
            for c in range(2):
                zero_rows(c)

            with sp.Fori(0, L) as layer:
                with sp.Fori(1, NPAIR) as i:
                    for s in range(2):
                        c = sp.snap(i * 2 + s)
                        load_chunk(c, sp.snap(layer * NCH + c), s)
                        with sp.If(layer < 1):
                            zero_rows(c)
                with sp.If(layer < 1):
                    sp.wait_ge(counted, NCH + C)
                    sp.dma_start(cnttab, counts[:, :]).then_inc(cnt_out, 16)
                    sp.wait_ge(cnt_out, 16)
                    sp.dma_start(cnt, cnt_v).then_inc(cnt_in, 16)
                for s in range(2):
                    load_chunk(s, sp.snap(layer * NCH + (NCH + s)), s)
                for s in range(2):
                    sp.wait_ge(stored[s], layer * (16 * NPAIR) + 16 * (NPAIR + 1))
                for j in range(4):
                    load_group(layer, j // 2, j % 2)
                with sp.Fori(2, NGP) as j:
                    for s in range(2):
                        load_group(layer, j, s)
                        store_group(layer, j - 2, s)
                for j in range(NG - 4, NG):
                    store_group(layer, j // 2, j % 2)

            def load_x(q, s):
                sp.wait_ge(q_x1, q + 1)
                hold(sp, "sp")
                sp.dma_start(xold[s], xtab_v[:, bass.ds(q * G, G), :]).then_inc(q_in[s], 16)
                sp.dma_start(xnew[s], x_v[:, bass.ds(q * G, G), :]).then_inc(q_in[s], 16)

            for s in range(2):
                sp.wait_ge(xnew_out[s], 16 * (L * NGP + 1))
            for q in range(2):
                load_x(q, q)
            with sp.Fori(0, NGP - 1) as i:
                for s in range(2):
                    q = sp.snap(i * 2 + s)
                    load_x(q + 2, s)

            for s in range(2):
                sp.wait_ge(q_sc[s], NGP * NGATH)
                sp.wait_ge(q_out[s], NGP * 32 + 32)

            def load_q(c, s):
                sp.wait_ge(qv_done, c + 1)
                hold(sp, "sp")
                sp.dma_start(qs[s], qst_t[:, bass.ds(c * T, T), :]).then_inc(qs_in[s], 16)

            for s in range(2):
                load_q(s, s)
            with sp.Fori(1, NPAIR) as i:
                for s in range(2):
                    c = sp.snap(i * 2 + s)
                    load_chunk(c, sp.snap(c + L * NCH), s)
                    load_q(c, s)

            for s in range(2):
                sp.wait_ge(ms_out[s], 16 * (NPAIR + 1))

            with sp.Fori(0, NGP) as j:
                for s in range(2):
                    sp.wait_ge(o_done, j * 2 + s + 1 + C)
                    sp.dma_start(out_v[:, bass.ds((j * 2 + s) * G, G), :], xnew[s]).then_inc(o_out[s], 16)
            for s in range(2):
                sp.wait_ge(o_out[s], 16 * (NGP + 1))

        @block.gpsimd
        def _(pool):
            pool.sem_inc(q_free, C)
            pool.memset(ident[:, :], 0.0).then_inc(pool_pro, 1)
            pool.memset(tri[:, :], 1.0).then_inc(pool_pro, 1)
            pool.iota(iota_i, pattern=[[1, HB]], base=0, channel_multiplier=0).then_inc(pool_pro, 1)
            pool.iota(pcol_i, pattern=[[0, 1]], base=EP - 1, channel_multiplier=EP).then_inc(pool_pro, 1)
            pool.wait_ge(pool_pro, 4)
            pool.affine_select(out=ident[:, :], in_=ident[:, :], compare_op=ALU.not_equal, fill=1.0, base=0,
                               pattern=[[-1, P]], channel_multiplier=1).then_inc(pool_pro, 1)
            pool.affine_select(out=tri[:, :], in_=tri[:, :], compare_op=ALU.is_gt, fill=0.0, base=0,
                               pattern=[[1, P]], channel_multiplier=-1).then_inc(pool_pro, 1)

            pool.wait_ge(dve_pro, 4)
            flag = pool.value_load(unsorted[0:1, 0:1], min_val=0, max_val=P)
            with pool.If(flag > 0):
                pool.sem_inc(so_free, 1)
                for moves in (False, True):
                    n, loads, scatters = (TILES, 4, 2) if moves else (0, 2, 1)
                    with pool.Fori(0, TILES // 2) as i:
                        pool.wait_ge(so_in, i * (16 * loads) + 16 * (n + loads))
                        hold(pool, "pool")
                        for k in range(2):
                            pool.indirect_dma_start(base_i, None, place,
                                                    bass.IndirectOffsetOnAxis(ap=node_i[k], axis=0)).then_inc(so_place, 16)
                            pool.wait_ge(so_ready, i * 2 + (n + k + 1))
                            hold(pool, "pool")
                            pool.indirect_dma_start(place, bass.IndirectOffsetOnAxis(ap=last_i, axis=0), next_i, None,
                                                    bounds_check=N - 1, oob_is_err=False).then_inc(so_sc, 16)
                            if moves:
                                pool.indirect_dma_start(edges_s, bass.IndirectOffsetOnAxis(ap=pos_i, axis=0),
                                                        edge[:, k, :], None).then_inc(so_sc, 16)
                            pool.wait_ge(so_sc, i * (32 * scatters) + 16 * (n + (k + 1) * scatters))
                            pool.sem_inc(so_free, 1)

            for s in range(2):
                pool.wait_ge(p_out[s], 16 * (NGP + 1))
            with pool.Fori(0, L) as layer:
                with pool.Fori(0, NPAIR) as i:
                    for s in range(2):
                        g = pool.snap(layer * NCH + i * 2 + s)
                        u = pool.snap(layer * NPAIR + i)
                        pool.wait_ge(idx_in[s], (u + 1) * 16)
                        pool.wait_ge(z_done, g + 1)
                        hold(pool, "pool")
                        for k in range(T):
                            pool.indirect_dma_start(xg[s][:, k, :], None, xtab,
                                                    bass.IndirectOffsetOnAxis(ap=idx[s][:, k:k + 1], axis=0)).then_inc(gathered[s], 16)
                for s in range(2):
                    pool.wait_ge(stored[s], layer * (16 * NPAIR) + 16 * (NPAIR + 1))
                pool.wait_ge(const_out, 32)
                hold(pool, "pool")
                pool.indirect_dma_start(headnd[:, :], None, ndrows,
                                        bass.IndirectOffsetOnAxis(ap=hidx[:, :], axis=0)).then_inc(head_in, 16)
                pool.wait_ge(br_dve, layer * BRK + BRK)
                hold(pool, "pool")
                pool.indirect_dma_start(ndrows, bass.IndirectOffsetOnAxis(ap=hidx[:, :], axis=0),
                                        fixed[:, :], None).then_inc(head_out, 16)
                pool.wait_ge(head_out, layer * 16 + 16)
                hold(pool, "pool")
                for j in range(NG):
                    pool.wait_ge(h0_done, layer * NG + (j + 1))
                    hold(pool, "pool")
                    for k in range(G):
                        pool.indirect_dma_start(nd[j % 2][:, k, :], None, ndrows,
                                                bass.IndirectOffsetOnAxis(ap=endix[:, j * G + k:j * G + k + 1], axis=0)).then_inc(nd_in[j % 2], 16)
                for s in range(2):
                    pool.wait_ge(xnew_out[s], layer * (16 * NGP) + 16 * (NGP + 1))

            pool.wait_ge(qzero, 16 * NCH)
            for j in range(NG):
                pool.wait_ge(q_kc, j + 1 + C)
                for k in range(G):
                    pool.indirect_dma_start(qstart, bass.IndirectOffsetOnAxis(ap=startix[:, j * G + k:j * G + k + 1], axis=0),
                                            kvq[j % 2][:, k, 2 * D:3 * D], None,
                                            bounds_check=E - 1, oob_is_err=False).then_inc(q_sc[j % 2], 16)
                if j:
                    pool.wait_ge(q_sc[(j - 1) % 2], ((j - 1) // 2 + 1) * NGATH)
                    pool.sem_inc(q_free, 1)
            for s in range(2):
                pool.wait_ge(q_out[s], NGP * 32 + 32)
            pool.indirect_dma_start(qhead[:, :], None, qtab,
                                    bass.IndirectOffsetOnAxis(ap=dsthead[:, :], axis=0)).then_inc(qhead_in, 16)
            with pool.Fori(0, NPAIR) as i:
                for s in range(2):
                    pool.wait_ge(idx_in[s], i * 16 + (16 + 16 * L * NPAIR))
                    pool.wait_ge(msg_done, i * 2 + s + 1)
                    hold(pool, "pool")
                    for k in range(T):
                        pool.indirect_dma_start(kvg[s][:, k, :], None, kvtab,
                                                bass.IndirectOffsetOnAxis(ap=idx[s][:, k:k + 1], axis=0)).then_inc(gathered[s], 16)
            for s in range(2):
                pool.wait_ge(ms_out[s], 16 * (NPAIR + 1))
            pool.indirect_dma_start(headnd[:, 0:D], None, msrows,
                                    bass.IndirectOffsetOnAxis(ap=hidx[:, :], axis=0)).then_inc(mhead_in, 16)
            pool.wait_ge(b_dve, 3)
            pool.indirect_dma_start(msrows, bass.IndirectOffsetOnAxis(ap=hidx[:, :], axis=0),
                                    fixed[:, 0:D], None).then_inc(mhead_out, 16)
            pool.wait_ge(mhead_out, 16)
            for j in range(NG):
                pool.wait_ge(o_done, j + 1)
                for k in range(G):
                    pool.indirect_dma_start(nd[j % 2][:, k, 0:D], None, msrows,
                                            bass.IndirectOffsetOnAxis(ap=endix[:, j * G + k:j * G + k + 1], axis=0)).then_inc(o_in[j % 2], 16)

        @block.scalar
        def _(act):
            for x in (l_done, flag_done, er_done, fr_done, e_done, f_done, rows_done, qv_done, q_kc, ro_done):
                act.sem_inc(x, C)
            for s in range(2):
                act.sem_inc(stored[s], 16)
                act.sem_inc(ms_out[s], 16)

            act.sem_inc(p_new, C)

            def root(q):
                act.wait_ge(p_ln, q * LNK + 5)
                act.activation(std2[:, :], ss2[:, :], ACT.Sqrt, bias=epscol[0:NP, :], scale=1.0 / D).then_inc(p_std, 1)

            def turned(q, s):
                act.wait_ge(p_hT, q + 1 + C)
                act.activation(hT[s].rearrange("p (g c) -> p g c", c=P)[0:D, :, 0:NP], psT[:, :, 0:NP], ACT.Copy).then_inc(p_hc, 1)

            def encoded(q, u, s):
                act.wait_ge(p_x, q + 1)
                act.wait_ge(p_out[s], u * 16 + 16)
                hold(act, "act")
                act.activation(xnew[s], psX, ACT.Copy).then_inc(p_new, 1)

            root(0)
            turned(0, 0)
            root(1)
            with act.Fori(0, NGP - 1) as i:
                for s in range(2):
                    q = act.snap(i * 2 + s)
                    turned(q + 1, 1 - s)
                    root(q + 2)
                    encoded(q, i, s)
            turned(NG - 1, 1)
            for s in range(2):
                encoded(NG - 2 + s, NGP - 1, s)

            def flags_and_logits(c, g, s, layer):
                act.wait_ge(s_done, g + C)
                act.activation(flagx[:, :, 1:T + 1],
                               start_f[:, bass.ds(c * T + 1, T)].unsqueeze(1).to_broadcast([P, D, T]),
                               ACT.Copy, scale=-BIG).then_inc(flag_done, 1)
                act.wait_ge(m_done, g + 1 + C)
                act.wait_ge(cs_done, g + C)
                hold(act, "act")
                act.activation(lbuf[:, :, 1:T + 1], mbuf[s][:, :, :], ACT.Copy, scale=tcol[:, bass.ds(layer, 1)]).then_inc(l_done, 1)

            def exponentials(g):
                act.wait_ge(w_done, g + 1 + C)
                act.wait_ge(cn_done, g + C)
                act.activation(ebuf[:, :, 1:W], wbuf[:, :, :], ACT.Relu, scale=-1.0).then_inc(er_done, 1)
                act.wait_ge(er_done, g + 1 + C)
                act.activation(ebuf[:, :, 1:W], ebuf[:, :, 1:W], ACT.Exp, scale=-1.0).then_inc(e_done, 1)
                act.activation(fbuf[:, :, 1:W], wbuf[:, :, :], ACT.Relu).then_inc(fr_done, 1)
                act.wait_ge(fr_done, g + 1 + C)
                act.activation(fbuf[:, :, 1:W], fbuf[:, :, 1:W], ACT.Exp, scale=-1.0).then_inc(f_done, 1)

            def store_rows(c, g, u, s):
                act.wait_ge(d_done, g + 1 + C)
                act.wait_ge(stored[s], u * 16 + 16)
                act.activation(rows[s][:, :, D:2 * D].rearrange("p t c -> p c t"), dscan[:, :, 1:W], ACT.Copy)
                act.wait_ge(n_done, g + 1 + C)
                act.activation(rows[s][:, :, 0:D].rearrange("p t c -> p c t"), nscan[:, :, 1:W], ACT.Copy).then_inc(rows_done, 1)
                act.wait_ge(rows_done, g + 1 + C)
                act.dma_start(nd_v[:, bass.ds(c * T, T), :], rows[s][:, :, :]).then_inc(stored[s], 16)

            with act.Fori(0, L) as layer:
                g0 = act.snap(layer * NCH)
                u0 = act.snap(layer * NPAIR)
                act.wait_ge(reset_done, layer + 1)
                flags_and_logits(0, g0, 0, layer)
                exponentials(g0)
                with act.Fori(0, NPAIR - 1) as i:
                    for s in range(2):
                        c = act.snap(i * 2 + s)
                        g = act.snap(g0 + c)
                        flags_and_logits(c + 1, g + 1, 1 - s, layer)
                        store_rows(c, g, u0 + i, s)
                        exponentials(g + 1)
                store_rows(NCH - 2, g0 + (NCH - 2), u0 + (NPAIR - 1), 0)
                flags_and_logits(NCH - 1, g0 + (NCH - 1), 1, layer)
                exponentials(g0 + (NCH - 1))
                store_rows(NCH - 1, g0 + (NCH - 1), u0 + (NPAIR - 1), 1)
                act.activation(tailr[:, :, :], smax[:, :, T].unsqueeze(1).to_broadcast([P, 2, D]), ACT.Copy).then_inc(tail_done, 1)
                act.wait_ge(br_dve, layer * BRK + 4)
                act.activation(g12[:, :, :], g12[:, :, :], ACT.Exp).then_inc(br_act, 1)
                act.wait_ge(br_dve, layer * BRK + 10)
                act.activation(ab[:, :, :], ab[:, :, :], ACT.Exp).then_inc(br_act, 1)

                def transposed(q):
                    act.wait_ge(h0T_done, q + 1)
                    act.activation(h0T[0:D, :].rearrange("p (g c) -> p g c", c=P)[:, :, 0:NP], psT[:, :, 0:NP], ACT.Copy).then_inc(h0c_done, 1)

                def squares(q):
                    act.wait_ge(hw1_done, q + 1)
                    act.activation(sqb, psH, ACT.Square).then_inc(sq_done, 1)
                    act.wait_ge(ss_done, q + 1)
                    act.activation(std[:, :], ss[:, :], ACT.Sqrt, bias=epscol[0:NP, :], scale=1.0 / (2 * D)).then_inc(std_done, 1)

                def normed():
                    for k in range(G):
                        ins = act.activation(hn[:, k, :], psH[:, k, :], ACT.Copy, scale=rstd[:, k:k + 1])
                    ins.then_inc(hn_done, 1)

                def hidden(q):
                    act.wait_ge(hnT_done, q + 1)
                    hold(act, "act")
                    act.activation(hrT.rearrange("p (g c) -> p g c", c=P)[:, :, 0:NP], psN[:, :, 0:NP], ACT.Relu,
                                   bias=lnb[:, bass.ds(layer, 1)], scale=lng[:, bass.ds(layer, 1)]).then_inc(hr_done, 1)

                def residual_squares(j, q):
                    act.wait_ge(xadd_done, q + 1 + C)
                    hold(act, "act")
                    act.activation(lnsq, x3[:, bass.ds(j * G, G), :], ACT.Square).then_inc(sq2_done, 1)

                def residual_std(q):
                    act.wait_ge(ss2_done, q + 1)
                    act.activation(std2[:, :], ss2[:, :], ACT.Sqrt, bias=epscol[0:NP, :], scale=1.0 / D).then_inc(std2_done, 1)

                q0 = act.snap(layer * NG)
                transposed(q0)
                squares(q0)
                transposed(q0 + 1)
                act.wait_ge(rstd_done, q0 + 1)
                normed()
                hidden(q0)
                with act.Fori(1, NG - 1) as j:
                    q = act.snap(q0 + j)
                    squares(q)
                    transposed(q + 1)
                    act.wait_ge(rstd_done, q + 1)
                    normed()
                    residual_squares(j - 1, q - 1)
                    hidden(q)
                    residual_std(q - 1)
                squares(q0 + (NG - 1))
                act.wait_ge(rstd_done, q0 + NG)
                normed()
                residual_squares(NG - 2, q0 + (NG - 2))
                hidden(q0 + (NG - 1))
                residual_std(q0 + (NG - 2))
                residual_squares(NG - 1, q0 + (NG - 1))
                residual_std(q0 + (NG - 1))

            for s in range(2):
                act.sem_inc(q_out[s], 32)

            def x_T(q):
                act.wait_ge(q_hT, q + 1)
                act.activation(h0T[0:D, :].rearrange("p (g c) -> p g c", c=P)[:, :, 0:NP], psT[:, :, 0:NP], ACT.Copy).then_inc(q_hc, 1)

            def x1_std(q):
                act.wait_ge(q_ln, q * LNK + 5)
                act.activation(std2[:, :], ss2[:, :], ACT.Sqrt, bias=epscol[0:NP, :], scale=1.0 / D).then_inc(q_std, 1)

            def h_T(q):
                act.wait_ge(q_h2T, q + 1 + C)
                act.activation(hrT[0:D, :].rearrange("p (g c) -> p g c", c=P)[:, :, 0:NP], psT[:, :, 0:NP], ACT.Copy).then_inc(q_h2c, 1)

            def store_kvq(q, u, s):
                act.wait_ge(q_kvq, q + 1)
                act.wait_ge(q_out[s], u * 32 + 32)
                act.wait_ge(q_free, q + 1)
                hold(act, "act")
                act.activation(kvq[s], psK[:, :, 0:3 * D], ACT.Copy).then_inc(q_kc, 1)
                act.wait_ge(q_kc, q + 1 + C)
                act.dma_start(kvtab_v[:, bass.ds(q * G, G), :], kvq[s][:, :, 0:2 * D]).then_inc(q_out[s], 16)
                act.dma_start(qtab_v[:, bass.ds(q * G, G), :], kvq[s][:, :, 2 * D:3 * D]).then_inc(q_out[s], 16)

            x_T(0)
            x_T(1)
            x1_std(0)
            h_T(0)
            x1_std(1)
            with act.Fori(0, NGP - 1) as i:
                for s in range(2):
                    q = act.snap(i * 2 + s)
                    x_T(q + 2)
                    store_kvq(q, i, s)
                    h_T(q + 1)
                    x1_std(q + 2)
            store_kvq(NG - 2, NGP - 1, 0)
            h_T(NG - 1)
            store_kvq(NG - 1, NGP - 1, 1)

            act.wait_ge(a_reset, 1)
            with act.Fori(0, NPAIR) as i:
                for s in range(2):
                    c = act.snap(i * 2 + s)
                    act.wait_ge(ssc_done, c + C)
                    act.activation(keepx[:, :, 1:W], start_f[:, bass.ds(c * T, T)].unsqueeze(1).to_broadcast([P, D, T]),
                                   ACT.Copy, bias=1.0, scale=-1.0).then_inc(keep_done, 1)
                    act.wait_ge(qs_in[s], i * 16 + 16)
                    act.wait_ge(qsc_done, c + C)
                    act.activation(ebuf[:, :, 1:W], qs[s].rearrange("p t c -> p c t"), ACT.Copy).then_inc(qv_done, 1)
                    act.wait_ge(c2_done, c + 1)
                    act.activation(score[:, :, :], score[:, :, :], ACT.Exp).then_inc(ex_done, 1)
                    act.wait_ge(ssc_done, c + 1 + C)
                    act.wait_ge(ms_out[s], i * 16 + 16)
                    act.activation(msout[s].rearrange("p t c -> p c t"), nscan[:, :, 1:W], ACT.Copy).then_inc(ro_done, 1)
                    act.wait_ge(ro_done, c + 1 + C)
                    act.dma_start(ms_v[:, bass.ds(c * T, T), :], msout[s]).then_inc(ms_out[s], 16)

        @block.tensor
        def _(pe):
            pe.sem_inc(ea_done, C)
            pe.sem_inc(p_hT, C)

            def transposes(out, rows_, last):
                hold(pe, "pe")
                for k in range(G):
                    ins = pe.transpose(out[:, k, 0:NP], rows_[:, k, :], ident[0:NP, 0:NP])
                ins.then_inc(last, 1)

            pe.wait_ge(dve_pro, 3)
            pe.matmul(psOrd, col[1], col[1], start=True, stop=True).then_inc(ordered, 1)
            pe.wait_ge(pool_pro, 6)
            pe.wait_ge(dve_pro, 4)
            flag = pe.value_load(unsorted[0:1, 0:1], min_val=0, max_val=P)
            with pe.If(flag > 0):
                pe.wait_ge(so_scan, 1)
                pe.matmul(psOff, tri[0:NP, 0:NP], place_f[:, NJ - 1:NJ], start=True, stop=True).then_inc(so_off, 1)
                with pe.Fori(0, NCH) as c:
                    pe.wait_ge(so_rows, c * 16 + 16)
                    hold(pe, "pe")
                    for k in range(T):
                        ins = pe.transpose(psS[:, k * P:(k + 1) * P], sorted_rows[:, k, 0:D], ident[:, :])
                    ins.then_inc(so_T, 1)
            pe.wait_ge(w_in, 16 * (NW + 5))
            def input_T(q):
                pe.wait_ge(p_h, q + 1)
                transposes(psT, h0, p_hT)

            def times_enc(q, s):
                pe.wait_ge(p_new, q + C)
                hold(pe, "pe")
                for k in range(G):
                    ins = pe.matmul(psX[:, k, :], hT[s][:, k * P:k * P + NP], encw[:, :], start=True, stop=True)
                ins.then_inc(p_x, 1)

            input_T(0)
            with pe.Fori(0, NGP - 1) as i:
                for s in range(2):
                    q = pe.snap(i * 2 + s)
                    pe.wait_ge(p_hc, q + 1)
                    hold(pe, "pe")
                    input_T(q + 1)
                    times_enc(q, s)
            pe.wait_ge(p_hc, NG - 1)
            input_T(NG - 1)
            times_enc(NG - 2, 0)
            pe.wait_ge(p_hc, NG)
            times_enc(NG - 1, 1)
            pe.wait_ge(p_new, NG + C)
            pe.wait_ge(dve_pro, 5)
            pe.matmul(psA, wbc, ident[:, :], start=True, stop=True).then_inc(passT, 1)

            def edge_terms(g, u, s, weight):
                pe.wait_ge(attr_in[s], u * 16 + 16)
                pe.wait_ge(z_done, g + 1)
                for k in range(T):
                    ins = pe.matmul(ea[s][:, k, :], attr[s][:, k * P:(k + 1) * P], weight[:, :], start=True, stop=True)
                ins.then_inc(ea_done, 1)

            with pe.Fori(0, L) as layer:
                with pe.Fori(0, NPAIR) as i:
                    for s in range(2):
                        c = pe.snap(i * 2 + s)
                        with pe.If(layer < 1):
                            pe.wait_ge(counted, c + C)
                            hold(pe, "pe")
                        edge_terms(pe.snap(layer * NCH + c), pe.snap(layer * NPAIR + i), s, eew)
                        with pe.If(layer < 1):
                            pe.wait_ge(onehots, c + 1)
                            hold(pe, "pe")
                            for k in range(T):
                                ins = pe.matmul(psHist, oh_hi[:, k, :], oh_lo[:, k, :], start=k == 0, stop=k == T - 1)
                            ins.then_inc(hist, 1)
                with pe.If(layer < 1):
                    pe.wait_ge(tables, 1)
                    pe.matmul(psOff, tri[0:NP, 0:NP], cum[:, NJ - 1:NJ], start=True, stop=True).then_inc(offs, 1)
                pe.wait_ge(tail_done, layer + 1)
                pe.wait_ge(cn_done, layer * NCH + NCH + C)
                pe.transpose(psA, tailr[:, :, :].rearrange("p a c -> p (a c)"), ident[:, :])
                pe.transpose(psB, rows[1][:, T - 1, :], ident[:, :]).then_inc(br_pe, 1)
                pe.wait_ge(br_dve, layer * BRK + 6)
                pe.transpose(psA2, rsc[:, 0:P], ident[:, :])
                pe.transpose(psB2, xsc[:, 0:P], ident[:, :]).then_inc(br_pe, 1)
                def sums_T(q):
                    pe.wait_ge(h0_done, q + 1 + C)
                    transposes(psT, h0, h0T_done)

                def times_w1(q):
                    pe.wait_ge(h0c_done, q + 1)
                    for k in range(G):
                        ins = pe.matmul(psH[:, k, :], h0T[:, k * P:k * P + NP], w1[:, bass.ds(layer * (2 * D), 2 * D)], start=True, stop=True)
                    ins.then_inc(hw1_done, 1)

                def hidden_T(q):
                    pe.wait_ge(hn_done, q + 1)
                    transposes(psN, hn, hnT_done)

                def times_w2(q):
                    pe.wait_ge(hr_done, q + 1)
                    pe.wait_ge(xadd_done, q + C)
                    hold(pe, "pe")
                    for k in range(G):
                        ins = pe.matmul(psX[:, k, :], hrT[:, k * P:k * P + NP], w2[:, bass.ds(layer * D, D)], start=True, stop=True)
                    ins.then_inc(hw2_done, 1)

                q0 = pe.snap(layer * NG)
                sums_T(q0)
                times_w1(q0)
                sums_T(q0 + 1)
                hidden_T(q0)
                with pe.Fori(1, NG - 1) as j:
                    q = pe.snap(q0 + j)
                    times_w1(q)
                    sums_T(q + 1)
                    times_w2(q - 1)
                    hidden_T(q)
                times_w1(q0 + (NG - 1))
                times_w2(q0 + (NG - 2))
                hidden_T(q0 + (NG - 1))
                times_w2(q0 + (NG - 1))
                pe.wait_ge(xadd_done, layer * NG + NG + C)

            pe.sem_inc(q_h2T, C)

            def x_T(u, s):
                pe.wait_ge(q_in[s], u * 32 + 32)
                transposes(psT, xold[s], q_hT)

            def times_lin(q):
                pe.wait_ge(q_hc, q + 1)
                pe.wait_ge(q_x1, q + C)
                hold(pe, "pe")
                for k in range(G):
                    ins = pe.matmul(psX[:, k, :], h0T[:, k * P:k * P + NP], linw[:, :], start=True, stop=True)
                ins.then_inc(q_lin, 1)

            def h_T(q, taken):
                pe.wait_ge(q_h, q + 1)
                pe.wait_ge(q_hc, taken)
                transposes(psT, h0, q_h2T)

            def times_kvq(q):
                pe.wait_ge(q_h2c, q + 1)
                pe.wait_ge(q_kc, q + C)
                hold(pe, "pe")
                for k in range(G):
                    ins = pe.matmul(psK[:, k, 0:3 * D], hrT[0:D + 1, k * P:k * P + NP], kvqw[:, :], start=True, stop=True)
                ins.then_inc(q_kvq, 1)

            x_T(0, 0)
            times_lin(0)
            x_T(0, 1)
            h_T(0, 2)
            times_lin(1)
            with pe.Fori(0, NGP - 1) as i:
                for s in range(2):
                    q = pe.snap(i * 2 + s)
                    pe.wait_ge(q_h2c, q + 1)
                    hold(pe, "pe")
                    x_T(i + 1, s)
                    times_kvq(q)
                    h_T(q + 1, q + 3)
                    times_lin(q + 2)
            times_kvq(NG - 2)
            h_T(NG - 1, NG)
            times_kvq(NG - 1)
            pe.wait_ge(q_kc, NG + C)
            with pe.Fori(0, NPAIR) as i:
                for s in range(2):
                    edge_terms(pe.snap(i * 2 + (s + L * NCH)), pe.snap(i + L * NPAIR), s, wew)
            pe.wait_ge(ro_done, NCH + C)
            pe.transpose(psA[0:D, :], msout[1][:, T - 1, :], ident[:, :]).then_inc(b_pe, 1)
            pe.wait_ge(b_dve, 1)
            pe.transpose(psB2[:, 0:D], xsc[0:D, 0:P], ident[0:D, 0:D]).then_inc(b_pe, 1)

        @block.vector
        def _(v):
            for x in (z_done, m_done, s_done, w_done, cs_done, me_done, d_done, n_done, cd_done, cn_done,
                      h0_done, xadd_done, q_x1, counted, msg_done, qsc_done, ssc_done, o_done):
                v.sem_inc(x, C)
            for s in range(2):
                v.sem_inc(xnew_out[s], 16)
                v.sem_inc(o_out[s], 16)
                v.sem_inc(p_out[s], 16)
            chain = sem("dve_chain")
            count = [0, 0]

            def link(ins):
                count[0] += 1
                ins.then_inc(chain, 1)
                v.wait_ge(chain, count[0])

            def signal(ins):
                count[1] += 1
                ins.then_inc(dve_pro, 1)
                v.wait_ge(dve_pro, count[1])

            signal(v.memset(dprev, -1))
            v.memset(zeros[:, :], 0.0)
            v.memset(nrow[:, 0:D], 0.0)
            signal(v.memset(nrow[:, D:2 * D], 1.0))
            for s in range(2):
                v.memset(hT[s][D:D + 1, :], 1.0)
            v.memset(rsc[:, 0:1], -BIG)
            v.memset(xsc[:, 0:1], 0.0)
            link(v.memset(epscol[:, :], LN_EPS))

            v.wait_ge(dst_in, 32)
            link(v.tensor_copy(dst_f, dst_i))
            link(v.tensor_copy(col[0], dprev))
            v.tensor_tensor(ne_f[:, 1:EP], dst_f[:, 0:EP - 1], dst_f[:, 1:EP], ALU.is_gt)
            link(v.tensor_tensor(ne_f[:, 0:1], col[0], dst_f[:, 0:1], ALU.is_gt))
            signal(v.tensor_reduce(col[1], ne_f, AX.X, ALU.max))
            v.wait_ge(ordered, 1)
            signal(v.tensor_copy(unsorted[:, :], psOrd))
            flag = v.value_load(unsorted[0:1, 0:1], min_val=0, max_val=P)

            with v.If(flag > 0):
                v.wait_ge(pool_pro, 6)
                for moves in (False, True):
                    with v.Fori(0, TILES // 2) as i:
                        v.wait_ge(so_in, i * 64 + (16 * TILES + 64) if moves else i * 32 + 32)
                        hold(v, "dve")
                        for k in range(2):
                            n = v.snap(i * 2 + ((TILES if moves else 0) + k))
                            step = [0]

                            def place_step(ins):
                                step[0] += 1
                                ins.then_inc(so_steps, 1)
                                v.wait_ge(so_steps, n * SOK + step[0])
                                hold(v, "dve")

                            v.tensor_copy(row_f, row_i[:, k, :])
                            place_step(v.tensor_copy(node_f, node_i[k]))
                            place_step(v.tensor_scalar(same, row_f, node_f, None, ALU.is_equal))
                            v.tensor_reduce(total, same, AX.X, ALU.add)
                            place_step(v.tensor_tensor(after, same, tri[:, :], ALU.mult))
                            place_step(v.tensor_reduce(later, after, AX.X, ALU.add))
                            v.wait_ge(so_place, n * 16 + 16)
                            hold(v, "dve")
                            place_step(v.tensor_copy(base_f, base_i))
                            place_step(v.tensor_tensor(next_f, base_f, total, ALU.add))
                            v.tensor_scalar(skip_f, later, 1.0, float(1 << 20), ALU.min, ALU.mult)
                            place_step(v.tensor_tensor(pos_f, next_f, later, ALU.subtract))
                            v.tensor_tensor(last_f, skip_f, node_f, ALU.add)
                            place_step(v.tensor_scalar(pos_f, pos_f, -1.0, None, ALU.add))
                            v.wait_ge(so_free, n + 1)
                            hold(v, "dve")
                            v.tensor_copy(next_i, next_f)
                            v.tensor_copy(last_i, last_f)
                            place_step(v.tensor_copy(pos_i, pos_f))
                            v.sem_inc(so_ready, 1)
                            assert step[0] == SOK
                    if not moves:
                        v.wait_ge(so_back, 16)
                        v.tensor_copy(place_c, place_i).then_inc(so_new, 1)
                        v.wait_ge(so_new, 1)
                        v.tensor_tensor_scan(place_f, place_c, place_c, 0.0, ALU.add, ALU.max).then_inc(so_scan, 1)
                        v.wait_ge(so_scan, 1)
                        v.tensor_tensor(place_c, place_f, place_c, ALU.subtract).then_inc(so_new, 1)
                        v.wait_ge(so_new, 2)
                        v.wait_ge(so_off, 1)
                        v.tensor_copy(place_o[:, 0:1], psOff).then_inc(so_scan, 1)
                        v.wait_ge(so_scan, 2)
                        v.tensor_scalar(place_i, place_c, place_o[:, 0:1], None, ALU.add).then_inc(so_new, 1)
                        v.wait_ge(so_new, 3)
                with v.Fori(0, NCH) as c:
                    v.wait_ge(so_T, c + 1)
                    hold(v, "dve")
                    v.tensor_copy(attr[0][0:D, :], psS)
                    v.tensor_copy(idx[0][:, :], sorted_rows[:, :, D].bitcast(I32))
                    v.tensor_copy(idx[1][:, :], sorted_rows[:, :, D + 1].bitcast(I32)).then_inc(so_copied, 1)
                v.wait_ge(so_back, 48)
                hold(v, "dve")

            def layer_norm(x, q, steps, std_sem):
                hold(v, "dve")
                v.tensor_reduce(mu[:, :], x, AX.X, ALU.add).then_inc(steps, 1)
                v.wait_ge(steps, q * LNK + 1)
                v.tensor_scalar(mu[:, :], mu[:, :], 1.0 / D, None, ALU.mult).then_inc(steps, 1)
                v.wait_ge(steps, q * LNK + 2)
                v.tensor_tensor(lnx, x, mu[:, :].unsqueeze(2).to_broadcast([NP, G, D]), ALU.subtract).then_inc(steps, 1)
                v.wait_ge(steps, q * LNK + 3)
                v.tensor_tensor(lnsq, lnx, lnx, ALU.mult).then_inc(steps, 1)
                v.wait_ge(steps, q * LNK + 4)
                v.tensor_reduce(ss2[:, :], lnsq, AX.X, ALU.add).then_inc(steps, 1)
                v.wait_ge(std_sem, q + 1)
                v.reciprocal(rstd2[:, :], std2[:, :]).then_inc(steps, 1)
                v.wait_ge(steps, q * LNK + 6)
                v.tensor_tensor(lnx, lnx, rstd2[:, :].unsqueeze(2).to_broadcast([NP, G, D]), ALU.mult).then_inc(steps, 1)
                v.wait_ge(steps, q * LNK + 7)

            v.wait_ge(x_in, 16)
            with v.Fori(0, NG) as q:
                layer_norm(x3[:, bass.ds(q * G, G), :], q, p_ln, p_std)
                v.wait_ge(p_hT, q + C)
                v.tensor_scalar(h0, lnx, 0.0, None, ALU.max).then_inc(p_h, 1)
                v.wait_ge(p_h, q + 1)
            for s in range(2):
                v.memset(attr[s][D:D + 1, :], 1.0)
            v.memset(counts[:, :], 0.0)

            v.wait_ge(pool_pro, 6)
            link(v.tensor_copy(dst_f, dst_i))
            v.tensor_copy(dsthead[:, :], dst_i[:, 0:1])
            link(v.tensor_copy(col[0], dprev))
            v.tensor_tensor(start_f[:, 1:EP], dst_f[:, 1:EP], dst_f[:, 0:EP - 1], ALU.not_equal)
            v.memset(start_f[:, EP:EP + 1], 0.0)
            v.tensor_tensor(start_f[:, 0:1], dst_f[:, 0:1], col[0], ALU.not_equal)
            v.tensor_tensor(cont[:, :], dst_f[:, 0:1], col[0], ALU.is_equal)
            link(v.tensor_scalar(ne_f, dst_f, dst_f[:, 0:1], None, ALU.not_equal))
            v.tensor_scalar(headneg[:, :], ne_f, -BIG, None, ALU.mult)
            v.tensor_scalar(contneg[:, :], cont[:, :], -1.0, BIG, ALU.add, ALU.mult)
            v.tensor_copy(col[1], pcol_i)
            link(v.tensor_reduce(col[2], ne_f, AX.X, ALU.add))
            link(v.tensor_tensor(col[3], col[1], col[2], ALU.subtract))
            v.tensor_copy(hidx[:, :], col[3])
            link(v.tensor_scalar(col[4], col[2], 0.0, None, ALU.is_equal))
            link(v.tensor_tensor(col[5], col[4], cont[:, :], ALU.mult))
            signal(v.tensor_copy(wbc, col[5].to_broadcast([P, P])))
            v.wait_ge(passT, 1)
            link(v.tensor_copy(passkeep[:, :], psA))
            link(v.tensor_scalar(passneg[:, :], passkeep[:, :], -1.0, BIG, ALU.add, ALU.mult))

            v.tensor_copy(iota_b, iota_i)
            link(v.tensor_scalar(tmp_i, dst_i, 7, None, ALU.logical_shift_right))
            link(v.tensor_copy(hi_b, tmp_i))
            link(v.tensor_scalar(tmp_i, dst_i, HB - 1, None, ALU.bitwise_and))
            link(v.tensor_copy(lo_b, tmp_i))

            def one_hots(c):
                v.tensor_tensor(oh_hi, hi_b[:, bass.ds(c * T, T)].unsqueeze(2).to_broadcast([P, T, HR]),
                                iota_b[:, 0:HR].unsqueeze(1).to_broadcast([P, T, HR]), ALU.is_equal)
                v.tensor_tensor(oh_lo, lo_b[:, bass.ds(c * T, T)].unsqueeze(2).to_broadcast([P, T, HB]),
                                iota_b.unsqueeze(1).to_broadcast([P, T, HB]), ALU.is_equal).then_inc(onehots, 1)

            def add_counts(c):
                v.wait_ge(counted, c + C)
                v.wait_ge(hist, c + 1)
                v.tensor_tensor(counts[:, :], counts[:, :], psHist, ALU.add).then_inc(counted, 1)

            for c in range(2):
                one_hots(c)
                add_counts(c)

            v.wait_ge(w_in, 16 * (NW + 5))
            for weight, mean, k, n in ((w1, w1m, D + 1, 2 * D), (w2, w2m, 2 * D, D), (b2, b2m, NP, D)):
                wv = weight[:, :].rearrange("k (l n) -> k l n", l=L)
                link(v.tensor_reduce(mean[:, :], wv, AX.X, ALU.add))
                link(v.tensor_scalar(mean[:, :], mean[:, :], 1.0 / n, None, ALU.mult))
                link(v.tensor_tensor(wv, wv, mean[:, :].unsqueeze(2).to_broadcast([k, L, n]), ALU.subtract))
            v.wait_ge(const_out, 32)
            for s in range(2):
                v.wait_ge(p_out[s], 16 * (NGP + 1))
            v.memset(lbuf[:, :, T + 1:WM], -BIG)
            v.memset(flagx[:, :, 0:1], 0.0)
            v.memset(flagx[:, :, T + 1:WM], -BIG)
            link(v.memset(fbuf[:, :, 0:1], 0.0))

            def node_tables():
                steps = [0]

                def table(ins):
                    steps[0] += 1
                    ins.then_inc(tables, 1)
                    v.wait_ge(tables, steps[0])

                v.wait_ge(cnt_in, 16)
                table(v.tensor_tensor_scan(cum, cnt, cnt, 0.0, ALU.add, ALU.max))
                v.tensor_scalar(has, cnt, 0.0, None, ALU.is_gt)
                v.wait_ge(offs, 1)
                table(v.tensor_copy(off, psOff))
                table(v.tensor_scalar(cum, cum, off, None, ALU.add))
                table(v.tensor_tensor(spos, cum, cnt, ALU.subtract))
                for pos, before in ((epos, 1.0), (spos, 0.0)):
                    table(v.tensor_scalar(pos, cum if before else spos, -before - E, None, ALU.add))
                    table(v.tensor_tensor(pos, pos, has, ALU.mult))
                    table(v.tensor_scalar(pos, pos, float(E), None, ALU.add))
                v.tensor_copy(endix[:, :], epos)
                table(v.tensor_copy(startix[:, :], spos))
                table(v.tensor_copy(x3, b2[:, 0:D].unsqueeze(1).to_broadcast([NP, NJ, D])))

            def message(c, g, u, s):
                v.wait_ge(gathered[s], u * GATH + GATH)
                v.wait_ge(ea_done, g + 1 + C)
                v.wait_ge(cs_done, g + C)
                v.tensor_tensor(zbuf[:, :, :], ea[s].rearrange("p t c -> p c t"), xg[s].rearrange("p t c -> p c t"),
                                ALU.add).then_inc(z_done, 1)
                v.wait_ge(z_done, g + 1 + C)
                v.tensor_scalar(mbuf[s][:, :, :], zbuf[:, :, :], 0.0, EPS, ALU.max, ALU.add).then_inc(m_done, 1)

            def maximum(c, g, s):
                v.wait_ge(l_done, g + 1 + C)
                v.wait_ge(cs_done, g + C)
                v.tensor_tensor_scan(flat(smax), flat(lbuf), flat(flagx), -BIG, ALU.max, ALU.add).then_inc(s_done, 1)
                v.wait_ge(s_done, g + 1 + C)
                v.wait_ge(f_done, g + C)
                v.tensor_tensor(wbuf[:, :, :], lbuf[:, :, 1:T + 1], smax[:, :, 0:T], ALU.subtract).then_inc(w_done, 1)
                v.tensor_tensor(zbuf[:, :, :], lbuf[:, :, 1:T + 1],
                                headneg[:, bass.ds(c * T, T)].unsqueeze(1).to_broadcast([P, D, T]), ALU.add).then_inc(hadd_done, 1)
                v.wait_ge(hadd_done, g + 1)
                v.tensor_reduce(headr2[:, :], zbuf[:, :, :], AX.X, ALU.max).then_inc(hred_done, 1)
                v.wait_ge(hred_done, g + 1)
                v.tensor_tensor(headr[:, :], headr[:, :], headr2[:, :], ALU.max).then_inc(hmax_done, 1)
                v.wait_ge(hmax_done, g + 1)
                v.tensor_copy(lbuf[:, :, 0], smax[:, :, T]).then_inc(cs_done, 1)

            def sums(g, s):
                v.wait_ge(e_done, g + 1 + C)
                v.wait_ge(cn_done, g + C)
                v.tensor_tensor(mebuf[:, :, 1:W], mbuf[s][:, :, :], ebuf[:, :, 1:W], ALU.mult).then_inc(me_done, 1)
                v.wait_ge(f_done, g + 1 + C)
                v.wait_ge(rows_done, g + C)
                v.tensor_tensor_scan(flat(dscan), flat(fbuf), flat(ebuf), 0.0, ALU.mult, ALU.add).then_inc(d_done, 1)
                v.wait_ge(me_done, g + 1 + C)
                v.tensor_tensor_scan(flat(nscan), flat(fbuf), flat(mebuf), 0.0, ALU.mult, ALU.add).then_inc(n_done, 1)
                v.wait_ge(d_done, g + 1 + C)
                v.tensor_copy(ebuf[:, :, 0], dscan[:, :, T]).then_inc(cd_done, 1)
                v.wait_ge(n_done, g + 1 + C)
                v.tensor_copy(mebuf[:, :, 0], nscan[:, :, T]).then_inc(cn_done, 1)

            with v.Fori(0, L) as layer:
                g0 = v.snap(layer * NCH)
                u0 = v.snap(layer * NPAIR)
                v.memset(lbuf[:, :, 0:1], -BIG)
                v.memset(ebuf[:, :, 0:1], 0.0)
                v.memset(mebuf[:, :, 0:1], 0.0)
                v.memset(headr[:, :], -BIG).then_inc(reset_done, 1)
                v.wait_ge(reset_done, layer + 1)
                message(0, g0, u0, 0)
                maximum(0, g0, 0)
                with v.Fori(0, NPAIR - 1) as i:
                    for s in range(2):
                        c = v.snap(i * 2 + s)
                        g = v.snap(g0 + c)
                        message(c + 1, g + 1, u0 + i + s, 1 - s)
                        with v.If(layer < 1):
                            one_hots(c + 2)
                        sums(g, s)
                        maximum(c + 1, g + 1, 1 - s)
                        with v.If(layer < 1):
                            add_counts(c + 2)
                with v.If(layer > 0):
                    v.tensor_tensor(x3, x3, b2[:, bass.ds(layer * D, D)].unsqueeze(1).to_broadcast([NP, NJ, D]), ALU.add)
                sums(g0 + (NCH - 2), 0)
                with v.If(layer < 1):
                    node_tables()
                message(NCH - 1, g0 + (NCH - 1), u0 + (NPAIR - 1), 1)
                maximum(NCH - 1, g0 + (NCH - 1), 1)
                sums(g0 + (NCH - 1), 1)

                step = [0]

                def bridge(ins):
                    step[0] += 1
                    ins.then_inc(br_dve, 1)
                    v.wait_ge(br_dve, layer * BRK + step[0])

                v.wait_ge(br_pe, layer * 2 + 1)
                bridge(v.tensor_tensor_scan(rsc[:, 1:P + 1], passneg[:, :], psA, -BIG, ALU.add, ALU.max))
                bridge(v.tensor_tensor(g12[:, 0, :], rsc[:, 0:P], passneg[:, :], ALU.add))
                bridge(v.tensor_tensor(g12[:, 0, :], g12[:, 0, :], rsc[:, 1:P + 1], ALU.subtract))
                bridge(v.tensor_tensor(g12[:, 1, :], psA, rsc[:, 1:P + 1], ALU.subtract))
                v.wait_ge(br_act, layer * 2 + 1)
                bridge(v.tensor_tensor(g12[:, 1, :], g12[:, 1, :], psB, ALU.mult))
                bridge(v.tensor_tensor_scan(xsc[:, 1:P + 1], g12[:, 0, :], g12[:, 1, :], 0.0, ALU.mult, ALU.add))
                v.wait_ge(br_pe, layer * 2 + 2)
                bridge(v.tensor_scalar(rcar[:, :], psA2[:, 0:D], contneg[:, :], None, ALU.add))
                bridge(v.tensor_tensor(headr2[:, :], rcar[:, :], headr[:, :], ALU.max))
                bridge(v.tensor_tensor(ab[:, 0, :], rcar[:, :], headr2[:, :], ALU.subtract))
                bridge(v.tensor_tensor(ab[:, 1, :], headr[:, :], headr2[:, :], ALU.subtract))
                v.wait_ge(br_act, layer * 2 + 2)
                nd2 = [t.rearrange("p (a c) -> p a c", a=2) for t in (fixed[:, :], psB2, headnd[:, :])]
                bridge(v.tensor_tensor(nd2[0], nd2[1], ab[:, 0, :].unsqueeze(1).to_broadcast([P, 2, D]), ALU.mult))
                v.wait_ge(head_in, layer * 16 + 16)
                bridge(v.tensor_tensor(nd2[2], nd2[2], ab[:, 1, :].unsqueeze(1).to_broadcast([P, 2, D]), ALU.mult))
                bridge(v.tensor_tensor(fixed[:, :], fixed[:, :], headnd[:, :], ALU.add))
                assert step[0] == BRK

                hold(v, "dve")
                q0 = v.snap(layer * NG)
                n0 = v.snap(layer * NGP)

                def reciprocals(u, s):
                    v.wait_ge(nd_in[s], u * NGATH + NGATH)
                    v.reciprocal(recd, nd[s][:, :, D:2 * D]).then_inc(rec_done, 1)

                def aggregates(q, u, s):
                    v.wait_ge(rec_done, q + 1)
                    v.tensor_tensor(recd, recd, nd[s][:, :, 0:D], ALU.mult).then_inc(agg_done, 1)
                    v.wait_ge(agg_done, q + 1)
                    v.wait_ge(xold_in[s], u * 16 + 16)
                    v.tensor_tensor(h0, recd, xold[s], ALU.add).then_inc(h0_done, 1)

                def deviation(q):
                    v.wait_ge(sq_done, q + 1)
                    v.tensor_reduce(ss[:, :], sqb, AX.X, ALU.add).then_inc(ss_done, 1)
                    v.wait_ge(std_done, q + 1)
                    v.reciprocal(rstd[:, :], std[:, :]).then_inc(rstd_done, 1)

                def residual(j, q):
                    grp = bass.ds(j * G, G)
                    v.wait_ge(hw2_done, q + 1)
                    hold(v, "dve")
                    v.tensor_tensor(x3[:, grp, :], x3[:, grp, :], psX, ALU.add).then_inc(xadd_done, 1)

                def norm(j, q, u, s):
                    v.wait_ge(sq2_done, q + 1)
                    v.tensor_reduce(ss2[:, :], lnsq, AX.X, ALU.add).then_inc(ss2_done, 1)
                    v.wait_ge(std2_done, q + 1)
                    v.reciprocal(rstd2[:, :], std2[:, :]).then_inc(rstd2_done, 1)
                    v.wait_ge(rstd2_done, q + 1)
                    hold(v, "dve")
                    v.tensor_tensor(lnx, x3[:, bass.ds(j * G, G), :], rstd2[:, :].unsqueeze(2).to_broadcast([NP, G, D]), ALU.mult).then_inc(aff_done, 1)
                    v.wait_ge(aff_done, q * 3 + 1)
                    v.tensor_tensor(lnx, lnx, ng[:, bass.ds(layer * D, D)].unsqueeze(1).to_broadcast([NP, G, D]), ALU.mult).then_inc(aff_done, 1)
                    v.wait_ge(aff_done, q * 3 + 2)
                    v.tensor_tensor(lnx, lnx, nb[:, bass.ds(layer * D, D)].unsqueeze(1).to_broadcast([NP, G, D]), ALU.add).then_inc(aff_done, 1)
                    v.wait_ge(aff_done, q * 3 + 3)
                    v.wait_ge(xnew_out[s], u * 16 + 16)
                    v.tensor_scalar(xnew[s], lnx, 0.0, None, ALU.max).then_inc(xnew_done, 1)

                reciprocals(n0, 0)
                aggregates(q0, n0, 0)
                v.wait_ge(h0T_done, q0 + 1)
                reciprocals(n0, 1)
                aggregates(q0 + 1, n0, 1)
                deviation(q0)
                v.wait_ge(h0T_done, q0 + 2)
                reciprocals(n0 + 1, 0)
                aggregates(q0 + 2, n0 + 1, 0)
                with v.Fori(0, NGP - 2) as i:
                    for n in range(2):
                        j = v.snap(i * 2 + (n + 1))
                        q = v.snap(q0 + j)
                        u = v.snap(n0 + i)
                        deviation(q)
                        v.wait_ge(h0T_done, q + 2)
                        reciprocals(u + 1 + n, 1 - n)
                        residual(j - 1, q - 1)
                        aggregates(q + 2, u + 1 + n, 1 - n)
                        norm(j - 1, q - 1, u, n)
                j = NG - 3
                deviation(q0 + j)
                v.wait_ge(h0T_done, q0 + (j + 2))
                reciprocals(n0 + (NGP - 1), 1)
                residual(j - 1, q0 + (j - 1))
                aggregates(q0 + (j + 2), n0 + (NGP - 1), 1)
                norm(j - 1, q0 + (j - 1), n0 + (NGP - 2), 0)
                for j in (NG - 2, NG - 1):
                    deviation(q0 + j)
                    residual(j - 1, q0 + (j - 1))
                    norm(j - 1, q0 + (j - 1), n0 + (j - 1) // 2, (j - 1) % 2)
                residual(NG - 1, q0 + (NG - 1))
                norm(NG - 1, q0 + (NG - 1), n0 + (NGP - 1), 1)
                v.wait_ge(xnew_done, q0 + NG)

            v.memset(hrT[D:D + 1, :], 1.0)
            with v.Fori(0, NGP) as i:
                for s in range(2):
                    q = v.snap(i * 2 + s)
                    grp = bass.ds(q * G, G)
                    v.wait_ge(q_lin, q + 1)
                    v.wait_ge(q_in[s], i * 32 + 32)
                    hold(v, "dve")
                    v.tensor_tensor(x3[:, grp, :], psX, xnew[s], ALU.add).then_inc(q_x1, 1)
                    v.wait_ge(q_x1, q + 1 + C)
                    layer_norm(x3[:, grp, :], q, q_ln, q_std)
                    v.wait_ge(q_h2T, q + C)
                    v.tensor_scalar(h0, lnx, 0.0, None, ALU.max).then_inc(q_h, 1)
                    v.wait_ge(q_h, q + 1)

            v.wait_ge(qhead_in, 16)
            v.wait_ge(q_kc, NG + C)
            v.memset(keepx[:, :, 0:1], 0.0)
            v.tensor_copy(ebuf[:, :, 0], qhead[:, :])
            v.memset(mebuf[:, :, 0:1], 0.0).then_inc(a_reset, 1)
            v.wait_ge(a_reset, 1)
            with v.Fori(0, NPAIR) as i:
                for s in range(2):
                    c = v.snap(i * 2 + s)
                    g = v.snap(c + L * NCH)
                    kg, vg = kvg[s][:, :, 0:D], kvg[s][:, :, D:2 * D]
                    v.wait_ge(gathered[s], i * GATH + (L * NPAIR + 1) * GATH)
                    v.wait_ge(ea_done, g + 1 + C)
                    v.tensor_tensor(zt, ea[s], kg, ALU.mult).then_inc(z_done, 1)
                    v.wait_ge(keep_done, c + 1)
                    v.wait_ge(qv_done, c + 1 + C)
                    v.tensor_tensor_scan(flat(dscan), flat(flagx)[:, 0:D * W], flat(ebuf), 0.0, ALU.mult, ALU.add).then_inc(qsc_done, 1)
                    v.wait_ge(qsc_done, c + 1 + C)
                    v.tensor_copy(ebuf[:, :, 0], dscan[:, :, T]).then_inc(qc_done, 1)
                    v.tensor_tensor(zt, zt, dscan[:, :, 1:W].rearrange("p c t -> p t c"), ALU.mult).then_inc(kq_done, 1)
                    v.wait_ge(kq_done, c + 1)
                    v.tensor_reduce(score[:, :, :], zt.rearrange("p t (h d) -> p t h d", h=H), AX.X, ALU.add).then_inc(sr_done, 1)
                    v.wait_ge(sr_done, c + 1)
                    v.tensor_scalar(score[:, :, :], score[:, :, :], INV_SQRT_HD, 5.0, ALU.mult, ALU.min).then_inc(c1_done, 1)
                    v.wait_ge(c1_done, c + 1)
                    v.tensor_scalar(score[:, :, :], score[:, :, :], -5.0, None, ALU.max).then_inc(c2_done, 1)
                    v.wait_ge(ex_done, c + 1)
                    v.tensor_tensor(mebuf[:, :, 1:W].rearrange("p (h d) t -> p t h d", h=H),
                                    vg.rearrange("p t (h d) -> p t h d", h=H),
                                    score[:, :, :].unsqueeze(3).to_broadcast([P, T, H, D // H]), ALU.mult).then_inc(msg_done, 1)
                    v.wait_ge(msg_done, c + 1 + C)
                    v.wait_ge(ro_done, c + C)
                    v.tensor_tensor_scan(flat(nscan), flat(flagx)[:, 0:D * W], flat(mebuf), 0.0, ALU.mult, ALU.add).then_inc(ssc_done, 1)
                    v.wait_ge(ssc_done, c + 1 + C)
                    v.tensor_copy(mebuf[:, :, 0], nscan[:, :, T]).then_inc(sc_done, 1)
                    v.wait_ge(sc_done, c + 1)

            v.wait_ge(b_pe, 1)
            v.tensor_tensor_scan(xsc[0:D, 1:P + 1], passkeep[0:D, :], psA[0:D, :], 0.0, ALU.mult, ALU.add).then_inc(b_dve, 1)
            v.wait_ge(b_pe, 2)
            v.tensor_scalar(fixed[:, 0:D], psB2[:, 0:D], cont[:, :], None, ALU.mult).then_inc(b_dve, 1)
            v.wait_ge(b_dve, 2)
            v.wait_ge(mhead_in, 16)
            v.tensor_tensor(fixed[:, 0:D], fixed[:, 0:D], headnd[:, 0:D], ALU.add).then_inc(b_dve, 1)

            with v.Fori(0, NGP) as j:
                for s in range(2):
                    v.wait_ge(o_in[s], j * NGATH + NGATH)
                    v.wait_ge(o_out[s], j * 16 + 16)
                    v.tensor_tensor(xnew[s], x3[:, bass.ds((j * 2 + s) * G, G), :], nd[s][:, :, 0:D], ALU.add).then_inc(o_done, 1)


def kernel(x, src, dst, edge_attr_64, **w):
    import numpy as np
    import concourse.bacc as bacc
    from concourse.bass_utils import run_bass_kernel_spmd

    w = {k: np.asarray(v) for k, v in w.items()}
    ins = {"x": x, "src": src, "dst": dst,
           "attr": edge_attr_64, "attrT": np.asarray(edge_attr_64).reshape(P, EP, D).transpose(2, 1, 0).reshape(D, E),
           "convLnG_T": w["L0_gnn_convLnG"].T, "convLnB_T": w["L0_gnn_convLnB"].T}
    for n in ("encW", "encb", "eencW", "eencb", "convW1", "convb1", "convW2", "convb2", "t", "normG", "normB", "linW", "linb"):
        ins[n] = w["L0_gnn_" + n]
    for n in ("WQ", "bQ", "WK", "bK", "WE", "bE", "WV", "bV"):
        ins[n] = w["L1_gnn_" + n]
    nc = bacc.Bacc("TRN2", target_bir_lowering=False, num_devices=1)
    arrays, aps = {}, {}
    for n, v in ins.items():
        v = np.ascontiguousarray(v)
        arrays["in_" + n] = v
        aps[n] = nc.dram_tensor("in_" + n, v.shape, mybir.dt.from_np(v.dtype), kind="ExternalInput").ap()
    out = nc.dram_tensor("out", (N, D), F32, kind="ExternalOutput").ap()
    gnn_kernel(nc, aps, out)
    r = run_bass_kernel_spmd(nc, [arrays], core_ids=[0])
    return r.results[0]["out"]
```
